# Optimizing a Trainium2 kernel written in Bass

```python
import numpy as np
import jax
import jax.numpy as jnp

def _softmax(x, axis=-1):
    return jax.nn.softmax(x, axis=axis)

def _gelu(x):
    return jax.nn.gelu(x, approximate=True)

def _silu(x):
    return jax.nn.silu(x)

def _sigmoid(x):
    return jax.nn.sigmoid(x)

def _layernorm(x, axis=-1, eps=1e-05):
    m = jnp.mean(x, axis=axis, keepdims=True)
    v = jnp.var(x, axis=axis, keepdims=True)
    return (x - m) / jnp.sqrt(v + eps)

def _scatter_add(tgt, idx, src, axis=0):
    return tgt.at[idx].add(src)

def _segment_sum(src, seg, n):
    return jax.ops.segment_sum(src, seg, n)
kernel_name = 'mk_hybrid_d2_jaxref_r8_e64ec9'

def setup_inputs(seed: int=0):
    np.random.seed(seed)
    _w = jnp.asarray

    def _L0_attn_a_setup():
        import jax, jax.numpy as jnp
        import numpy as np
        from jax import lax
        B, L, D, H = (4, 256, 128, 16)
        DK = D // H
        DV = D // H
        SCALE = DK ** (-0.5)

        def _gla_forward(hidden_states, Wq, Wf, Wi, Wo):
            b, l, d = hidden_states.shape
            q_logits = hidden_states @ Wq
            f_logits = hidden_states @ Wf
            v = hidden_states @ Wi
            q = jax.nn.softmax(q_logits, axis=-1)
            k = 1.0 - jax.nn.softmax(f_logits, axis=-1)
            g = jax.nn.log_softmax(f_logits, axis=-1)

            def split_heads(x, hd):
                return x.reshape(b, l, H, hd).transpose(1, 0, 2, 3)
            q_t = split_heads(q, DK)
            k_t = split_heads(k, DK)
            g_t = split_heads(g, DK)
            v_t = split_heads(v, DV)

            def step(S, inp):
                qt, kt, vt, gt = inp
                S = S * jnp.exp(gt)[..., None] + kt[..., None] * vt[..., None, :]
                ot = jnp.einsum('bhk,bhkv->bhv', qt * SCALE, S)
                return (S, ot)
            S0 = jnp.zeros((b, H, DK, DV), hidden_states.dtype)
            _, o = lax.scan(step, S0, (q_t, k_t, v_t, g_t))
            o = o.transpose(1, 0, 2, 3).reshape(b, l, d)
            return o @ Wo
        key = jax.random.key(seed)
        ks = jax.random.split(key, 5)
        std = 0.02
        return {'hidden_states': jax.random.normal(ks[0], (B, L, D), jnp.float32), 'Wq': jax.random.normal(ks[1], (D, D), jnp.float32) * std, 'Wf': jax.random.normal(ks[2], (D, D), jnp.float32) * std, 'Wi': jax.random.normal(ks[3], (D, D), jnp.float32) * std, 'Wo': jax.random.normal(ks[4], (D, D), jnp.float32) * std}
    _L0_attn_a_in = _L0_attn_a_setup()

    def _L0_attn_b_setup():
        import jax, jax.numpy as jnp
        import numpy as np
        HEADS, D_MODEL, D_V = (16, 128, 64)
        D_K = D_MODEL // HEADS
        key = jax.random.key(seed)
        k1, k2, k3, k4, k5 = jax.random.split(key, 5)
        B, T = (2, 256)
        s = 1.0 / np.sqrt(D_MODEL)
        return {'x': jax.random.normal(k1, (B, T, D_MODEL), dtype=jnp.float32), 'Wq': jax.random.normal(k2, (D_MODEL, HEADS * D_K), dtype=jnp.float32) * s, 'Wk': jax.random.normal(k3, (D_MODEL, HEADS * D_K), dtype=jnp.float32) * s, 'Wv': jax.random.normal(k4, (D_MODEL, HEADS * D_V), dtype=jnp.float32) * s, 'Wo': jax.random.normal(k5, (HEADS * D_V, D_MODEL), dtype=jnp.float32) * (1.0 / np.sqrt(HEADS * D_V))}
    _L0_attn_b_in = _L0_attn_b_setup()

    def _L0_ffn_setup():
        import jax, jax.numpy as jnp
        import numpy as np
        B, L, H, E, I = (4, 256, 128, 8, 512)
        S = B * L
        CAP_FACTOR_EVAL = 2.0
        MIN_CAP = 4
        _cap = int(np.floor(CAP_FACTOR_EVAL * S / E))
        _cap += _cap % 2
        CAPACITY = max(_cap, MIN_CAP)

        def _layer_norm(x, g, b, eps=1e-05):
            mu = x.mean(-1, keepdims=True)
            var = ((x - mu) ** 2).mean(-1, keepdims=True)
            return (x - mu) * jax.lax.rsqrt(var + eps) * g + b
        key = jax.random.key(seed)
        ks = jax.random.split(key, 8)
        gate_std = float(np.sqrt(0.1 / H))
        return {'inputs': jax.random.normal(ks[0], (B, L, H), jnp.float32), 'gate_weight': jax.random.normal(ks[1], (E, H), jnp.float32) * gate_std, 'ln_gamma': jnp.ones((H,), jnp.float32), 'ln_beta': jnp.zeros((H,), jnp.float32), 'wi': jax.random.normal(ks[2], (E, H, I), jnp.float32) * float(1.0 / np.sqrt(H)), 'wo': jax.random.normal(ks[3], (E, I, H), jnp.float32) * float(1.0 / np.sqrt(I)), 'conf_w1': jax.random.normal(ks[4], (H // 2, H), jnp.float32) * float(np.sqrt(2.0 / (H + H // 2))), 'conf_b1': -jnp.ones((H // 2,), jnp.float32), 'conf_w2': jax.random.normal(ks[5], (1, H // 2), jnp.float32) * float(np.sqrt(2.0 / (1 + H // 2))), 'conf_b2': -jnp.ones((1,), jnp.float32), 'comp_w': jax.random.normal(ks[6], (1, H), jnp.float32) * float(1.0 / np.sqrt(H)), 'comp_b': jnp.zeros((1,), jnp.float32)}
    _L0_ffn_in = _L0_ffn_setup()

    def _L1_attn_a_setup():
        import math
        import jax, jax.numpy as jnp
        import numpy as np
        N_HEAD = 16

        def _rope_cos_sin(l, head_dim):
            scale = jnp.arange(0, head_dim, 2, dtype=jnp.float32)[:head_dim // 2]
            freqs = 1.0 / 10000.0 ** scale
            angles = jnp.arange(l, dtype=jnp.float32)[:, None] * freqs[None, :]
            return (jnp.cos(angles), jnp.sin(angles))

        def _rope_apply(x, cos, sin):
            b, l, h, hd = x.shape
            xp = x.astype(jnp.float32).reshape(b, l, h, hd // 2, 2)
            xr, xi = (xp[..., 0], xp[..., 1])
            c = cos[None, :, None, :]
            s = sin[None, :, None, :]
            out_r = xr * c - xi * s
            out_i = xr * s + xi * c
            out = jnp.stack([out_r, out_i], axis=-1).reshape(b, l, h, hd)
            return out.astype(x.dtype)
        key = jax.random.key(seed)
        ks = jax.random.split(key, 9)
        b, l, d = (2, 256, 128)
        sc = 1.0 / math.sqrt(d)
        inp = {'x': jax.random.normal(ks[0], (b, l, d), dtype=jnp.float32), 'Wq': jax.random.normal(ks[1], (d, d), dtype=jnp.float32) * sc, 'bq': jnp.zeros((d,), dtype=jnp.float32), 'Wk': jax.random.normal(ks[2], (d, d), dtype=jnp.float32) * sc, 'bk': jnp.zeros((d,), dtype=jnp.float32), 'Wv': jax.random.normal(ks[3], (d, d), dtype=jnp.float32) * sc, 'bv': jnp.zeros((d,), dtype=jnp.float32), 'Wo': jax.random.normal(ks[4], (d, d), dtype=jnp.float32) * sc, 'bo': jnp.zeros((d,), dtype=jnp.float32)}
        return inp
    _L1_attn_a_in = _L1_attn_a_setup()

    def _L1_attn_b_setup():
        import jax, jax.numpy as jnp
        import numpy as np
        import math
        B, T, C = (2, 256, 128)
        H = 16
        D = C // H

        def alibi_slopes(n_heads):
            start = 2.0 ** (-2.0 ** (-(math.log2(n_heads) - 3)))
            return jnp.asarray([start * start ** i for i in range(n_heads)], dtype=jnp.float32)
        key = jax.random.key(seed)
        ks = jax.random.split(key, 6)
        x = jax.random.normal(ks[0], (B, T, C), dtype=jnp.float32)
        W_attn = jax.random.normal(ks[1], (C, 3 * C), dtype=jnp.float32) * 0.02
        b_attn = jnp.zeros((3 * C,), dtype=jnp.float32)
        W_proj = jax.random.normal(ks[2], (C, C), dtype=jnp.float32) * 0.02
        b_proj = jnp.zeros((C,), dtype=jnp.float32)
        temperature = jnp.ones((1,), dtype=jnp.float32) * 2.0
        return {'x': x, 'W_attn': W_attn, 'b_attn': b_attn, 'W_proj': W_proj, 'b_proj': b_proj, 'temperature': temperature}
    _L1_attn_b_in = _L1_attn_b_setup()

    def _L1_ffn_setup():
        import jax, jax.numpy as jnp
        import numpy as np
        D_IN, D_HID = (128, 512)

        def _ternary(key, shape):
            return jax.random.randint(key, shape, -1, 2).astype(jnp.float32)

        def _tlin(x, w, s):
            return jnp.einsum('bsi,oi->bso', x, w) * s
        key = jax.random.key(seed)
        ks = jax.random.split(key, 12)
        inv = lambda fan: 1.0 / np.sqrt(fan).astype(np.float32)
        return {'x': jax.random.normal(ks[0], (4, 256, D_IN), dtype=jnp.float32), 'w1_w': _ternary(ks[1], (D_HID, D_IN)), 'w1_s': jax.random.uniform(ks[2], (D_HID,), dtype=jnp.float32) * inv(D_IN), 'w2_w': _ternary(ks[3], (D_HID, D_IN)), 'w2_s': jax.random.uniform(ks[4], (D_HID,), dtype=jnp.float32) * inv(D_IN), 'h1_w': _ternary(ks[5], (D_HID, D_HID)), 'h1_s': jax.random.uniform(ks[6], (D_HID,), dtype=jnp.float32) * inv(D_HID), 'h2_w': _ternary(ks[7], (D_HID, D_HID)), 'h2_s': jax.random.uniform(ks[8], (D_HID,), dtype=jnp.float32) * inv(D_HID), 'w3_w': _ternary(ks[9], (D_IN, D_HID)), 'w3_s': jax.random.uniform(ks[10], (D_IN,), dtype=jnp.float32) * inv(D_HID)}
    _L1_ffn_in = _L1_ffn_setup()
    _d = {'L0_attn_a_hidden_states': _L0_attn_a_in['hidden_states'], 'L0_attn_a_Wq': _L0_attn_a_in['Wq'], 'L0_attn_a_Wf': _L0_attn_a_in['Wf'], 'L0_attn_a_Wi': _L0_attn_a_in['Wi'], 'L0_attn_a_Wo': _L0_attn_a_in['Wo'], 'L0_attn_b_Wq': _L0_attn_b_in['Wq'], 'L0_attn_b_Wk': _L0_attn_b_in['Wk'], 'L0_attn_b_Wv': _L0_attn_b_in['Wv'], 'L0_attn_b_Wo': _L0_attn_b_in['Wo'], 'L0_ffn_gate_weight': _L0_ffn_in['gate_weight'], 'L0_ffn_ln_gamma': _L0_ffn_in['ln_gamma'], 'L0_ffn_ln_beta': _L0_ffn_in['ln_beta'], 'L0_ffn_wi': _L0_ffn_in['wi'], 'L0_ffn_wo': _L0_ffn_in['wo'], 'L0_ffn_conf_w1': _L0_ffn_in['conf_w1'], 'L0_ffn_conf_b1': _L0_ffn_in['conf_b1'], 'L0_ffn_conf_w2': _L0_ffn_in['conf_w2'], 'L0_ffn_conf_b2': _L0_ffn_in['conf_b2'], 'L0_ffn_comp_w': _L0_ffn_in['comp_w'], 'L0_ffn_comp_b': _L0_ffn_in['comp_b'], 'L1_attn_a_Wq': _L1_attn_a_in['Wq'], 'L1_attn_a_bq': _L1_attn_a_in['bq'], 'L1_attn_a_Wk': _L1_attn_a_in['Wk'], 'L1_attn_a_bk': _L1_attn_a_in['bk'], 'L1_attn_a_Wv': _L1_attn_a_in['Wv'], 'L1_attn_a_bv': _L1_attn_a_in['bv'], 'L1_attn_a_Wo': _L1_attn_a_in['Wo'], 'L1_attn_a_bo': _L1_attn_a_in['bo'], 'L1_attn_b_W_attn': _L1_attn_b_in['W_attn'], 'L1_attn_b_b_attn': _L1_attn_b_in['b_attn'], 'L1_attn_b_W_proj': _L1_attn_b_in['W_proj'], 'L1_attn_b_b_proj': _L1_attn_b_in['b_proj'], 'L1_attn_b_temperature': _L1_attn_b_in['temperature'], 'L1_ffn_w1_w': _L1_ffn_in['w1_w'], 'L1_ffn_w1_s': _L1_ffn_in['w1_s'], 'L1_ffn_w2_w': _L1_ffn_in['w2_w'], 'L1_ffn_w2_s': _L1_ffn_in['w2_s'], 'L1_ffn_h1_w': _L1_ffn_in['h1_w'], 'L1_ffn_h1_s': _L1_ffn_in['h1_s'], 'L1_ffn_h2_w': _L1_ffn_in['h2_w'], 'L1_ffn_h2_s': _L1_ffn_in['h2_s'], 'L1_ffn_w3_w': _L1_ffn_in['w3_w'], 'L1_ffn_w3_s': _L1_ffn_in['w3_s']}
    _x0 = _d['L0_attn_a_hidden_states']
    _d['L0_attn_a_hidden_states'] = jax.random.normal(jax.random.fold_in(jax.random.key(seed), 1), (4, 1024, 128), dtype=_x0.dtype)
    del _x0
    return _d

def reference(L0_attn_a_hidden_states, L0_attn_a_Wq, L0_attn_a_Wf, L0_attn_a_Wi, L0_attn_a_Wo, L0_attn_b_Wq, L0_attn_b_Wk, L0_attn_b_Wv, L0_attn_b_Wo, L0_ffn_gate_weight, L0_ffn_ln_gamma, L0_ffn_ln_beta, L0_ffn_wi, L0_ffn_wo, L0_ffn_conf_w1, L0_ffn_conf_b1, L0_ffn_conf_w2, L0_ffn_conf_b2, L0_ffn_comp_w, L0_ffn_comp_b, L1_attn_a_Wq, L1_attn_a_bq, L1_attn_a_Wk, L1_attn_a_bk, L1_attn_a_Wv, L1_attn_a_bv, L1_attn_a_Wo, L1_attn_a_bo, L1_attn_b_W_attn, L1_attn_b_b_attn, L1_attn_b_W_proj, L1_attn_b_b_proj, L1_attn_b_temperature, L1_ffn_w1_w, L1_ffn_w1_s, L1_ffn_w2_w, L1_ffn_w2_s, L1_ffn_h1_w, L1_ffn_h1_s, L1_ffn_h2_w, L1_ffn_h2_s, L1_ffn_w3_w, L1_ffn_w3_s):

    def _L0_attn_a_ref(hidden_states, Wq, Wf, Wi, Wo):
        import jax, jax.numpy as jnp
        import numpy as np
        from jax import lax
        B, L, D, H = (4, 256, 128, 16)
        DK = D // H
        DV = D // H
        SCALE = DK ** (-0.5)

        def _gla_forward(hidden_states, Wq, Wf, Wi, Wo):
            b, l, d = hidden_states.shape
            q_logits = hidden_states @ Wq
            f_logits = hidden_states @ Wf
            v = hidden_states @ Wi
            q = jax.nn.softmax(q_logits, axis=-1)
            k = 1.0 - jax.nn.softmax(f_logits, axis=-1)
            g = jax.nn.log_softmax(f_logits, axis=-1)

            def split_heads(x, hd):
                return x.reshape(b, l, H, hd).transpose(1, 0, 2, 3)
            q_t = split_heads(q, DK)
            k_t = split_heads(k, DK)
            g_t = split_heads(g, DK)
            v_t = split_heads(v, DV)

            def step(S, inp):
                qt, kt, vt, gt = inp
                S = S * jnp.exp(gt)[..., None] + kt[..., None] * vt[..., None, :]
                ot = jnp.einsum('bhk,bhkv->bhv', qt * SCALE, S)
                return (S, ot)
            S0 = jnp.zeros((b, H, DK, DV), hidden_states.dtype)
            _, o = lax.scan(step, S0, (q_t, k_t, v_t, g_t))
            o = o.transpose(1, 0, 2, 3).reshape(b, l, d)
            return o @ Wo
        return _gla_forward(hidden_states, Wq, Wf, Wi, Wo)

    def _L0_attn_b_ref(x, Wq, Wk, Wv, Wo):
        import jax, jax.numpy as jnp
        import numpy as np
        HEADS, D_MODEL, D_V = (16, 128, 64)
        D_K = D_MODEL // HEADS
        B, T, _ = x.shape
        scale = jnp.asarray(np.sqrt(D_K), x.dtype)
        q = (x @ Wq).reshape(B, T, HEADS, D_K).transpose(0, 2, 1, 3)
        k = (x @ Wk).reshape(B, T, HEADS, D_K).transpose(0, 2, 1, 3)
        v = (x @ Wv).reshape(B, T, HEADS, D_V).transpose(0, 2, 1, 3)
        scores = jnp.einsum('bhqd,bhkd->bhqk', q, k) / scale
        causal = jnp.triu(jnp.ones((T, T), dtype=bool), k=1)
        scores = jnp.where(causal, jnp.asarray(-jnp.inf, scores.dtype), scores)
        attn = jax.nn.softmax(scores, axis=-1)
        ctx = jnp.einsum('bhqk,bhkd->bhqd', attn, v)
        out = ctx.transpose(0, 2, 1, 3).reshape(B, T, HEADS * D_V)
        return out @ Wo

    def _L0_ffn_ref(inputs, gate_weight, ln_gamma, ln_beta, wi, wo, conf_w1, conf_b1, conf_w2, conf_b2, comp_w, comp_b):
        import jax, jax.numpy as jnp
        import numpy as np
        B, L, H, E, I = (4, 256, 128, 8, 512)
        S = B * L
        CAP_FACTOR_EVAL = 2.0
        MIN_CAP = 4
        _cap = int(np.floor(CAP_FACTOR_EVAL * S / E))
        _cap += _cap % 2
        CAPACITY = max(_cap, MIN_CAP)

        def _layer_norm(x, g, b, eps=1e-05):
            mu = x.mean(-1, keepdims=True)
            var = ((x - mu) ** 2).mean(-1, keepdims=True)
            return (x - mu) * jax.lax.rsqrt(var + eps) * g + b
        tokens = inputs.reshape(-1, H)
        residual = tokens
        tokens = _layer_norm(tokens, ln_gamma, ln_beta)
        complexity_score = jax.nn.sigmoid(tokens @ comp_w.T + comp_b).mean()
        hdn = jax.nn.relu(tokens @ conf_w1.T + conf_b1)
        confidence_score = jax.nn.sigmoid(hdn @ conf_w2.T + conf_b2).mean()
        logits = tokens.astype(jnp.float32) @ gate_weight.astype(jnp.float32).T
        probs = jax.nn.softmax(logits, axis=-1)
        top1 = jnp.argmax(logits, axis=-1)
        onehot = jax.nn.one_hot(top1, E, dtype=jnp.int32)
        rank_e = jnp.cumsum(onehot, axis=0) - onehot
        rank = jnp.sum(rank_e * onehot, axis=-1)
        keep = rank < CAPACITY
        weight = jnp.take_along_axis(probs, top1[:, None], axis=-1)[:, 0]
        weight = (weight * keep).astype(tokens.dtype)
        slot = jnp.where(keep, rank, 0)
        dispatch = jnp.zeros((E, CAPACITY, H), tokens.dtype)
        dispatch = dispatch.at[top1, slot].add(tokens * keep[:, None])
        h = jax.nn.gelu(jnp.einsum('ech,ehi->eci', dispatch, wi), approximate=False)
        expert_out = jnp.einsum('eci,eih->ech', h, wo)
        combined = weight[:, None] * expert_out[top1, slot]
        out = (residual + combined).reshape(inputs.shape)
        return out

    def _L1_attn_a_ref(x, Wq, bq, Wk, bk, Wv, bv, Wo, bo):
        import math
        import jax, jax.numpy as jnp
        import numpy as np
        N_HEAD = 16

        def _rope_cos_sin(l, head_dim):
            scale = jnp.arange(0, head_dim, 2, dtype=jnp.float32)[:head_dim // 2]
            freqs = 1.0 / 10000.0 ** scale
            angles = jnp.arange(l, dtype=jnp.float32)[:, None] * freqs[None, :]
            return (jnp.cos(angles), jnp.sin(angles))

        def _rope_apply(x, cos, sin):
            b, l, h, hd = x.shape
            xp = x.astype(jnp.float32).reshape(b, l, h, hd // 2, 2)
            xr, xi = (xp[..., 0], xp[..., 1])
            c = cos[None, :, None, :]
            s = sin[None, :, None, :]
            out_r = xr * c - xi * s
            out_i = xr * s + xi * c
            out = jnp.stack([out_r, out_i], axis=-1).reshape(b, l, h, hd)
            return out.astype(x.dtype)
        b, l, d = x.shape
        h = N_HEAD
        hd = d // h
        q = (x @ Wq + bq).reshape(b, l, h, hd)
        k = (x @ Wk + bk).reshape(b, l, h, hd)
        v = (x @ Wv + bv).reshape(b, l, h, hd)
        cos, sin = _rope_cos_sin(l, hd)
        q = _rope_apply(q, cos, sin)
        k = _rope_apply(k, cos, sin)
        score = jnp.einsum('blhd,bmhd->bhlm', q, k) / math.sqrt(hd)
        ctx = jnp.einsum('bhlm,bmhd->blhd', score, v).reshape(b, l, d)
        return ctx @ Wo + bo

    def _L1_attn_b_ref(x, W_attn, b_attn, W_proj, b_proj, temperature):
        import jax, jax.numpy as jnp
        import numpy as np
        import math
        B, T, C = (2, 256, 128)
        H = 16
        D = C // H

        def alibi_slopes(n_heads):
            start = 2.0 ** (-2.0 ** (-(math.log2(n_heads) - 3)))
            return jnp.asarray([start * start ** i for i in range(n_heads)], dtype=jnp.float32)
        Bc, Tc, Cc = x.shape
        qkv = x @ W_attn + b_attn
        q, k, v = jnp.split(qkv, 3, axis=-1)
        q = q.reshape(Bc, Tc, H, D)
        k = k.reshape(Bc, Tc, H, D)
        v = v.reshape(Bc, Tc, H, D)
        scale = 1.0 / math.sqrt(D)
        att = jnp.einsum('bqhd,bkhd->bhqk', q, k) * scale
        att = att / temperature
        pos = jnp.arange(Tc, dtype=jnp.float32)
        rel = pos[None, :] - pos[:, None]
        slopes = alibi_slopes(H)
        bias = slopes[:, None, None] * rel[None, :, :]
        causal = pos[None, :] <= pos[:, None]
        bias = jnp.where(causal[None, :, :], bias, -jnp.inf)
        att = att + bias[None, :, :, :]
        w = jax.nn.softmax(att, axis=-1)
        y = jnp.einsum('bhqk,bkhd->bqhd', w, v).reshape(Bc, Tc, Cc)
        return y @ W_proj + b_proj

    def _L1_ffn_ref(x, w1_w, w1_s, w2_w, w2_s, h1_w, h1_s, h2_w, h2_s, w3_w, w3_s):
        import jax, jax.numpy as jnp
        import numpy as np
        D_IN, D_HID = (128, 512)

        def _ternary(key, shape):
            return jax.random.randint(key, shape, -1, 2).astype(jnp.float32)

        def _tlin(x, w, s):
            return jnp.einsum('bsi,oi->bso', x, w) * s
        h = jax.nn.silu(_tlin(x, w1_w, w1_s)) * _tlin(x, w2_w, w2_s)
        h = jax.nn.gelu(_tlin(h, h1_w, h1_s), approximate=False)
        h = jax.nn.gelu(_tlin(h, h2_w, h2_s), approximate=False)
        return _tlin(h, w3_w, w3_s)
    x = L0_attn_a_hidden_states
    x = x + _L0_attn_a_ref(_layernorm(x, axis=-1), L0_attn_a_Wq, L0_attn_a_Wf, L0_attn_a_Wi, L0_attn_a_Wo)
    x = x + _L0_ffn_ref(_layernorm(x, axis=-1), L0_ffn_gate_weight, L0_ffn_ln_gamma, L0_ffn_ln_beta, L0_ffn_wi, L0_ffn_wo, L0_ffn_conf_w1, L0_ffn_conf_b1, L0_ffn_conf_w2, L0_ffn_conf_b2, L0_ffn_comp_w, L0_ffn_comp_b)
    x = x + _L0_attn_b_ref(_layernorm(x, axis=-1), L0_attn_b_Wq, L0_attn_b_Wk, L0_attn_b_Wv, L0_attn_b_Wo)
    x = x + _L0_ffn_ref(_layernorm(x, axis=-1), L0_ffn_gate_weight, L0_ffn_ln_gamma, L0_ffn_ln_beta, L0_ffn_wi, L0_ffn_wo, L0_ffn_conf_w1, L0_ffn_conf_b1, L0_ffn_conf_w2, L0_ffn_conf_b2, L0_ffn_comp_w, L0_ffn_comp_b)
    x = x + _L1_attn_a_ref(_layernorm(x, axis=-1), L1_attn_a_Wq, L1_attn_a_bq, L1_attn_a_Wk, L1_attn_a_bk, L1_attn_a_Wv, L1_attn_a_bv, L1_attn_a_Wo, L1_attn_a_bo)
    x = x + _L1_ffn_ref(_layernorm(x, axis=-1), L1_ffn_w1_w, L1_ffn_w1_s, L1_ffn_w2_w, L1_ffn_w2_s, L1_ffn_h1_w, L1_ffn_h1_s, L1_ffn_h2_w, L1_ffn_h2_s, L1_ffn_w3_w, L1_ffn_w3_s)
    x = x + _L1_attn_b_ref(_layernorm(x, axis=-1), L1_attn_b_W_attn, L1_attn_b_b_attn, L1_attn_b_W_proj, L1_attn_b_b_proj, L1_attn_b_temperature)
    x = x + _L1_ffn_ref(_layernorm(x, axis=-1), L1_ffn_w1_w, L1_ffn_w1_s, L1_ffn_w2_w, L1_ffn_w2_s, L1_ffn_h1_w, L1_ffn_h1_s, L1_ffn_h2_w, L1_ffn_h2_s, L1_ffn_w3_w, L1_ffn_w3_s)
    return x

_drawn_inputs = setup_inputs


def setup_inputs(seed=0):
    import zlib

    import numpy as np

    out = dict(_drawn_inputs(seed))
    spreads = {'L0_ffn_ln_gamma': (1.0, 0.2),
     'L0_ffn_ln_beta': (0.0, 0.1),
     'L0_ffn_conf_b1': (-1.0, 0.2),
     'L1_attn_a_bq': (0.0, 0.1),
     'L1_attn_a_bk': (0.0, 0.1),
     'L1_attn_a_bv': (0.0, 0.1),
     'L1_attn_a_bo': (0.0, 0.1),
     'L1_attn_b_b_attn': (0.0, 0.1),
     'L1_attn_b_b_proj': (0.0, 0.1)}
    factors = {}
    for name, (base, spread) in spreads.items():
        noise = np.random.default_rng([zlib.crc32(name.encode()), seed]).standard_normal(out[name].shape)
        drawn = base * np.exp(spread * noise) if base else spread * noise
        out[name] = jnp.asarray(drawn.astype(out[name].dtype))
    for name, factor in factors.items():
        out[name] = (out[name] * factor).astype(out[name].dtype)
    return out
```

```python
from contextlib import ExitStack

import numpy as np

import concourse.bass as bass
from concourse import mybir

F32 = mybir.dt.float32
BF16 = mybir.dt.bfloat16
U32 = mybir.dt.uint32
ALU = mybir.AluOpType
ACT = mybir.ActivationFunctionType
AX = mybir.AxisListType

P = 128
CHUNK = 512
TPC = CHUNK // P
EPS = 1e-5
HEADS = 16


class Scope:

    def __init__(self, nc, ctx, tag):
        self.nc, self.ctx, self.tag = nc, ctx, tag

    def sb(self, name, shape, dt=F32):
        return self.ctx.enter_context(self.nc.sbuf_tensor(f"{self.tag}_{name}", shape, dt))

    def sem(self, name):
        return self.nc.alloc_semaphore(name=f"{self.tag}_{name}")


def loop(eng, n, body):
    if n > 1:
        with eng.Fori(0, n - 1) as k:
            body(k, True)
    body(n - 1, False)


class Norm:

    def __init__(self, m, res, tiles=TPC, name="ln"):
        self.tiles = tiles
        self.minus_half = res.minus_half
        self.stats = m.sb(f"{name}_stats", [P, tiles, 6])
        self.mv = m.sb(f"{name}_mv", [P, tiles, 2])
        self.var = m.sb(f"{name}_var", [P, tiles])
        self.rstd = m.sb(f"{name}_rstd", [P, tiles])
        self.hold = m.sb(f"{name}_hold", [P, 1])
        self.step = m.sem(f"{name}_step")
        self.root = m.sem(f"{name}_root")

    def vector(self, dve, k, src, dst):
        for j in range(self.tiles):
            last = dve.bn_stats(self.stats[:, j, :], src(j))
        last.then_inc(self.step, 1)
        dve.wait_ge(self.step, k * 3 + 1)
        dve.memset(self.hold[:, :], 0.0)
        for j in range(self.tiles):
            last = dve.bn_aggr(self.mv[:, j, :], self.stats[:, j, :])
        last.then_inc(self.step, 1)
        dve.wait_ge(self.step, k * 3 + 2)
        dve.tensor_scalar(self.var[:, :], self.mv[:, :, 1], EPS, None, ALU.add).then_inc(self.step, 1)
        dve.wait_ge(self.root, k + 1)
        for j in range(self.tiles):
            last = dve.tensor_scalar(dst(j), src(j), self.mv[:, j, 0:1], self.rstd[:, j:j + 1],
                                     ALU.subtract, ALU.mult)
        return last

    def gpsimd(self, pool, k):
        pool.wait_ge(self.step, k * 3 + 3)
        pool.tensor_tensor(self.rstd[:, :], self.var[:, :], self.minus_half[:, 0:self.tiles], ALU.pow).then_inc(self.root, 1)


def transpose_blocks(nc, res, tag, jobs, arrived):
    turned, copied = nc.alloc_semaphore(name=f"{tag}_turned"), nc.alloc_semaphore(name=f"{tag}_copied")
    NB = len(res.banks)
    with nc.Block() as block:
        @block.tensor
        def _(pe):
            for sem, n in arrived:
                pe.wait_ge(sem, n)
            for i, (_, src) in enumerate(jobs):
                if i >= NB:
                    pe.wait_ge(copied, i - NB + 1)
                nc.tensor.transpose(res.banks[i % NB][:, 0:P], src, res.ident[:, :]).then_inc(turned, 1)

        @block.scalar
        def _(act):
            for i, (dst, _) in enumerate(jobs):
                act.wait_ge(turned, i + 1)
                nc.scalar.copy(dst, res.banks[i % NB][:, 0:P]).then_inc(copied, 1)


def ternary_ffn(nc, res, tag, w):
    X, banks, ident = res.X, res.banks, res.ident
    NCH = res.T // CHUNK
    HT = w.w1T.shape[1] // P
    with ExitStack() as ctx:
        m = Scope(nc, ctx, tag)
        norm = Norm(m, res)
        h = m.sb("h", [P, TPC, P])
        hT = m.sb("hT", [P, CHUNK])
        gate = m.sb("gate", [P, HT, CHUNK])
        acts = [m.sb(f"act{n}", [P, HT, CHUNK]) for n in range(3)]
        scaled = m.sb("scaled", [P, TPC, P])
        psA, psB, psT, psO = banks[0:3], banks[3:5], banks[5], banks[6]
        h_ready = m.sem("h_ready")
        turned = m.sem("turned")
        hT_ready = m.sem("hT_ready")
        a_ready = m.sem("a_ready")
        a_out = m.sem("a_out")
        b_ready = m.sem("b_ready")
        b_out = m.sem("b_out")
        o_ready = m.sem("o_ready")
        o_out = m.sem("o_out")
        x_ready = m.sem("x_ready")

        with nc.Block() as block:
            @block.vector
            def _(dve):
                dve.sem_inc(b_out, 2)
                dve.sem_inc(o_out, 1)

                def norm_chunk(k):
                    norm.vector(dve, k, lambda j: X[:, bass.ds(k * TPC + j, 1), :], lambda j: h[:, j, :]).then_inc(h_ready, 1)

                def chunk(k, more):
                    for mt in range(HT):
                        dve.wait_ge(b_ready, k * HT + mt + 1)
                        dve.wait_ge(a_out, k * 3 * HT + mt + 4)
                        nc.vector.scalar_tensor_tensor(acts[0][:, mt, :], psB[mt % 2][:, :], w.s2[:, mt:mt + 1],
                                                       gate[:, mt, :], ALU.mult, ALU.mult).then_inc(b_out, 1)
                    if more:
                        dve.wait_ge(turned, k + 1)
                        norm_chunk(k + 1)
                    dve.wait_ge(o_ready, k + 1)
                    nc.vector.tensor_tensor(scaled[:, :, :], psO[:, :].rearrange("p (j n) -> p j n", j=TPC),
                                            w.s3[:, :].unsqueeze(1).to_broadcast([P, TPC, P]), ALU.mult).then_inc(o_out, 1)
                    dve.wait_ge(o_out, k + 2)
                    xk = X[:, bass.ds(k * TPC, TPC), :]
                    nc.vector.tensor_tensor(xk, xk, scaled[:, :, :], ALU.add).then_inc(x_ready, 1)

                norm_chunk(0)
                loop(dve, NCH, chunk)

            @block.gpsimd
            def _(pool):
                with pool.Fori(0, NCH) as k:
                    norm.gpsimd(pool, k)

            @block.scalar
            def _(act):
                act.sem_inc(hT_ready, 1)
                act.sem_inc(a_out, 3)

                def copy_hT(k):
                    act.wait_ge(turned, k + 1)
                    nc.scalar.copy(hT[:, :], psT[:, :]).then_inc(hT_ready, 1)

                def chunk(k, more):
                    for mt in range(HT):
                        act.wait_ge(a_ready, k * 3 * HT + mt + 1)
                        nc.scalar.activation(gate[:, mt, :], psA[mt % 3][:, :], ACT.Silu,
                                             scale=w.s1[:, mt:mt + 1]).then_inc(a_out, 1)
                    if more:
                        copy_hT(k + 1)
                    for layer, scale in ((1, w.sh1), (2, w.sh2)):
                        for mt in range(HT):
                            n = layer * HT + mt
                            act.wait_ge(a_ready, k * 3 * HT + n + 1)
                            nc.scalar.activation(acts[layer][:, mt, :], psA[n % 3][:, :], ACT.Gelu,
                                                 scale=scale[:, mt:mt + 1]).then_inc(a_out, 1)

                copy_hT(0)
                loop(act, NCH, chunk)

            @block.tensor
            def _(pe):
                def turn(k):
                    pe.wait_ge(h_ready, k + 1)
                    pe.wait_ge(hT_ready, k + 1)
                    for j in range(TPC):
                        last = nc.tensor.transpose(psT[:, j * P:(j + 1) * P], h[:, j, :], ident[:, :])
                    last.then_inc(turned, 1)

                def chunk(k, more):
                    pe.wait_ge(hT_ready, k + 2)
                    for mt in range(HT):
                        pe.wait_ge(a_out, k * 3 * HT + mt + 1)
                        nc.tensor.matmul(psA[mt % 3][:, :], w.w1T[:, mt * P:(mt + 1) * P], hT[:, :],
                                         start=True, stop=True).then_inc(a_ready, 1)
                        pe.wait_ge(b_out, k * HT + mt + 1)
                        nc.tensor.matmul(psB[mt % 2][:, :], w.w2T[:, mt * P:(mt + 1) * P], hT[:, :],
                                         start=True, stop=True).then_inc(b_ready, 1)
                    if more:
                        turn(k + 1)
                    for layer, wT in ((1, w.h1T), (2, w.h2T)):
                        for mt in range(HT):
                            n = layer * HT + mt
                            pe.wait_ge(a_out, k * 3 * HT + n + 1)
                            for kt in range(HT):
                                if mt == 0:
                                    if layer == 1:
                                        pe.wait_ge(b_out, k * HT + kt + 3)
                                    else:
                                        pe.wait_ge(a_out, k * 3 * HT + HT + kt + 4)
                                last = nc.tensor.matmul(psA[n % 3][:, :], wT[:, kt, mt * P:(mt + 1) * P],
                                                        acts[layer - 1][:, kt, :], start=(kt == 0), stop=(kt == HT - 1))
                            last.then_inc(a_ready, 1)
                    pe.wait_ge(o_out, k + 1)
                    pe.wait_ge(a_out, (k + 1) * 3 * HT + 3)
                    for j in range(TPC):
                        for kt in range(HT):
                            last = nc.tensor.matmul(psO[:, j * P:(j + 1) * P], acts[2][:, kt, j * P:(j + 1) * P],
                                                    w.w3T[:, kt, :], start=(kt == 0), stop=(kt == HT - 1))
                    last.then_inc(o_ready, 1)

                turn(0)
                loop(pe, NCH, chunk)


def gated_attention(nc, res, tag, ins):
    X, banks, ident = res.X, res.banks, res.ident
    NB, CPB, TPB = res.B, res.L // CHUNK, res.L // P
    D, H = P, 16
    DV = D // H
    assert CPB == 2
    with ExitStack() as ctx:
        m = Scope(nc, ctx, tag)
        norm = Norm(m, res)
        wqf, wi = m.sb("wqf", [P, 2 * D]), m.sb("wi", [P, D])
        wir, wor = m.sb("wir", [P, DV, D]), m.sb("wor", [P, DV, D])
        h = m.sb("h", [P, TPC, P])
        hT = m.sb("hT", [P, CPB, CHUNK])
        neg, total, inv = m.sb("neg", [P, TPC, 2]), m.sb("total", [P, TPC * 2]), m.sb("inv", [P, TPC * 2])
        e = m.sb("e", [P, TPC, 2, P])
        qT, fT, kT = (m.sb(n, [P, CPB, CHUNK]) for n in ("qT", "fT", "kT"))
        kv = m.sb("kv", [P, 2, CHUNK])
        S = m.sb("S", [P, CPB, DV, CHUNK])
        qS = m.sb("qS", [P, DV, CHUNK])
        psT, psL, psV, psQ, psF, psO = banks[0], banks[1:3], banks[3:5], banks[5], banks[6], banks[7]
        loaded = m.sem("loaded")
        spread = m.sem("spread")
        h_ready = m.sem("h_ready")
        turned = m.sem("turned")
        hT_ready = m.sem("hT_ready")
        l_ready = m.sem("l_ready")
        neg_ready = m.sem("neg_ready")
        e_ready = m.sem("e_ready")
        inv_ready = m.sem("inv_ready")
        soft_ready = m.sem("soft_ready")
        qf_turned = m.sem("qf_turned")
        qf_ready = m.sem("qf_ready")
        k_ready = m.sem("k_ready")
        v_ready = m.sem("v_ready")
        kv_ready = m.sem("kv_ready")
        s_ready = m.sem("s_ready")
        qs_ready = m.sem("qs_ready")
        o_ready = m.sem("o_ready")
        x_ready = m.sem("x_ready")
        LOADS = 3 + DV

        with nc.Block() as block:
            @block.sync
            def _(sp):
                for t, name in ((wqf[:, 0:D], "Wq"), (wqf[:, D:2 * D], "Wf"), (wi[:, :], "Wi")):
                    sp.dma_start(t, ins["L0_attn_a_" + name]).then_inc(loaded, 16)
                rows = ins["L0_attn_a_Wo"].rearrange("(h v) n -> v h n", v=DV)
                for v in range(DV):
                    sp.dma_start(wor[:, v, :], rows[v].unsqueeze(1).to_broadcast([H, DV, D])).then_inc(loaded, 16)
                sp.wait_ge(loaded, 16 * LOADS)

            @block.vector
            def _(dve):
                dve.sem_inc(k_ready, 1)
                dve.sem_inc(kv_ready, 2)
                dve.sem_inc(x_ready, 1)

                def norm_chunk(k):
                    norm.vector(dve, k, lambda j: X[:, bass.ds(k * TPC + j, 1), :], lambda j: h[:, j, :]).then_inc(h_ready, 1)

                def maxima(k):
                    dve.wait_ge(l_ready, k + 1)
                    for half in range(2):
                        last = nc.vector.tensor_reduce(neg[:, 2 * half:2 * half + 2, :], psL[half][:, :].rearrange("p (j w n) -> p j w n", j=2, w=2),
                                                       AX.X, ALU.max, negate=True)
                    last.then_inc(neg_ready, 1)

                def inverse(k):
                    dve.wait_ge(e_ready, k + 2)
                    nc.vector.reciprocal(inv[:, :], total[:, :]).then_inc(inv_ready, 1)

                def one_minus(k, c):
                    dve.wait_ge(qf_ready, k + 2)
                    nc.vector.tensor_scalar(kT[:, c, :], fT[:, c, :], -1.0, 1.0, ALU.mult, ALU.add).then_inc(k_ready, 1)

                def scan(k, c, v):
                    n = k * DV + v
                    dve.wait_ge(v_ready, n + 1)
                    if v == 0:
                        dve.wait_ge(k_ready, k + 2)
                    nc.vector.tensor_tensor(kv[:, v % 2, :], psV[v % 2][:, :], kT[:, c, :], ALU.mult).then_inc(kv_ready, 1)
                    dve.wait_ge(kv_ready, n + 3)
                    nc.vector.tensor_tensor_scan(S[:, c, v, :], fT[:, c, :], kv[:, v % 2, :],
                                                 0.0 if c == 0 else S[:, 0, v, CHUNK - 1:CHUNK], ALU.mult, ALU.add).then_inc(s_ready, 1)

                dve.wait_ge(loaded, 16 * LOADS)
                for v in range(DV):
                    nc.vector.tensor_copy(wir[:, v, :].rearrange("p (h k) -> p h k", k=DV),
                                          wi[:, :].rearrange("p (h v) -> p v h", v=DV)[:, v, :].unsqueeze(2).to_broadcast([P, H, DV])).then_inc(spread, 1)
                norm_chunk(0)
                maxima(0)
                inverse(0)
                one_minus(0, 0)

                def batch(b, more):
                    for c in range(CPB):
                        k = b * CPB + c
                        ahead = c + 1 < CPB or more
                        for v in range(2):
                            scan(k, c, v)
                        if ahead:
                            norm_chunk(k + 1)
                        for v in range(2, 4):
                            scan(k, c, v)
                        if ahead:
                            maxima(k + 1)
                        for v in range(4, 6):
                            scan(k, c, v)
                        if ahead:
                            inverse(k + 1)
                        for v in range(6, 8):
                            scan(k, c, v)
                        if ahead:
                            one_minus(k + 1, 1 - c)
                        dve.wait_ge(o_ready, k + 2)
                        xk = X[:, bass.ds(k * TPC, TPC), :]
                        nc.vector.tensor_tensor(xk, xk, psO[:, :].rearrange("p (j n) -> p j n", j=TPC), ALU.add).then_inc(x_ready, 1)
                loop(dve, NB, batch)

            @block.gpsimd
            def _(pool):
                def soften(k):
                    pool.wait_ge(inv_ready, k + 1)
                    ev = e[:, :, :, :].rearrange("p j w n -> p (j w) n")
                    nc.gpsimd.tensor_tensor(ev, ev, inv[:, :].unsqueeze(2).to_broadcast([P, 2 * TPC, P]), ALU.mult).then_inc(soft_ready, 1)

                def read(k, c, v):
                    if v == 0:
                        pool.wait_ge(o_ready, k + 1)
                    pool.wait_ge(s_ready, k * DV + v + 1)
                    nc.gpsimd.tensor_tensor(qS[:, v, :], S[:, c, v, :], qT[:, c, :], ALU.mult).then_inc(qs_ready, 1)

                norm.gpsimd(pool, 0)
                soften(0)

                def batch(b, more):
                    for c in range(CPB):
                        k = b * CPB + c
                        ahead = c + 1 < CPB or more
                        for v in range(2):
                            read(k, c, v)
                        if ahead:
                            norm.gpsimd(pool, k + 1)
                        for v in range(2, 6):
                            read(k, c, v)
                        if ahead:
                            soften(k + 1)
                        for v in range(6, 8):
                            read(k, c, v)
                loop(pool, NB, batch)

            @block.scalar
            def _(act):
                act.sem_inc(e_ready, 1)
                act.sem_inc(qf_ready, 1)

                def front(k, c):
                    act.wait_ge(turned, k + 1)
                    nc.scalar.copy(hT[:, c, :], psT[:, :]).then_inc(hT_ready, 1)
                    act.wait_ge(neg_ready, k + 1)
                    for j in range(TPC):
                        for which in range(2):
                            col = (j % 2) * 2 * P + which * P
                            last = nc.scalar.activation(e[:, j, which, :], psL[j // 2][:, col:col + P], ACT.Exp,
                                                        bias=neg[:, j, which:which + 1],
                                                        accum_out=total[:, 2 * j + which:2 * j + which + 1])
                    last.then_inc(e_ready, 1)
                    act.wait_ge(qf_turned, k + 1)
                    nc.scalar.copy(fT[:, c, :], psF[:, :])
                    nc.scalar.copy(qT[:, c, :], psQ[:, :]).then_inc(qf_ready, 1)

                act.wait_ge(loaded, 16 * LOADS)
                nc.scalar.mul(wor[:, :, :], wor[:, :, :], float(np.float32(DV ** -0.5))).then_inc(spread, 1)
                front(0, 0)

                def batch(b, more):
                    for c in range(CPB):
                        if c + 1 < CPB or more:
                            front(b * CPB + c + 1, 1 - c)
                loop(act, NB, batch)

            @block.tensor
            def _(pe):
                pe.sem_inc(o_ready, 1)

                def turn(k):
                    pe.wait_ge(h_ready, k + 1)
                    for j in range(TPC):
                        last = nc.tensor.transpose(psT[:, j * P:(j + 1) * P], h[:, j, :], ident[:, :])
                    last.then_inc(turned, 1)

                def logits(k, c):
                    pe.wait_ge(hT_ready, k + 1)
                    pe.wait_ge(e_ready, k + 1)
                    for j in range(TPC):
                        last = nc.tensor.matmul(psL[j // 2][:, (j % 2) * 2 * P:(j % 2 + 1) * 2 * P], hT[:, c, j * P:(j + 1) * P],
                                                wqf[:, :], start=True, stop=True)
                    last.then_inc(l_ready, 1)

                def turn_softmaxes(k):
                    pe.wait_ge(soft_ready, k + 1)
                    pe.wait_ge(qf_ready, k + 1)
                    for which, ps in ((0, psQ), (1, psF)):
                        for j in range(TPC):
                            last = nc.tensor.transpose(ps[:, j * P:(j + 1) * P], e[:, j, which, :], ident[:, :])
                    last.then_inc(qf_turned, 1)

                def values(k, c, v):
                    pe.wait_ge(kv_ready, k * DV + v + 1)
                    nc.tensor.matmul(psV[v % 2][:, :], wir[:, v, :], hT[:, c, :], start=True, stop=True).then_inc(v_ready, 1)

                def batch(b, more):
                    for c in range(CPB):
                        k = b * CPB + c
                        ahead = c + 1 < CPB or more
                        for v in range(4):
                            values(k, c, v)
                        if ahead:
                            turn(k + 1)
                        values(k, c, 4)
                        if ahead:
                            logits(k + 1, 1 - c)
                        for v in range(5, 8):
                            values(k, c, v)
                        if ahead:
                            turn_softmaxes(k + 1)
                        pe.wait_ge(qs_ready, (k + 1) * DV)
                        pe.wait_ge(x_ready, k + 1)
                        for j in range(TPC):
                            for v in range(DV):
                                last = nc.tensor.matmul(psO[:, j * P:(j + 1) * P], qS[:, v, j * P:(j + 1) * P], wor[:, v, :],
                                                        start=(v == 0), stop=(v == DV - 1))
                        last.then_inc(o_ready, 1)

                pe.wait_ge(spread, DV + 1)
                turn(0)
                logits(0, 0)
                turn_softmaxes(0)
                loop(pe, NB, batch)


def expert_ffn(nc, res, tag, ins):
    X, banks, ident = res.X, res.banks, res.ident
    NCH, NT = res.T // CHUNK, res.NT
    NE, D, I = ins["L0_ffn_wi"].shape
    CAP = 256
    SLOTS, IT, ST = NE * CAP, I // P, CAP // P
    tok_dram = nc.dram_tensor(f"{tag}_tokens", [SLOTS, D], F32).ap()
    out_dram = nc.dram_tensor(f"{tag}_outs", [SLOTS + 1, D], F32).ap()
    with ExitStack() as outer:
        o = Scope(nc, outer, tag)
        Hres = o.sb("Hres", [P, NT, D])
        tok = o.sb("tok", [P, NT, D])
        weight = o.sb("weight", [P, NT])
        to_slot, from_slot = o.sb("to_slot", [P, NT], U32), o.sb("from_slot", [P, NT], U32)
        zeros = o.sb("zeros", [P, SLOTS * D // P])
        zeroed = o.sem("zeroed")

        with ExitStack() as ctx:
            m = Scope(nc, ctx, tag + "r")
            norm1, norm2 = Norm(m, res, name="ln1"), Norm(m, res, name="ln2")
            gamma, beta = m.sb("gamma", [P, D]), m.sb("beta", [P, D])
            gate = m.sb("gate", [P, NE])
            n2 = m.sb("n2", [P, TPC, D])
            t2 = m.sb("t2", [P, TPC, D])
            tT = m.sb("tT", [P, CHUNK])
            lg = m.sb("lg", [P, NE, NT])
            countdown = m.sb("countdown", [P, NE])
            best, first = m.sb("best", [P, NT]), m.sb("first", [P, NT])
            a, b_, oneh, incl = (m.sb(n, [P, NE, NT]) for n in ("a", "b", "oneh", "incl"))
            keepmask = m.sb("keepmask", [P, NE, NT])
            onehb, exclb = m.sb("onehb", [P, NE, NT], BF16), m.sb("exclb", [P, NE, NT], BF16)
            rank, keep, slot, slot2 = (m.sb(n, [P, NT]) for n in ("rank", "keep", "slot", "slot2"))
            sums = m.sb("sums", [P, NT])
            before, ones = m.sb("before", [P, P], BF16), m.sb("ones", [P, P], BF16)
            psT, psL, psR = banks[0], banks[1], banks[2]
            loaded = m.sem("loaded")
            made, ones_made = m.sem("made"), m.sem("ones_made")
            n1_ready = m.sem("n1_ready")
            n2_ready = m.sem("n2_ready")
            g_ready = m.sem("g_ready")
            t2_ready = m.sem("t2_ready")
            turned = m.sem("turned")
            tT_ready = m.sem("tT_ready")
            tok_kept = m.sem("tok_kept")
            l_ready = m.sem("l_ready")
            lg_ready = m.sem("lg_ready")
            ch = m.sem("ch")
            diff_ready, exp_ready = m.sem("diff_ready"), m.sem("exp_ready")
            count_ready, r_ready = m.sem("count_ready"), m.sem("r_ready")

            with nc.Block() as block:
                @block.sync
                def _(sp):
                    sp.dma_start(gamma[:, :], ins["L0_ffn_ln_gamma"].partition_broadcast(P)).then_inc(loaded, 16)
                    sp.dma_start(beta[:, :], ins["L0_ffn_ln_beta"].partition_broadcast(P)).then_inc(loaded, 16)
                    with nc.allow_non_contiguous_dma(reason="a small matrix, turned"):
                        sp.dma_start(gate[:, :], ins["L0_ffn_gate_weight"].rearrange("e d -> d e")).then_inc(loaded, 16)
                    sp.wait_ge(made, 1)
                    sp.dma_start(tok_dram.rearrange("(p s) d -> p (s d)", p=P), zeros[:, :]).then_inc(zeroed, 16)
                    sp.dma_start(out_dram[SLOTS:SLOTS + 1, :], zeros[0:1, 0:D]).then_inc(zeroed, 16)
                    sp.wait_ge(zeroed, 32)
                    sp.wait_ge(loaded, 48)

                @block.vector
                def _(dve):
                    dve.sem_inc(lg_ready, 1)
                    nc.vector.memset(zeros[:, :], 0.0).then_inc(made, 1)
                    nc.vector.memset(keepmask[:, :, :], 1.0).then_inc(ch, 1)
                    for e in range(NE):
                        nc.vector.memset(countdown[:, e:e + 1], float(NE - e))
                    dve.wait_ge(ch, 1)
                    nc.vector.memset(keepmask[:, :, 0:1], 0.0).then_inc(ch, 1)

                    def norms(k):
                        x = lambda j: X[:, bass.ds(k * TPC + j, 1), :]
                        hr = lambda j: Hres[:, bass.ds(k * TPC + j, 1), :]
                        norm1.vector(dve, k, x, hr).then_inc(n1_ready, 1)
                        dve.wait_ge(n1_ready, k + 1)
                        nc.vector.memset(norm2.hold[:, :], 0.0)
                        norm2.vector(dve, k, hr, lambda j: n2[:, j, :]).then_inc(n2_ready, 1)

                    def chunk(k, more):
                        if more:
                            dve.wait_ge(g_ready, k + 1)
                            norms(k + 1)
                        xk, hk = X[:, bass.ds(k * TPC, TPC), :], Hres[:, bass.ds(k * TPC, TPC), :]
                        nc.vector.tensor_tensor(xk, xk, hk, ALU.add)
                        dve.wait_ge(l_ready, k + 1)
                        nc.vector.tensor_copy(lg[:, :, bass.ds(k * TPC, TPC)],
                                              psL[:, 0:TPC * NE].rearrange("p (j e) -> p e j", e=NE)).then_inc(lg_ready, 1)

                    norms(0)
                    loop(dve, NCH, chunk)

                    steps = [2]

                    def then(ins_):
                        steps[0] += 1
                        ins_.then_inc(ch, 1)
                        dve.wait_ge(ch, steps[0])

                    by_e = lambda t: t[:, :, :].rearrange("p e t -> p t e")
                    over_e = lambda t: t[:, :].unsqueeze(1).to_broadcast([P, NE, NT])
                    over_t = lambda t: t[:, :].unsqueeze(2).to_broadcast([P, NE, NT])
                    dve.wait_ge(lg_ready, NCH + 1)
                    then(nc.vector.tensor_reduce(best[:, :], by_e(lg), AX.X, ALU.max))
                    nc.vector.tensor_tensor(a[:, :, :], lg[:, :, :], over_e(best), ALU.subtract).then_inc(diff_ready, 1)
                    then(nc.vector.tensor_tensor(b_[:, :, :], lg[:, :, :], over_e(best), ALU.is_equal))
                    then(nc.vector.tensor_tensor(b_[:, :, :], b_[:, :, :], over_t(countdown), ALU.mult))
                    then(nc.vector.tensor_reduce(first[:, :], by_e(b_), AX.X, ALU.max))
                    then(nc.vector.tensor_tensor(oneh[:, :, :], over_e(first), over_t(countdown), ALU.is_equal))
                    then(nc.vector.tensor_tensor_scan(incl[:, :, :].rearrange("p e t -> p (e t)"), keepmask[:, :, :].rearrange("p e t -> p (e t)"),
                                                      oneh[:, :, :].rearrange("p e t -> p (e t)"), 0.0, ALU.mult, ALU.add))
                    nc.vector.tensor_copy(onehb[:, :, :], oneh[:, :, :])
                    nc.vector.tensor_tensor(exclb[:, :, :], incl[:, :, :], oneh[:, :, :], ALU.subtract).then_inc(count_ready, 1)
                    dve.wait_ge(exp_ready, 1)
                    then(nc.vector.tensor_reduce(sums[:, :], by_e(a), AX.X, ALU.add))
                    then(nc.vector.reciprocal(sums[:, :], sums[:, :]))
                    dve.wait_ge(r_ready, 1)
                    then(nc.vector.tensor_tensor(b_[:, :, :], psR[:, 0:NE * NT].rearrange("p (e t) -> p e t", e=NE), oneh[:, :, :], ALU.mult))
                    then(nc.vector.tensor_reduce(rank[:, :], by_e(b_), AX.X, ALU.add))
                    then(nc.vector.tensor_scalar(keep[:, :], rank[:, :], float(CAP), None, ALU.is_lt))
                    nc.vector.tensor_tensor(weight[:, :], sums[:, :], keep[:, :], ALU.mult)
                    then(nc.vector.scalar_tensor_tensor(slot[:, :], first[:, :], -float(CAP), rank[:, :], ALU.mult, ALU.add))
                    then(nc.vector.scalar_tensor_tensor(slot[:, :], keep[:, :], -2.0 * SLOTS, slot[:, :], ALU.mult, ALU.add))
                    then(nc.vector.tensor_scalar(slot[:, :], slot[:, :], float(NE * CAP + 2 * SLOTS), None, ALU.add))
                    nc.vector.tensor_copy(to_slot[:, :], slot[:, :])
                    then(nc.vector.tensor_scalar(slot2[:, :], slot[:, :], float(SLOTS), None, ALU.min))
                    nc.vector.tensor_copy(from_slot[:, :], slot2[:, :])

                @block.gpsimd
                def _(pool):
                    pool.sem_inc(turned, 1)
                    pool.memset(ones[:, :], 1.0).then_inc(ones_made, 1)
                    pool.wait_ge(ones_made, 1)
                    pool.affine_select(out=before[:, :], in_=ones[:, :], compare_op=ALU.is_gt, fill=0.0, base=0,
                                       pattern=[[1, P]], channel_multiplier=-1).then_inc(ones_made, 1)
                    pool.wait_ge(loaded, 48)

                    def chunk(k, more):
                        norm1.gpsimd(pool, k)
                        norm2.gpsimd(pool, k)
                        pool.wait_ge(n2_ready, k + 1)
                        pool.wait_ge(turned, k + 1)
                        pool.wait_ge(tok_kept, k + 1)
                        wide = lambda t: t[:, :].unsqueeze(1).to_broadcast([P, TPC, D])
                        nc.gpsimd.tensor_tensor(t2[:, :, :], n2[:, :, :], wide(gamma), ALU.mult).then_inc(g_ready, 1)
                        pool.wait_ge(g_ready, k + 1)
                        nc.gpsimd.tensor_tensor(t2[:, :, :], t2[:, :, :], wide(beta), ALU.add).then_inc(t2_ready, 1)
                    loop(pool, NCH, chunk)

                @block.scalar
                def _(act):
                    act.sem_inc(tok_kept, 1)

                    def chunk(k, more):
                        act.wait_ge(t2_ready, k + 1)
                        nc.scalar.copy(tok[:, bass.ds(k * TPC, TPC), :], t2[:, :, :]).then_inc(tok_kept, 1)
                        act.wait_ge(turned, k + 2)
                        nc.scalar.copy(tT[:, :], psT[:, :]).then_inc(tT_ready, 1)
                    loop(act, NCH, chunk)
                    act.wait_ge(diff_ready, 1)
                    nc.scalar.activation(a[:, :, :], a[:, :, :], ACT.Exp).then_inc(exp_ready, 1)

                @block.tensor
                def _(pe):
                    pe.wait_ge(loaded, 48)

                    def chunk(k, more):
                        pe.wait_ge(t2_ready, k + 1)
                        for j in range(TPC):
                            last = nc.tensor.transpose(psT[:, j * P:(j + 1) * P], t2[:, j, :], ident[:, :])
                        last.then_inc(turned, 1)
                        pe.wait_ge(tT_ready, k + 1)
                        pe.wait_ge(lg_ready, k + 1)
                        for j in range(TPC):
                            last = nc.tensor.matmul(psL[:, j * NE:(j + 1) * NE], tT[:, j * P:(j + 1) * P], gate[:, :], start=True, stop=True)
                        last.then_inc(l_ready, 1)
                    loop(pe, NCH, chunk)
                    pe.wait_ge(ones_made, 2)
                    pe.wait_ge(count_ready, 1)
                    nc.tensor.matmul(psR[:, 0:NE * NT], before[:, :], onehb[:, :, :].rearrange("p e t -> p (e t)"), start=True, stop=False)
                    nc.tensor.matmul(psR[:, 0:NE * NT], ones[:, :], exclb[:, :, :].rearrange("p e t -> p (e t)"), start=False, stop=True).then_inc(r_ready, 1)

        with ExitStack() as ctx:
            m = Scope(nc, ctx, tag + "e")
            wi, wo = m.sb("wi", [P, 2, I]), m.sb("wo", [P, 2, IT, D])
            dsp = m.sb("dsp", [P, 2, ST, D])
            dT = m.sb("dT", [P, 2, CAP])
            hid = m.sb("hid", [P, 2, IT, CAP])
            eo = m.sb("eo", [P, 2, ST, D])
            psT, psU, psD = banks[0], banks[1:5], banks[5:7]
            scattered = m.sem("scattered")
            w_in = [m.sem(f"w_in{n}") for n in range(2)]
            d_in = [m.sem(f"d_in{n}") for n in range(2)]
            turned = m.sem("turned")
            dT_ready = m.sem("dT_ready")
            u_ready = m.sem("u_ready")
            h_ready = m.sem("h_ready")
            d_ready = m.sem("d_ready")
            eo_ready = m.sem("eo_ready")
            eo_sent = m.sem("eo_sent")
            eo_free = m.sem("eo_free")

            with nc.Block() as block:
                @block.gpsimd
                def _(pool):
                    for t in range(NT):
                        pool.indirect_dma_start(out=tok_dram, out_offset=bass.IndirectOffsetOnAxis(ap=to_slot[:, t:t + 1], axis=0),
                                                in_=tok[:, t, :], in_offset=None, bounds_check=SLOTS - 1, oob_is_err=False).then_inc(scattered, 16)
                    pool.wait_ge(scattered, 16 * NT)
                    with pool.Fori(0, NE // 2) as i:
                        for par in range(2):
                            e = i * 2 + par
                            pool.wait_ge(eo_ready, e + 3)
                            pool.dma_start(out_dram[bass.ds(e * CAP, CAP), :].rearrange("(s p) d -> p s d", p=P), eo[:, par, :, :]).then_inc(eo_sent, 16)
                            pool.wait_ge(eo_sent, e * 16 + 16)
                            pool.sem_inc(eo_free, 1)

                @block.sync
                def _(sp):
                    with sp.Fori(0, NE // 2) as i:
                        for par in range(2):
                            e = i * 2 + par
                            sp.wait_ge(d_ready, e + 1)
                            sp.dma_start(wi[:, par, :], ins["L0_ffn_wi"][bass.ds(e, 1)].rearrange("o d i -> (o d) i")).then_inc(w_in[par], 16)
                            sp.dma_start(wo[:, par, :, :], ins["L0_ffn_wo"][bass.ds(e, 1)].rearrange("o (c p) d -> (o p) c d", p=P)).then_inc(w_in[par], 16)
                            sp.wait_ge(scattered, 16 * NT)
                            sp.dma_start(dsp[:, par, :, :], tok_dram[bass.ds(e * CAP, CAP), :].rearrange("(s p) d -> p s d", p=P)).then_inc(d_in[par], 16)

                @block.scalar
                def _(act):
                    act.sem_inc(dT_ready, 1)
                    act.sem_inc(h_ready, 4)
                    act.sem_inc(eo_free, 2)
                    with act.Fori(0, NE // 2) as i:
                        for par in range(2):
                            e = i * 2 + par
                            act.wait_ge(turned, e + 1)
                            nc.scalar.copy(dT[:, par, :], psT[:, 0:CAP]).then_inc(dT_ready, 1)
                            for g in range(2):
                                act.wait_ge(u_ready, e * 2 + g + 1)
                                nc.scalar.activation(hid[:, par, 2 * g:2 * g + 2, :], psU[2 * par + g][:, :].rearrange("p (c s) -> p c s", c=2),
                                                     ACT.Gelu).then_inc(h_ready, 1)

                @block.vector
                def _(dve):
                    dve.sem_inc(eo_ready, 2)
                    with dve.Fori(0, NE // 2) as i:
                        for par in range(2):
                            e = i * 2 + par
                            dve.wait_ge(d_ready, e + 3)
                            dve.wait_ge(eo_free, e + 1)
                            nc.vector.tensor_copy(eo[:, par, :, :], psD[par][:, 0:ST * D].rearrange("p (s d) -> p s d", s=ST)).then_inc(eo_ready, 1)

                @block.tensor
                def _(pe):
                    pe.sem_inc(d_ready, 2)

                    def turn(i, par):
                        e = i * 2 + par
                        pe.wait_ge(d_in[par], i * 16 + 16)
                        pe.wait_ge(dT_ready, e + 1)
                        for s in range(ST):
                            last = nc.tensor.transpose(psT[:, s * P:(s + 1) * P], dsp[:, par, s, :], ident[:, :])
                        last.then_inc(turned, 1)

                    def pair(i, more):
                        for par in range(2):
                            e = i * 2 + par
                            pe.wait_ge(w_in[par], i * 32 + 32)
                            pe.wait_ge(dT_ready, e + 2)
                            for g in range(2):
                                pe.wait_ge(h_ready, e * 2 + g + 1)
                                for c in (2 * g, 2 * g + 1):
                                    last = nc.tensor.matmul(psU[2 * par + g][:, (c % 2) * CAP:(c % 2 + 1) * CAP], wi[:, par, c * P:(c + 1) * P],
                                                            dT[:, par, :], start=True, stop=True)
                                last.then_inc(u_ready, 1)
                            if par == 0:
                                turn(i, 1)
                            elif more:
                                turn(i + 1, 0)
                            pe.wait_ge(h_ready, e * 2 + 6)
                            pe.wait_ge(eo_ready, e + 1)
                            for s in range(ST):
                                for c in range(IT):
                                    last = nc.tensor.matmul(psD[par][:, s * D:(s + 1) * D], hid[:, par, c, s * P:(s + 1) * P], wo[:, par, c, :],
                                                            start=(c == 0), stop=(c == IT - 1))
                            last.then_inc(d_ready, 1)

                    turn(0, 0)
                    loop(pe, NE // 2, pair)

        with ExitStack() as ctx:
            m = Scope(nc, ctx, tag + "c")
            back = m.sb("back", [P, NT, D])
            came = [m.sem(f"came{n}") for n in range(NCH)]
            x_ready = m.sem("x_ready")
            with nc.Block() as block:
                @block.gpsimd
                def _(pool):
                    for t in range(NT):
                        pool.indirect_dma_start(out=back[:, t, :], out_offset=None, in_=out_dram,
                                                in_offset=bass.IndirectOffsetOnAxis(ap=from_slot[:, t:t + 1], axis=0)).then_inc(came[t // TPC], 16)

                @block.vector
                def _(dve):
                    for t in range(NT):
                        if t % TPC == 0:
                            dve.wait_ge(came[t // TPC], 16 * TPC)
                        last = nc.vector.scalar_tensor_tensor(X[:, t, :], back[:, t, :], weight[:, t:t + 1], X[:, t, :], ALU.mult, ALU.add)
                    last.then_inc(x_ready, 1)


def rope_tables(L, D, hd):
    scale = np.arange(0, hd, 2, dtype=np.float32)
    freqs = (np.float32(1.0) / np.float32(10000.0) ** scale).astype(np.float32)
    angles = np.arange(L, dtype=np.float32)[:, None] * freqs[None, :]
    cos, sin = np.cos(angles).astype(np.float32), np.sin(angles).astype(np.float32)
    cos = np.tile(np.repeat(cos, 2, axis=1), (1, D // hd))
    sin = np.tile(np.stack([-sin, sin], axis=-1).reshape(L, hd), (1, D // hd))
    head = np.arange(D) // hd
    diag = (head[:, None] == head[None, :]).astype(np.float32) / np.sqrt(np.float32(hd))
    return cos, sin, diag.astype(np.float32)


def rope_attention(nc, res, tag, ins):
    X, banks, ident = res.X, res.banks, res.ident
    NB, CPB = res.B, res.L // CHUNK
    TPB = res.L // P
    assert CPB == 2
    with ExitStack() as ctx:
        m = Scope(nc, ctx, tag)
        norm = Norm(m, res)
        wqkv = m.sb("wqkv", [P, 3 * P])
        wo = m.sb("wo", [P, P])
        bqkv = m.sb("bqkv", [P, 3 * P])
        bo = m.sb("bo", [P, P])
        cos, sin = m.sb("cos", [P, TPB, P]), m.sb("sin", [P, TPB, P])
        diag = m.sb("diag", [P, P])
        h = m.sb("h", [P, TPC, P])
        hT = m.sb("hT", [P, CHUNK])
        raw = m.sb("raw", [P, CPB, TPC, 3 * P])
        byc = m.sb("byc", [P, CPB, TPC, 2 * P])
        bys = m.sb("bys", [P, CPB, TPC, 2 * P])
        qT = m.sb("qT", [P, CPB, CHUNK])
        vk = m.sb("vk", [P, P])
        G = m.sb("G_", [P, P])
        psT, psP, psKV, psQ, psG, psO = banks[0], banks[1:3], banks[3], banks[4], banks[5], banks[6:8]
        loaded = m.sem("loaded")
        h_ready = m.sem("h_ready")
        turned = m.sem("turned")
        hT_ready = m.sem("hT_ready")
        p_ready = m.sem("p_ready")
        raw_ready = m.sem("raw_ready")
        byc_ready = m.sem("byc_ready")
        bys_ready = m.sem("bys_ready")
        rot_ready = m.sem("rot_ready")
        used = m.sem("used")
        qT_ready = m.sem("qT_ready")
        vk_ready = m.sem("vk_ready")
        g_product = m.sem("g_product")
        g_ready = m.sem("g_ready")
        o_ready = m.sem("o_ready")
        x_ready = m.sem("x_ready")
        x_done = m.sem("x_done")

        def pairs(ap, first):
            return ap.rearrange("p j (n t) -> p j n t", t=2)[:, :, :, first:first + 1].squeeze(3)

        with nc.Block() as block:
            @block.sync
            def _(sp):
                for n, name in enumerate(("Wq", "Wk", "Wv")):
                    sp.dma_start(wqkv[:, n * P:(n + 1) * P], ins["L1_attn_a_" + name]).then_inc(loaded, 16)
                for n, name in enumerate(("bq", "bk", "bv")):
                    sp.dma_start(bqkv[:, n * P:(n + 1) * P], ins["L1_attn_a_" + name].partition_broadcast(P)).then_inc(loaded, 16)
                sp.dma_start(cos[:, :, :], ins["rope_cos"].rearrange("(t p) d -> p t d", p=P)).then_inc(loaded, 16)
                sp.dma_start(sin[:, :, :], ins["rope_sin"].rearrange("(t p) d -> p t d", p=P)).then_inc(loaded, 16)
                sp.dma_start(diag[:, :], ins["head_diag"]).then_inc(loaded, 16)
                sp.dma_start(wo[:, :], ins["L1_attn_a_Wo"]).then_inc(loaded, 16)
                sp.dma_start(bo[:, :], ins["L1_attn_a_bo"].partition_broadcast(P)).then_inc(loaded, 16)
                sp.wait_ge(loaded, 11 * 16)

            @block.vector
            def _(dve):
                dve.sem_inc(raw_ready, 2)
                dve.sem_inc(vk_ready, 1)
                dve.sem_inc(x_done, 1)

                def norm_chunk(k):
                    norm.vector(dve, k, lambda j: X[:, bass.ds(k * TPC + j, 1), :], lambda j: h[:, j, :]).then_inc(h_ready, 1)

                def batch(b, more):
                    for c in range(CPB):
                        k = b * CPB + c
                        dve.wait_ge(used, k + 1)
                        for j in range(TPC):
                            dve.wait_ge(p_ready, k * TPC + j + 1)
                            nc.vector.tensor_tensor(raw[:, c, j, :], psP[j % 2][:, 0:3 * P], bqkv[:, :], ALU.add).then_inc(raw_ready, 1)
                        dve.wait_ge(raw_ready, (k + 1) * TPC + 2)
                        for half in range(2):
                            s = slice(half * P, (half + 1) * P)
                            last = nc.vector.tensor_tensor(byc[:, c, :, s], raw[:, c, :, s],
                                                           cos[:, c * TPC:(c + 1) * TPC, :], ALU.mult)
                        last.then_inc(byc_ready, 1)
                        if c + 1 < CPB or more:
                            norm_chunk(k + 1)
                        dve.wait_ge(byc_ready, k + 1)
                        dve.wait_ge(bys_ready, k + 1)
                        nc.vector.tensor_tensor(byc[:, c, :, :], byc[:, c, :, :], bys[:, c, :, :], ALU.add).then_inc(rot_ready, 1)
                    dve.wait_ge(used, (b + 1) * CPB + 2)
                    nc.vector.tensor_tensor(vk[:, :], psKV[:, 0:P], diag[:, :], ALU.mult).then_inc(vk_ready, 1)
                    dve.wait_ge(o_ready, b + 1)
                    for c in range(CPB):
                        xk = X[:, bass.ds(b * TPB + c * TPC, TPC), :]
                        nc.vector.tensor_tensor(xk, xk, psO[c][:, :].rearrange("p (j n) -> p j n", j=TPC), ALU.add).then_inc(x_ready, 1)
                    dve.wait_ge(x_ready, b * 2 + 2)
                    xb = X[:, bass.ds(b * TPB, TPB), :]
                    nc.vector.tensor_tensor(xb, xb, bo[:, :].unsqueeze(1).to_broadcast([P, TPB, P]), ALU.add).then_inc(x_done, 1)

                norm_chunk(0)
                dve.wait_ge(loaded, 11 * 16)
                loop(dve, NB, batch)

            @block.gpsimd
            def _(pool):
                norm.gpsimd(pool, 0)
                pool.wait_ge(loaded, 11 * 16)

                def batch(b, more):
                    for c in range(CPB):
                        k = b * CPB + c
                        if c + 1 < CPB or more:
                            norm.gpsimd(pool, k + 1)
                        pool.wait_ge(raw_ready, (k + 1) * TPC + 2)
                        for half in range(2):
                            s = slice(half * P, (half + 1) * P)
                            for first in range(2):
                                last = nc.gpsimd.tensor_tensor(pairs(bys[:, c, :, s], first), pairs(raw[:, c, :, s], 1 - first),
                                                               pairs(sin[:, c * TPC:(c + 1) * TPC, :], first), ALU.mult)
                        last.then_inc(bys_ready, 1)
                loop(pool, NB, batch)

            @block.scalar
            def _(act):
                act.sem_inc(hT_ready, 1)
                act.sem_inc(qT_ready, 1)

                def copy_hT(k):
                    act.wait_ge(turned, k + 1)
                    nc.scalar.copy(hT[:, :], psT[:, :]).then_inc(hT_ready, 1)

                def batch(b, more):
                    for c in range(CPB):
                        k = b * CPB + c
                        if c + 1 < CPB or more:
                            copy_hT(k + 1)
                        act.wait_ge(used, k + 3)
                        nc.scalar.copy(qT[:, c, :], psQ[:, :]).then_inc(qT_ready, 1)
                    act.wait_ge(g_product, b + 1)
                    nc.scalar.copy(G[:, :], psG[:, 0:P]).then_inc(g_ready, 1)

                copy_hT(0)
                loop(act, NB, batch)

            @block.tensor
            def _(pe):
                pe.sem_inc(used, 2)

                def turn(k):
                    pe.wait_ge(h_ready, k + 1)
                    pe.wait_ge(hT_ready, k + 1)
                    for j in range(TPC):
                        last = nc.tensor.transpose(psT[:, j * P:(j + 1) * P], h[:, j, :], ident[:, :])
                    last.then_inc(turned, 1)

                def batch(b, more):
                    for c in range(CPB):
                        k = b * CPB + c
                        pe.wait_ge(hT_ready, k + 2)
                        for j in range(TPC):
                            pe.wait_ge(raw_ready, k * TPC + j + 1)
                            nc.tensor.matmul(psP[j % 2][:, 0:3 * P], hT[:, j * P:(j + 1) * P], wqkv[:, :],
                                             start=True, stop=True).then_inc(p_ready, 1)
                        if c + 1 < CPB or more:
                            turn(k + 1)
                        pe.wait_ge(rot_ready, k + 1)
                        if c == 0:
                            pe.wait_ge(vk_ready, b + 1)
                        for j in range(TPC):
                            nc.tensor.matmul(psKV[:, 0:P], raw[:, c, j, 2 * P:3 * P], byc[:, c, j, P:2 * P],
                                             start=(c == 0 and j == 0), stop=(c == CPB - 1 and j == TPC - 1))
                        pe.wait_ge(qT_ready, k + 1)
                        for j in range(TPC):
                            last = nc.tensor.transpose(psQ[:, j * P:(j + 1) * P], byc[:, c, j, 0:P], ident[:, :])
                        last.then_inc(used, 1)
                    pe.wait_ge(vk_ready, b + 2)
                    nc.tensor.matmul(psG[:, 0:P], vk[:, :], wo[:, :], start=True, stop=True).then_inc(g_product, 1)
                    pe.wait_ge(g_ready, b + 1)
                    pe.wait_ge(x_done, b + 1)
                    pe.wait_ge(qT_ready, (b + 1) * CPB + 1)
                    for c in range(CPB):
                        for j in range(TPC):
                            last = nc.tensor.matmul(psO[c][:, j * P:(j + 1) * P], qT[:, c, j * P:(j + 1) * P], G[:, :],
                                                    start=True, stop=True)
                    last.then_inc(o_ready, 1)

                turn(0)
                pe.wait_ge(loaded, 11 * 16)
                loop(pe, NB, batch)


def alibi_rows(L, H):
    import math
    start = 2.0 ** (-2.0 ** (-(math.log2(H) - 3)))
    slopes = np.array([start * start ** i for i in range(H)], dtype=np.float32)
    bf = mybir.dt.np(BF16)
    parts, rest = [], slopes
    for _ in range(3):
        parts.append(rest.astype(bf))
        rest = rest - parts[-1].astype(np.float32)
    pos = np.arange(L)
    tile, place = (pos // P * P).astype(bf), (pos % P).astype(bf)
    keys, queries = np.zeros((H, 12, L), bf), np.zeros((H, 12, L), bf)
    for n, part in enumerate(parts):
        keys[:, 4 * n], queries[:, 4 * n] = tile, part[:, None]
        keys[:, 4 * n + 1], queries[:, 4 * n + 1] = place, part[:, None]
        keys[:, 4 * n + 2], queries[:, 4 * n + 2] = part[:, None], -tile
        keys[:, 4 * n + 3], queries[:, 4 * n + 3] = part[:, None], -place
    return keys, queries


MASKED = -1e30


def softmax_attention(nc, res, tag, w):
    X, banks, ident = res.X, res.banks, res.ident
    NB, L, D, H, DK, DV = res.B, res.L, P, w.H, w.DK, w.DV
    NCH, CPB, TPB = res.T // CHUNK, L // CHUNK, L // P
    E = DV + 1
    NV = H * DV
    VB = -(-NV // 512)
    VW = min(NV, 512)
    HPV = VW // DV
    qk_dram = nc.dram_tensor(f"{tag}_qk", [2, 3, D, res.T], BF16).ap()
    v_dram = nc.dram_tensor(f"{tag}_v", [NB, H, P, TPB, E], F32).ap()
    m_dram = nc.dram_tensor(f"{tag}_m", [NB * H, 2, TPB, P], BF16).ap()

    with ExitStack() as ctx:
        m = Scope(nc, ctx, tag + "p")
        norm = Norm(m, res)
        wq, wk, wv = m.sb("wq", [P, D]), m.sb("wk", [P, D]), m.sb("wv", [P, NV])
        h = m.sb("h", [P, TPC, P])
        hT = m.sb("hT", [P, CHUNK])
        qk = m.sb("qk", [P, 2, CHUNK])
        parts = m.sb("parts", [P, 2, 3, CHUNK], BF16)
        rest = m.sb("rest", [P, 2, CHUNK])
        vout = m.sb("vout", [P, H, TPC, E])
        if w.biases:
            bq, bk, bv, bo = m.sb("bq", [P, 1]), m.sb("bk", [P, 1]), m.sb("bv", [P, NV]), m.sb("bo", [P, P])
            temp, qscale, qbias = m.sb("temp", [P, 1]), m.sb("qscale", [P, 1]), m.sb("qbias", [P, 1])
        psT, psQK, psV = banks[0], banks[1:3], banks[3:7]
        loaded = m.sem("loaded")
        NLOAD = 3 + 5 * bool(w.biases)
        scaled = m.sem("scaled")
        ones_set = m.sem("ones_set")
        h_ready = m.sem("h_ready")
        turned = m.sem("turned")
        hT_ready = m.sem("hT_ready")
        qk_product = m.sem("qk_product")
        qk_ready = m.sem("qk_ready")
        part1 = m.sem("part1")
        rest1 = m.sem("rest1")
        part2 = m.sem("part2")
        part3 = m.sem("part3")
        qk_sent = m.sem("qk_sent")
        v_product = m.sem("v_product")
        v_ready = m.sem("v_ready")
        v_sent = m.sem("v_sent")
        VPC = TPC * VB

        with nc.Block() as block:
            @block.sync
            def _(sp):
                sp.sem_inc(qk_sent, 32)
                sp.sem_inc(v_sent, 16)
                for t, src in ((wq, w.Wq), (wk, w.Wk), (wv, w.Wv)):
                    sp.dma_start(t[:, :], src).then_inc(loaded, 16)
                if w.biases:
                    for t, src in ((bq, w.bq), (bk, w.bk)):
                        sp.dma_start(t[:, :], src.rearrange("(p o) -> p o", o=1)).then_inc(loaded, 16)
                    for t, src in ((bv, w.bv), (bo, w.bo), (temp, w.temperature)):
                        sp.dma_start(t[:, :], src.partition_broadcast(P)).then_inc(loaded, 16)

                def batch(b, more):
                    for c in range(CPB):
                        k = b * CPB + c
                        sp.wait_ge(part3, k + 2)
                        for n in range(2):
                            sp.dma_start(qk_dram[n, :, :, bass.ds(k * CHUNK, CHUNK)].rearrange("r p t -> p r t"),
                                         parts[:, n, :, :]).then_inc(qk_sent, 16)
                        sp.wait_ge(v_ready, (k + 1) * VPC + 4)
                        sp.dma_start(v_dram[bass.ds(b, 1), :, :, c * TPC:(c + 1) * TPC, :].rearrange("o h p t e -> p (o h) (t e)"),
                                     vout[:, :, :, :].rearrange("p h t e -> p h (t e)")).then_inc(v_sent, 16)
                loop(sp, NB, batch)
                sp.wait_ge(qk_sent, 32 * NCH + 32)
                sp.wait_ge(v_sent, 16 * (NCH + 1))

            @block.vector
            def _(dve):
                dve.sem_inc(v_ready, 4)
                dve.memset(vout[:, :, :, DV:E], 1.0).then_inc(ones_set, 1)

                def norm_chunk(k):
                    norm.vector(dve, k, lambda j: X[:, bass.ds(k * TPC + j, 1), :], lambda j: h[:, j, :]).then_inc(h_ready, 1)
                    if w.biases:
                        dve.wait_ge(h_ready, k + 1)
                        xk = X[:, bass.ds(k * TPC, TPC), :]
                        nc.vector.tensor_tensor(xk, xk, bo[:, :].unsqueeze(1).to_broadcast([P, TPC, P]), ALU.add)

                def chunk(k, more):
                    if more:
                        dve.wait_ge(turned, k + 1)
                        norm_chunk(k + 1)
                    dve.wait_ge(part1, k + 1)
                    nc.vector.tensor_tensor(rest[:, :, :], qk[:, :, :], parts[:, :, 0, :], ALU.subtract).then_inc(rest1, 1)
                    dve.wait_ge(v_sent, k * 16 + 16)
                    for n in range(VPC):
                        j, vb = n // VB, n % VB
                        dve.wait_ge(v_product, k * VPC + n + 1)
                        dst = vout[:, vb * HPV:(vb + 1) * HPV, j, 0:DV]
                        src = psV[n % 4][:, 0:VW].rearrange("p (h d) -> p h d", d=DV)
                        if w.biases:
                            nc.vector.tensor_tensor(dst, src, bv[:, :].rearrange("p (h d) -> p h d", d=DV), ALU.add).then_inc(v_ready, 1)
                        else:
                            nc.vector.tensor_copy(dst, src).then_inc(v_ready, 1)

                dve.wait_ge(loaded, NLOAD * 16)
                if w.biases:
                    dve.tensor_scalar(temp[:, :], temp[:, :], float(np.float32(np.sqrt(DK))), None, ALU.mult).then_inc(scaled, 1)
                    dve.wait_ge(scaled, 1)
                    dve.reciprocal(qscale[:, :], temp[:, :]).then_inc(scaled, 1)
                    dve.wait_ge(scaled, 2)
                    dve.tensor_tensor(qbias[:, :], bq[:, :], qscale[:, :], ALU.mult).then_inc(scaled, 1)
                norm_chunk(0)
                dve.wait_ge(ones_set, 1)
                loop(dve, NCH, chunk)

            @block.gpsimd
            def _(pool):
                pool.sem_inc(part3, 1)
                norm.gpsimd(pool, 0)

                def chunk(k, more):
                    if more:
                        norm.gpsimd(pool, k + 1)
                    pool.wait_ge(part2, k + 1)
                    nc.gpsimd.tensor_tensor(parts[:, :, 2, :], rest[:, :, :], parts[:, :, 1, :], ALU.subtract).then_inc(part3, 1)
                loop(pool, NCH, chunk)

            @block.scalar
            def _(act):
                act.sem_inc(hT_ready, 1)
                act.sem_inc(qk_ready, 1)

                def copy_hT(k):
                    act.wait_ge(turned, k + 1)
                    nc.scalar.copy(hT[:, :], psT[:, :]).then_inc(hT_ready, 1)

                def chunk(k, more):
                    act.wait_ge(part3, k + 1)
                    act.wait_ge(qk_product, k + 1)
                    if w.biases:
                        nc.scalar.activation(qk[:, 0, :], psQK[0][:, :], ACT.Identity, bias=qbias[:, 0:1], scale=qscale[:, 0:1])
                        nc.scalar.activation(qk[:, 1, :], psQK[1][:, :], ACT.Identity, bias=bk[:, 0:1]).then_inc(qk_ready, 1)
                    else:
                        nc.scalar.activation(qk[:, 0, :], psQK[0][:, :], ACT.Copy, scale=float(np.float32(DK ** -0.5)))
                        nc.scalar.copy(qk[:, 1, :], psQK[1][:, :]).then_inc(qk_ready, 1)
                    act.wait_ge(qk_ready, k + 2)
                    act.wait_ge(qk_sent, 32 * k + 32)
                    nc.scalar.copy(parts[:, :, 0, :], qk[:, :, :]).then_inc(part1, 1)
                    act.wait_ge(rest1, k + 1)
                    nc.scalar.copy(parts[:, :, 1, :], rest[:, :, :]).then_inc(part2, 1)
                    if more:
                        copy_hT(k + 1)

                copy_hT(0)
                if w.biases:
                    act.wait_ge(scaled, 3)
                loop(act, NCH, chunk)

            @block.tensor
            def _(pe):
                def turn(k):
                    pe.wait_ge(h_ready, k + 1)
                    pe.wait_ge(hT_ready, k + 1)
                    for j in range(TPC):
                        last = nc.tensor.transpose(psT[:, j * P:(j + 1) * P], h[:, j, :], ident[:, :])
                    last.then_inc(turned, 1)

                def chunk(k, more):
                    pe.wait_ge(hT_ready, k + 2)
                    pe.wait_ge(qk_ready, k + 1)
                    for n, weight in enumerate((wq, wk)):
                        last = nc.tensor.matmul(psQK[n][:, :], weight[:, :], hT[:, :], start=True, stop=True)
                    last.then_inc(qk_product, 1)
                    for n in range(VPC):
                        j, vb = n // VB, n % VB
                        pe.wait_ge(v_ready, k * VPC + n + 1)
                        nc.tensor.matmul(psV[n % 4][:, 0:VW], hT[:, j * P:(j + 1) * P], wv[:, vb * VW:(vb + 1) * VW],
                                         start=True, stop=True).then_inc(v_product, 1)
                        if n == VPC - 1 and more:
                            turn(k + 1)

                turn(0)
                pe.wait_ge(loaded, NLOAD * 16)
                loop(pe, NCH, chunk)

    NH = NB * H
    RING, AHEAD = 8, 6
    R0 = 9 * DK + (12 if w.alibi else 0)
    R1 = R0 + 2
    OG = D // DV
    MAXES = [(j, 0, min(512, (j + 1) * P)) for j in range(TPB)] + [(j, 512, (j + 1) * P - 512) for j in range(4, TPB)]
    PROBS = [(i, i * P, 512 - i * P) for i in range(4)] + [(i, max(512, i * P), L - max(512, i * P)) for i in range(TPB)]
    at, col = {}, 0
    first_col = []
    for i, q0, nq in PROBS:
        first_col.append(col)
        for q in range(q0, q0 + nq, P):
            at[i, q // P] = col
            col += P
    NPR, NMX = len(PROBS), len(MAXES)
    LOADS = 7 + 2 * bool(w.alibi)
    assert L == 1024 and 64 < R0 and R1 <= P and NH % 2 == 0

    with ExitStack() as ctx:
        m = Scope(nc, ctx, tag + "a")
        qs, ks = m.sb("qs", [P, RING, L], BF16), m.sb("ks", [P, RING, L], BF16)
        vs = m.sb("vs", [P, RING, TPB * E])
        probs = m.sb("probs", [P, 2, col])
        identb, upper, lower = m.sb("identb", [P, P], BF16), m.sb("upper", [P, P], BF16), m.sb("lower", [P, P], BF16)
        mx, mh = m.sb("mx", [P, 2, NMX]), m.sb("mh", [P, 2, TPB])
        mparts = m.sb("mparts", [TPB, 2, 2, P], BF16)
        inv = m.sb("inv", [P, TPB])
        ctxs = m.sb("ctxs", [P, TPB, D])
        ctxT = m.sb("ctxT", [P, 2, CHUNK])
        wo = m.sb("wo", [P, H // OG, D])
        psM, psS, psO, psT, psY = banks[0:2], banks[2:4], banks[4:6], banks[6], banks[7]
        mT = psY[0:TPB, 0:P]
        mask_made = m.sem("mask_made")
        ring_set = m.sem("ring_set")
        wo_in = m.sem("wo_in")
        head_in = [m.sem(f"head_in{n}") for n in range(2)]
        m_product = m.sem("m_product")
        m_taken = m.sem("m_taken")
        mh_ready = m.sem("mh_ready")
        mT_ready = m.sem("mT_ready")
        mp_first = m.sem("mp_first")
        mp_ready = m.sem("mp_ready")
        m_sent = m.sem("m_sent")
        mparts_free = m.sem("mparts_free")
        m_in = m.sem("m_in")
        s_product = m.sem("s_product")
        p_ready = m.sem("p_ready")
        o_product = m.sem("o_product")
        inv_ready = m.sem("inv_ready")
        c_ready = m.sem("c_ready")
        c_turned = m.sem("c_turned")
        cT_ready = m.sem("cT_ready")
        y_product = m.sem("y_product")
        x_ready = m.sem("x_ready")
        PPG = OG // 2

        def schedule(eng, pair, project):
            NP, LAST = NH // 2, (NH - AHEAD) // 2
            if PPG == 1:
                with eng.Fori(0, LAST) as p:
                    pair(p, 0, True, False)
                    project(p, True)
                with eng.Fori(LAST, NP - 1) as p:
                    pair(p, 0, False, False)
                    project(p, False)
                pair(NP - 1, 0, False, True)
                project(NP - 1, False)
            else:
                G = NP // PPG
                with eng.Fori(0, G - 1) as g:
                    with eng.Fori(0, PPG) as q:
                        pair(g * PPG + q, q, True, False)
                    project(g, True)
                with eng.Fori((G - 1) * PPG, LAST) as p:
                    pair(p, p - (G - 1) * PPG, True, False)
                with eng.Fori(LAST, NP - 1) as p:
                    pair(p, p - (G - 1) * PPG, False, False)
                pair(NP - 1, PPG - 1, False, True)
                project(G - 1, False)

        with nc.Block() as block:
            @block.sync
            def _(sp):
                sp.dma_start(wo[:, :, :], w.Wo.rearrange("(g p) n -> p g n", p=P)).then_inc(wo_in, 16)
                sp.wait_ge(ring_set, 1)

                def load(b, half, slot):
                    par, hd = slot % 2, half * RING + slot
                    pair = b * (H // 2) + half * (RING // 2) + slot // 2
                    toks, rows = bass.ds(b * L, L), bass.ds(hd * DK, DK)
                    sp.wait_ge(o_product, pair * 4 + par * 2 + 2)
                    sp.wait_ge(head_in[par], pair * LOADS * 16 + LOADS * 16)
                    for r in range(3):
                        rr = slice(3 * DK * r, 3 * DK * (r + 1))
                        sp.dma_start(qs[rr, slot, :], qk_dram[0, :, rows, toks]).then_inc(head_in[par], 16)
                        sp.dma_start(ks[rr, slot, :], qk_dram[1, r:r + 1, rows, toks].to_broadcast([3, DK, L])).then_inc(head_in[par], 16)
                    if w.alibi:
                        for t, rows12 in ((qs, w.alibi_q), (ks, w.alibi_k)):
                            sp.dma_start(t[9 * DK:R0, slot, :], rows12[bass.ds(hd, 1)].rearrange("o r t -> (o r) t")).then_inc(head_in[par], 16)
                    sp.dma_start(vs[:, slot, :], v_dram[bass.ds(b, 1), bass.ds(hd, 1)].rearrange("o u p t e -> (o u p) (t e)")).then_inc(head_in[par], 16)

                sp.sem_inc(head_in[0], LOADS * 16)
                sp.sem_inc(head_in[1], LOADS * 16)
                with sp.Fori(0, NB) as b:
                    with sp.Fori(0, H // RING) as half:
                        for slot in range(RING):
                            load(b, half, slot)

            @block.gpsimd
            def _(pool):
                pool.memset(ks[:, :, :], 1.0).then_inc(ring_set, 1)
                pool.sem_inc(mparts_free, 2)
                for t in (identb, upper, lower):
                    pool.memset(t[:, :], 0.0).then_inc(mask_made, 1)
                pool.wait_ge(mask_made, 3)
                pool.affine_select(out=identb[:, :], in_=identb[:, :], compare_op=ALU.not_equal, fill=1.0, base=0,
                                   pattern=[[-1, P]], channel_multiplier=1).then_inc(mask_made, 1)
                pool.affine_select(out=upper[:, :], in_=upper[:, :], compare_op=ALU.is_ge, fill=MASKED, base=0,
                                   pattern=[[-1, P]], channel_multiplier=1).then_inc(mask_made, 1)
                pool.affine_select(out=lower[:, :], in_=lower[:, :], compare_op=ALU.is_ge, fill=MASKED, base=0,
                                   pattern=[[1, P]], channel_multiplier=-1).then_inc(mask_made, 1)
                with pool.Fori(0, NH // 2) as p:
                    for par in range(2):
                        n = p * 2 + par
                        pool.wait_ge(mp_ready, n + 2)
                        pool.dma_start(m_dram[bass.ds(n, 1)].rearrange("o r j q -> (o j) r q"), mparts[:, par, :, :]).then_inc(m_sent, 16)
                        pool.wait_ge(m_sent, 16 * n + 16)
                        pool.sem_inc(mparts_free, 1)
                        pool.dma_start(qs[R0:R1, bass.ds(n % RING, 1), :],
                                       m_dram[bass.ds(n, 1)].rearrange("o r j q -> (o r) (j q)")).then_inc(m_in, 16)
                        pool.wait_ge(m_in, 16 * n + 16)

            @block.vector
            def _(dve):
                dve.sem_inc(m_taken, 2)
                dve.sem_inc(c_ready, 2)
                dve.sem_inc(mp_ready, 1)
                dve.sem_inc(x_ready, 1)

                def maximum(a, par, idx):
                    _, _, nk = MAXES[idx]
                    dve.wait_ge(m_product, a * NMX + idx + 1)
                    nc.vector.tensor_reduce(mx[:, par, idx:idx + 1], psM[idx % 2][:, 0:nk], AX.X, ALU.max).then_inc(m_taken, 1)

                def join_maxima(a, par):
                    dve.wait_ge(m_taken, (a + 1) * NMX + 2)
                    nc.vector.tensor_copy(mh[:, par, 0:4], mx[:, par, 0:4])
                    nc.vector.tensor_tensor(mh[:, par, 4:TPB], mx[:, par, 4:TPB], mx[:, par, TPB:NMX], ALU.max).then_inc(mh_ready, 1)

                def split_maxima(a, par):
                    dve.wait_ge(mT_ready, a + 1)
                    dve.wait_ge(mparts_free, a + 1)
                    nc.vector.tensor_scalar(mparts[:, par, 0, :], mT, -1.0, None, ALU.mult).then_inc(mp_first, 1)
                    dve.wait_ge(mp_first, a + 1)
                    nc.vector.scalar_tensor_tensor(mparts[:, par, 1, :], mT, -1.0, mparts[:, par, 0, :],
                                                   ALU.mult, ALU.subtract).then_inc(mp_ready, 1)

                def normalise(n, g, col0):
                    o = psO[g][:, 0:4 * E].rearrange("p (j e) -> p j e", e=E)
                    js = slice(4 * g, 4 * g + 4)
                    dve.wait_ge(o_product, n * 2 + g + 1 + 2 * RING)
                    nc.vector.reciprocal(inv[:, js].unsqueeze(2), o[:, :, DV:E]).then_inc(inv_ready, 1)
                    dve.wait_ge(inv_ready, n * 2 + g + 1)
                    nc.vector.tensor_tensor(ctxs[:, js, col0], o[:, :, 0:DV],
                                            inv[:, js].unsqueeze(2).to_broadcast([P, 4, DV]), ALU.mult).then_inc(c_ready, 1)

                def pair(p, q, maxima, last):
                    for par in range(2):
                        n = p * 2 + par
                        col0 = bass.ds((q * 2 + par) * DV, DV) if PPG > 1 else slice(par * DV, (par + 1) * DV)
                        a = n + AHEAD
                        if maxima:
                            for idx in range(NMX // 2):
                                maximum(a, par, idx)
                        normalise(n, 0, col0)
                        if maxima:
                            for idx in range(NMX // 2, NMX):
                                maximum(a, par, idx)
                            join_maxima(a, par)
                        normalise(n, 1, col0)
                        if maxima:
                            split_maxima(a, par)

                def project(g, maxima):
                    for half in range(2):
                        dve.wait_ge(y_product, g * 2 + half + 1)
                        tiles = X[:, bass.ds(g * OG // H * TPB + 4 * half, 4), :]
                        nc.vector.tensor_tensor(tiles, tiles, psY[:, :].rearrange("p (j n) -> p j n", j=4), ALU.add).then_inc(x_ready, 1)

                with dve.Fori(0, AHEAD // 2) as p:
                    for par in range(2):
                        for idx in range(NMX):
                            maximum(p * 2 + par, par, idx)
                        join_maxima(p * 2 + par, par)
                        split_maxima(p * 2 + par, par)
                schedule(dve, pair, project)

            @block.scalar
            def _(act):
                act.sem_inc(p_ready, 2)
                act.sem_inc(cT_ready, 1)

                def exps(n, par):
                    for idx, (i, q0, nq) in enumerate(PROBS):
                        act.wait_ge(s_product, n * NPR + idx + 1)
                        nc.scalar.activation(probs[:, par, first_col[idx]:first_col[idx] + nq], psS[idx % 2][:, 0:nq],
                                             ACT.Exp).then_inc(p_ready, 1)

                def pair(p, q, maxima, last):
                    exps(p * 2 + 1, 1)
                    if not last:
                        exps(p * 2 + 2, 0)

                def project(g, maxima):
                    for half in range(2):
                        act.wait_ge(c_turned, g * 2 + half + 1)
                        nc.scalar.copy(ctxT[:, half, :], psT[:, :]).then_inc(cT_ready, 1)

                exps(0, 0)
                schedule(act, pair, project)

            @block.tensor
            def _(pe):
                pe.sem_inc(o_product, 2 * RING)

                def max_scores(a, idx):
                    j, k0, nk = MAXES[idx]
                    slot = a % RING
                    pe.wait_ge(m_taken, a * NMX + idx + 1)
                    diagonal = k0 + nk == (j + 1) * P
                    last = nc.tensor.matmul(psM[idx % 2][:, 0:nk], qs[0:R0, slot, j * P:(j + 1) * P],
                                            ks[0:R0, slot, k0:k0 + nk], start=True, stop=not diagonal)
                    if diagonal:
                        last = nc.tensor.matmul(psM[idx % 2][:, nk - P:nk], identb[:, :], upper[:, :], start=False, stop=True)
                    last.then_inc(m_product, 1)

                def scores(n, idx):
                    i, q0, nq = PROBS[idx]
                    slot = n % RING
                    if idx == 0:
                        pe.wait_ge(m_in, 16 * n + 16)
                    pe.wait_ge(p_ready, n * NPR + idx + 1)
                    diagonal = q0 == i * P
                    last = nc.tensor.matmul(psS[idx % 2][:, 0:nq], ks[0:R1, slot, i * P:(i + 1) * P],
                                            qs[0:R1, slot, q0:q0 + nq], start=True, stop=not diagonal)
                    if diagonal:
                        last = nc.tensor.matmul(psS[idx % 2][:, 0:P], identb[:, :], lower[:, :], start=False, stop=True)
                    last.then_inc(s_product, 1)

                def turn_maxima(a, par):
                    pe.wait_ge(mh_ready, a + 1)
                    pe.wait_ge(mp_ready, a + 1)
                    nc.tensor.transpose(mT, mh[:, par, :], ident[:, :]).then_inc(mT_ready, 1)

                def outputs(n, par, blocks):
                    for j, i in blocks:
                        g = j // 4
                        if i == 0 and j % 4 == 0:
                            pe.wait_ge(c_ready, n * 2 + g + 1)
                        need = max(x for x, (t, q0, nq) in enumerate(PROBS) if t <= j and q0 <= j * P < q0 + nq)
                        if i == 0:
                            pe.wait_ge(p_ready, n * NPR + need + 3)
                        c0 = at[i, j]
                        last = nc.tensor.matmul(psO[g][:, (j % 4) * E:(j % 4 + 1) * E], probs[:, par, c0:c0 + P],
                                                vs[:, n % RING, i * E:(i + 1) * E], start=(i == 0), stop=(i == j))
                        if i == j and j % 4 == 3:
                            last.then_inc(o_product, 1)

                BLOCKS = [(j, i) for j in range(TPB) for i in range(j + 1)]
                PER = -(-len(BLOCKS) // NPR)

                def pair(p, q, maxima, last):
                    for par in range(2):
                        n = p * 2 + par
                        a = n + AHEAD
                        if maxima:
                            pe.wait_ge(head_in[par], (p + AHEAD // 2 + 2) * LOADS * 16)
                            max_scores(a, 0)
                        for step in range(NPR):
                            if not (last and par == 1):
                                scores(n + 1, step)
                            if maxima and step + 1 < NMX:
                                max_scores(a, step + 1)
                            outputs(n, par, BLOCKS[step * PER:(step + 1) * PER])
                        if maxima:
                            pe.wait_ge(x_ready, p // PPG * 2 + 1)
                            turn_maxima(a, par)

                def project(g, maxima):
                    pe.wait_ge(mp_ready, (g + 1) * OG + AHEAD + 1 if maxima else NH + 1)
                    for half in range(2):
                        pe.wait_ge(c_ready, (g + 1) * 2 * OG + 1 + half)
                        pe.wait_ge(cT_ready, g * 2 + half + 1)
                        for j in range(4):
                            last = nc.tensor.transpose(psT[:, j * P:(j + 1) * P], ctxs[:, half * 4 + j, :], ident[:, :])
                        last.then_inc(c_turned, 1)
                    for half in range(2):
                        pe.wait_ge(cT_ready, g * 2 + half + 2)
                        pe.wait_ge(x_ready, g * 2 + half + 1)
                        for j in range(4):
                            last = nc.tensor.matmul(psY[:, j * P:(j + 1) * P], ctxT[:, half, j * P:(j + 1) * P],
                                                    wo[:, g % (H // OG), :], start=True, stop=True)
                        last.then_inc(y_product, 1)

                pe.wait_ge(mask_made, 6)
                pe.wait_ge(wo_in, 16)
                with pe.Fori(0, AHEAD // 2) as p:
                    for par in range(2):
                        pe.wait_ge(head_in[par], (p + 2) * LOADS * 16)
                        for idx in range(NMX):
                            max_scores(p * 2 + par, idx)
                        turn_maxima(p * 2 + par, par)
                for idx in range(NPR):
                    scores(0, idx)
                schedule(pe, pair, project)


class Res:
    pass


def build_program(nc, ins, out):
    x_dram = ins["L0_attn_a_hidden_states"]
    B, L, D = x_dram.shape
    T = B * L
    NT = T // P
    res = Res()
    res.B, res.L, res.T, res.NT = B, L, T, NT
    with ExitStack() as ctx:
        g = Scope(nc, ctx, "g")
        res.X = X = g.sb("x", [P, NT, P])
        res.ident = ident = g.sb("ident", [P, P])
        res.banks = [ctx.enter_context(nc.psum_tensor(f"bank{i}", [P, 512], F32)) for i in range(8)]
        res.minus_half = g.sb("minus_half", [P, 8])
        x_in, w_in, id_ready, x_out = g.sem("x_in"), g.sem("w_in"), g.sem("id_ready"), g.sem("x_out")

        f = Res()
        DH = ins["L1_ffn_w1_w"].shape[0]
        HT = DH // P
        f.w1T, f.w2T = g.sb("w1T", [P, DH]), g.sb("w2T", [P, DH])
        f.h1T, f.h2T, f.w3T = g.sb("h1T", [P, HT, DH]), g.sb("h2T", [P, HT, DH]), g.sb("w3T", [P, HT, P])
        f.s1, f.s2, f.sh1, f.sh2 = (g.sb(n, [P, HT]) for n in ("s1", "s2", "sh1", "sh2"))
        f.s3 = g.sb("s3", [P, P])
        with ExitStack() as ctx2:
            ld = Scope(nc, ctx2, "ld")
            nat = {n: ld.sb(n, [P, HT, D]) for n in ("w1_w", "w2_w")}
            nat |= {n: ld.sb(n, [P, HT, DH]) for n in ("h1_w", "h2_w")}
            nat["w3_w"] = ld.sb("w3_w", [P, DH])
            with nc.Block() as block:
                @block.sync
                def _(sp):
                    for b in range(B):
                        sp.dma_start(X[:, b * L // P:(b + 1) * L // P, :],
                                     x_dram[b].rearrange("(t p) d -> p t d", p=P)).then_inc(x_in, 16)
                    sp.wait_ge(x_in, 16 * B)

                @block.scalar
                def _(act):
                    n = 0
                    for name in ("w1_w", "w2_w", "h1_w", "h2_w"):
                        act.dma_start(nat[name][:, :, :], ins["L1_ffn_" + name].rearrange("(o p) i -> p o i", p=P)).then_inc(w_in, 16)
                    act.dma_start(nat["w3_w"][:, :], ins["L1_ffn_w3_w"]).then_inc(w_in, 16)
                    with nc.allow_non_contiguous_dma(reason="one scale a partition"):
                        for name, t in (("w1_s", f.s1), ("w2_s", f.s2), ("h1_s", f.sh1), ("h2_s", f.sh2)):
                            act.dma_start(t[:, :], ins["L1_ffn_" + name].rearrange("(o p) -> p o", p=P)).then_inc(w_in, 16)
                    act.dma_start(f.s3[:, :], ins["L1_ffn_w3_s"].partition_broadcast(P)).then_inc(w_in, 16)
                    act.wait_ge(w_in, 160)

                @block.gpsimd
                def _(pool):
                    pool.memset(res.minus_half[:, :], -0.5)
                    pool.memset(ident[:, :], 0.0).then_inc(id_ready, 1)
                    pool.wait_ge(id_ready, 1)
                    pool.affine_select(out=ident[:, :], in_=ident[:, :], compare_op=ALU.not_equal, fill=1.0, base=0,
                                       pattern=[[-1, P]], channel_multiplier=1).then_inc(id_ready, 1)

            jobs = []
            for o in range(HT):
                so = slice(o * P, (o + 1) * P)
                jobs += [(f.w1T[:, so], nat["w1_w"][:, o, :]), (f.w2T[:, so], nat["w2_w"][:, o, :])]
                for i in range(HT):
                    si = slice(i * P, (i + 1) * P)
                    jobs += [(f.h1T[:, i, so], nat["h1_w"][:, o, si]), (f.h2T[:, i, so], nat["h2_w"][:, o, si])]
                jobs.append((f.w3T[:, o, :], nat["w3_w"][:, so]))
            transpose_blocks(nc, res, "ffnw", jobs, [(w_in, 160), (id_ready, 2)])

        wb = Res()
        wb.Wq, wb.Wk, wb.Wv, wb.Wo = (ins["L0_attn_b_" + n] for n in ("Wq", "Wk", "Wv", "Wo"))
        wb.H, wb.DK, wb.DV, wb.biases, wb.alibi = 16, 8, 64, False, False
        wc = Res()
        wat, bat = ins["L1_attn_b_W_attn"], ins["L1_attn_b_b_attn"]
        wc.Wq, wc.Wk, wc.Wv = (wat[:, n * D:(n + 1) * D] for n in range(3))
        wc.bq, wc.bk, wc.bv = (bat[n * D:(n + 1) * D] for n in range(3))
        wc.Wo, wc.bo, wc.temperature = ins["L1_attn_b_W_proj"], ins["L1_attn_b_b_proj"], ins["L1_attn_b_temperature"]
        wc.alibi_q, wc.alibi_k = ins["alibi_q"], ins["alibi_k"]
        wc.H, wc.DK, wc.DV, wc.biases, wc.alibi = 16, 8, 8, True, True
        steps = [lambda: gated_attention(nc, res, 'gla', ins), lambda: expert_ffn(nc, res, 'moe1', ins), lambda: softmax_attention(nc, res, "sma", wb), lambda: expert_ffn(nc, res, 'moe2', ins), lambda: rope_attention(nc, res, 'rope', ins),
                 lambda: ternary_ffn(nc, res, "ffn5", f), lambda: softmax_attention(nc, res, "smb", wc),
                 lambda: ternary_ffn(nc, res, "ffn7", f)]
        for step in steps:
            with nc.cleanup_on_exit():
                step()

        with nc.Block() as block:
            @block.sync
            def _(sp):
                for b in range(B):
                    sp.dma_start(out[b].rearrange("(t p) d -> p t d", p=P), X[:, b * L // P:(b + 1) * L // P, :]).then_inc(x_out, 16)
                sp.wait_ge(x_out, 16 * B)


def kernel(**inputs):
    import numpy as _np
    import concourse.bacc as _bacc
    from concourse import mybir as _mybir
    from concourse.bass_utils import run_bass_kernel_spmd as _run

    nc = _bacc.Bacc("TRN2", target_bir_lowering=False, num_devices=1)
    arrays, args = {}, {}
    x = inputs["L0_attn_a_hidden_states"]
    items = dict(inputs)
    items["rope_cos"], items["rope_sin"], items["head_diag"] = rope_tables(x.shape[1], x.shape[2], x.shape[2] // HEADS)
    items["alibi_k"], items["alibi_q"] = alibi_rows(x.shape[1], HEADS)
    for name, a in items.items():
        a = _np.ascontiguousarray(a)
        arrays[f"in_{name}_dram"] = a
        args[name] = nc.dram_tensor(f"in_{name}_dram", a.shape, _mybir.dt.from_np(a.dtype), kind="ExternalInput").ap()
    out = nc.dram_tensor("out_0_dram", x.shape, F32, kind="ExternalOutput").ap()
    build_program(nc, args, out)
    r = _run(nc, [arrays], core_ids=[0])
    return r.results[0]["out_0_dram"]
```

```python
from contextlib import ExitStack

import numpy as np

import concourse.bass as bass
from concourse import mybir

F32 = mybir.dt.float32
BF16 = mybir.dt.bfloat16
U32 = mybir.dt.uint32
ALU = mybir.AluOpType
ACT = mybir.ActivationFunctionType
AX = mybir.AxisListType

P = 128
CHUNK = 512
TPC = CHUNK // P
EPS = 1e-5
HEADS = 16


class Scope:

    def __init__(self, nc, ctx, tag):
        self.nc, self.ctx, self.tag = nc, ctx, tag

    def sb(self, name, shape, dt=F32):
        return self.ctx.enter_context(self.nc.sbuf_tensor(f"{self.tag}_{name}", shape, dt))

    def sem(self, name):
        return self.nc.alloc_semaphore(name=f"{self.tag}_{name}")


def loop(eng, n, body):
    if n > 1:
        with eng.Fori(0, n - 1) as k:
            body(k, True)
    body(n - 1, False)


class Norm:

    def __init__(self, m, res, tiles=TPC, name="ln"):
        self.tiles = tiles
        self.minus_half = res.minus_half
        self.stats = m.sb(f"{name}_stats", [P, tiles, 6])
        self.mv = m.sb(f"{name}_mv", [P, tiles, 2])
        self.var = m.sb(f"{name}_var", [P, tiles])
        self.rstd = m.sb(f"{name}_rstd", [P, tiles])
        self.hold = m.sb(f"{name}_hold", [P, 1])
        self.step = m.sem(f"{name}_step")
        self.root = m.sem(f"{name}_root")

    def vector(self, dve, k, src, dst):
        for j in range(self.tiles):
            last = dve.bn_stats(self.stats[:, j, :], src(j))
        last.then_inc(self.step, 1)
        dve.wait_ge(self.step, k * 3 + 1)
        dve.memset(self.hold[:, :], 0.0)
        for j in range(self.tiles):
            last = dve.bn_aggr(self.mv[:, j, :], self.stats[:, j, :])
        last.then_inc(self.step, 1)
        dve.wait_ge(self.step, k * 3 + 2)
        dve.tensor_scalar(self.var[:, :], self.mv[:, :, 1], EPS, None, ALU.add).then_inc(self.step, 1)
        dve.wait_ge(self.root, k + 1)
        for j in range(self.tiles):
            last = dve.tensor_scalar(dst(j), src(j), self.mv[:, j, 0:1], self.rstd[:, j:j + 1],
                                     ALU.subtract, ALU.mult)
        return last

    def gpsimd(self, pool, k):
        pool.wait_ge(self.step, k * 3 + 3)
        pool.tensor_tensor(self.rstd[:, :], self.var[:, :], self.minus_half[:, 0:self.tiles], ALU.pow).then_inc(self.root, 1)


def transpose_blocks(nc, res, tag, jobs, arrived):
    turned, copied = nc.alloc_semaphore(name=f"{tag}_turned"), nc.alloc_semaphore(name=f"{tag}_copied")
    NB = len(res.banks)
    with nc.Block() as block:
        @block.tensor
        def _(pe):
            for sem, n in arrived:
                pe.wait_ge(sem, n)
            for i, (_, src) in enumerate(jobs):
                if i >= NB:
                    pe.wait_ge(copied, i - NB + 1)
                nc.tensor.transpose(res.banks[i % NB][:, 0:P], src, res.ident[:, :]).then_inc(turned, 1)

        @block.scalar
        def _(act):
            for i, (dst, _) in enumerate(jobs):
                act.wait_ge(turned, i + 1)
                nc.scalar.copy(dst, res.banks[i % NB][:, 0:P]).then_inc(copied, 1)


def ternary_ffn(nc, res, tag, w):
    X, banks, ident = res.X, res.banks, res.ident
    NCH = res.T // CHUNK
    HT = w.w1T.shape[1] // P
    with ExitStack() as ctx:
        m = Scope(nc, ctx, tag)
        norm = Norm(m, res)
        h = m.sb("h", [P, TPC, P])
        hT = m.sb("hT", [P, CHUNK])
        gate = m.sb("gate", [P, HT, CHUNK])
        acts = [m.sb(f"act{n}", [P, HT, CHUNK]) for n in range(3)]
        scaled = m.sb("scaled", [P, TPC, P])
        psA, psB, psT, psO = banks[0:3], banks[3:5], banks[5], banks[6]
        h_ready = m.sem("h_ready")
        turned = m.sem("turned")
        hT_ready = m.sem("hT_ready")
        a_ready = m.sem("a_ready")
        a_out = m.sem("a_out")
        b_ready = m.sem("b_ready")
        b_out = m.sem("b_out")
        o_ready = m.sem("o_ready")
        o_out = m.sem("o_out")
        x_ready = m.sem("x_ready")
        EARLY = HT // 2

        def place(layer, mt, more):
            return {0: HT + mt + (HT if mt >= EARLY else 0), 1: mt, 2: HT + mt + (EARLY if more else 0)}[layer]

        with nc.Block() as block:
            @block.vector
            def _(dve):
                dve.sem_inc(b_out, 2)
                dve.sem_inc(o_out, 1)
                dve.sem_inc(x_ready, 1)

                def norm_chunk(k):
                    norm.vector(dve, k, lambda j: X[:, bass.ds(k * TPC + j, 1), :], lambda j: h[:, j, :]).then_inc(h_ready, 1)

                def gated(k, mt, n):
                    dve.wait_ge(b_ready, k * HT + mt + 1)
                    dve.wait_ge(a_out, n + 4)
                    nc.vector.scalar_tensor_tensor(acts[0][:, mt, :], psB[mt % 2][:, :], w.s2[:, mt:mt + 1],
                                                   gate[:, mt, :], ALU.mult, ALU.mult).then_inc(b_out, 1)

                def chunk(k, more):
                    if more:
                        dve.wait_ge(turned, k + 1)
                        norm_chunk(k + 1)
                        for mt in range(HT):
                            gated(k + 1, mt, HT + k * 3 * HT + place(0, mt, more))
                    dve.wait_ge(x_ready, k + 1)
                    dve.wait_ge(o_ready, k + 1)
                    nc.vector.tensor_tensor(scaled[:, :, :], psO[:, :].rearrange("p (j n) -> p j n", j=TPC),
                                            w.s3[:, :].unsqueeze(1).to_broadcast([P, TPC, P]), ALU.mult).then_inc(o_out, 1)
                    dve.wait_ge(o_out, k + 2)
                    xk = X[:, bass.ds(k * TPC, TPC), :]
                    nc.vector.tensor_tensor(xk, xk, scaled[:, :, :], ALU.add).then_inc(x_ready, 1)

                norm_chunk(0)
                for mt in range(HT):
                    gated(0, mt, mt)
                loop(dve, NCH, chunk)

            @block.gpsimd
            def _(pool):
                with pool.Fori(0, NCH) as k:
                    norm.gpsimd(pool, k)

            @block.scalar
            def _(act):
                act.sem_inc(hT_ready, 1)
                act.sem_inc(a_out, 3)

                def copy_hT(k):
                    act.wait_ge(turned, k + 1)
                    nc.scalar.copy(hT[:, :], psT[:, :]).then_inc(hT_ready, 1)

                def silu(mt, n, bank):
                    act.wait_ge(a_ready, n + 1)
                    nc.scalar.activation(gate[:, mt, :], psA[bank][:, :], ACT.Silu, scale=w.s1[:, mt:mt + 1]).then_inc(a_out, 1)

                def chunk(k, more):
                    first = HT + k * 3 * HT

                    def gelu(layer, scale, mt):
                        n = place(layer, mt, more)
                        act.wait_ge(a_ready, first + n + 1)
                        nc.scalar.activation(acts[layer][:, mt, :], psA[(HT + n) % 3][:, :], ACT.Gelu,
                                             scale=scale[:, mt:mt + 1]).then_inc(a_out, 1)

                    def next_silu(mts):
                        for mt in mts:
                            n = place(0, mt, more)
                            silu(mt, first + n, (HT + n) % 3)

                    for mt in range(HT):
                        gelu(1, w.sh1, mt)
                        if more and mt == HT - 2:
                            copy_hT(k + 1)
                    if more:
                        next_silu(range(EARLY))
                    for mt in range(HT):
                        gelu(2, w.sh2, mt)
                    if more:
                        next_silu(range(EARLY, HT))

                copy_hT(0)
                for mt in range(HT):
                    silu(mt, mt, mt % 3)
                loop(act, NCH, chunk)

            @block.tensor
            def _(pe):
                def turn(k):
                    pe.wait_ge(h_ready, k + 1)
                    pe.wait_ge(hT_ready, k + 1)
                    for j in range(TPC):
                        last = nc.tensor.transpose(psT[:, j * P:(j + 1) * P], h[:, j, :], ident[:, :])
                    last.then_inc(turned, 1)

                def first_layer(k, mt, n, bank):
                    pe.wait_ge(hT_ready, k + 2)
                    pe.wait_ge(a_out, n + 1)
                    nc.tensor.matmul(psA[bank][:, :], w.w1T[:, mt * P:(mt + 1) * P], hT[:, :],
                                     start=True, stop=True).then_inc(a_ready, 1)
                    pe.wait_ge(b_out, k * HT + mt + 1)
                    nc.tensor.matmul(psB[mt % 2][:, :], w.w2T[:, mt * P:(mt + 1) * P], hT[:, :],
                                     start=True, stop=True).then_inc(b_ready, 1)

                def chunk(k, more):
                    first = HT + k * 3 * HT

                    def hidden(layer, wT, mt):
                        n = place(layer, mt, more)
                        pe.wait_ge(a_out, first + n + 1)
                        for kt in range(HT):
                            if mt == 0:
                                if layer == 1:
                                    pe.wait_ge(b_out, k * HT + kt + 3)
                                else:
                                    pe.wait_ge(a_out, first + place(1, kt, more) + 4)
                            last = nc.tensor.matmul(psA[(HT + n) % 3][:, :], wT[:, kt, mt * P:(mt + 1) * P],
                                                    acts[layer - 1][:, kt, :], start=(kt == 0), stop=(kt == HT - 1))
                        last.then_inc(a_ready, 1)

                    def next_layer(mts):
                        for mt in mts:
                            n = place(0, mt, more)
                            first_layer(k + 1, mt, first + n, (HT + n) % 3)

                    for mt in range(HT):
                        if more and mt == HT - 1:
                            turn(k + 1)
                        hidden(1, w.h1T, mt)
                    if more:
                        next_layer(range(EARLY))
                    for mt in range(HT):
                        hidden(2, w.h2T, mt)
                    if more:
                        next_layer(range(EARLY, HT))
                    pe.wait_ge(o_out, k + 1)
                    pe.wait_ge(a_out, first + place(2, HT - 1, more) + 4)
                    for j in range(TPC):
                        for kt in range(HT):
                            last = nc.tensor.matmul(psO[:, j * P:(j + 1) * P], acts[2][:, kt, j * P:(j + 1) * P],
                                                    w.w3T[:, kt, :], start=(kt == 0), stop=(kt == HT - 1))
                    last.then_inc(o_ready, 1)

                turn(0)
                for mt in range(HT):
                    first_layer(0, mt, mt, mt % 3)
                loop(pe, NCH, chunk)


def gated_attention(nc, res, tag, ins):
    X, banks, ident = res.X, res.banks, res.ident
    NB, CPB, TPB = res.B, res.L // CHUNK, res.L // P
    D, H = P, 16
    DV = D // H
    assert CPB == 2
    with ExitStack() as ctx:
        m = Scope(nc, ctx, tag)
        norm = Norm(m, res)
        wqf, wi = m.sb("wqf", [P, 2 * D]), m.sb("wi", [P, D])
        wir, wor = m.sb("wir", [P, DV, D]), m.sb("wor", [P, DV, D])
        h = m.sb("h", [P, TPC, P])
        hT = m.sb("hT", [P, CPB, CHUNK])
        neg, total, inv = m.sb("neg", [P, TPC, 2]), m.sb("total", [P, TPC * 2]), m.sb("inv", [P, TPC * 2])
        e = m.sb("e", [P, TPC, 2, P])
        qT, fT, kT = (m.sb(n, [P, CPB, CHUNK]) for n in ("qT", "fT", "kT"))
        kv = m.sb("kv", [P, 2, CHUNK])
        S = m.sb("S", [P, CPB, DV, CHUNK])
        qS = m.sb("qS", [P, DV, CHUNK])
        psT, psL, psV, psQ, psF, psO = banks[0], banks[1:3], banks[3:5], banks[5], banks[6], banks[7]
        loaded = m.sem("loaded")
        spread = m.sem("spread")
        h_ready = m.sem("h_ready")
        turned = m.sem("turned")
        hT_ready = m.sem("hT_ready")
        l_ready = m.sem("l_ready")
        neg_ready = m.sem("neg_ready")
        e_ready = m.sem("e_ready")
        inv_ready = m.sem("inv_ready")
        soft_ready = m.sem("soft_ready")
        qf_turned = m.sem("qf_turned")
        qf_ready = m.sem("qf_ready")
        k_ready = m.sem("k_ready")
        v_ready = m.sem("v_ready")
        kv_ready = m.sem("kv_ready")
        s_ready = m.sem("s_ready")
        qs_ready = m.sem("qs_ready")
        o_ready = m.sem("o_ready")
        x_ready = m.sem("x_ready")
        LOADS = 3 + DV

        with nc.Block() as block:
            @block.sync
            def _(sp):
                for t, name in ((wqf[:, 0:D], "Wq"), (wqf[:, D:2 * D], "Wf"), (wi[:, :], "Wi")):
                    sp.dma_start(t, ins["L0_attn_a_" + name]).then_inc(loaded, 16)
                rows = ins["L0_attn_a_Wo"].rearrange("(h v) n -> v h n", v=DV)
                for v in range(DV):
                    sp.dma_start(wor[:, v, :], rows[v].unsqueeze(1).to_broadcast([H, DV, D])).then_inc(loaded, 16)
                sp.wait_ge(loaded, 16 * LOADS)

            @block.vector
            def _(dve):
                dve.sem_inc(k_ready, 1)
                dve.sem_inc(kv_ready, 2)
                dve.sem_inc(x_ready, 1)

                def norm_chunk(k):
                    norm.vector(dve, k, lambda j: X[:, bass.ds(k * TPC + j, 1), :], lambda j: h[:, j, :]).then_inc(h_ready, 1)

                def maxima(k):
                    dve.wait_ge(l_ready, k + 1)
                    for half in range(2):
                        last = nc.vector.tensor_reduce(neg[:, 2 * half:2 * half + 2, :], psL[half][:, :].rearrange("p (j w n) -> p j w n", j=2, w=2),
                                                       AX.X, ALU.max, negate=True)
                    last.then_inc(neg_ready, 1)

                def inverse(k):
                    dve.wait_ge(e_ready, k + 2)
                    nc.vector.reciprocal(inv[:, :], total[:, :]).then_inc(inv_ready, 1)

                def one_minus(k, c):
                    dve.wait_ge(qf_ready, k + 2)
                    nc.vector.tensor_scalar(kT[:, c, :], fT[:, c, :], -1.0, 1.0, ALU.mult, ALU.add).then_inc(k_ready, 1)

                def scan(k, c, v):
                    n = k * DV + v
                    dve.wait_ge(v_ready, n + 1)
                    if v == 0:
                        dve.wait_ge(k_ready, k + 2)
                    nc.vector.tensor_tensor(kv[:, v % 2, :], psV[v % 2][:, :], kT[:, c, :], ALU.mult).then_inc(kv_ready, 1)
                    dve.wait_ge(kv_ready, n + 3)
                    nc.vector.tensor_tensor_scan(S[:, c, v, :], fT[:, c, :], kv[:, v % 2, :],
                                                 0.0 if c == 0 else S[:, 0, v, CHUNK - 1:CHUNK], ALU.mult, ALU.add).then_inc(s_ready, 1)

                dve.wait_ge(loaded, 16 * LOADS)
                for v in range(DV):
                    nc.vector.tensor_copy(wir[:, v, :].rearrange("p (h k) -> p h k", k=DV),
                                          wi[:, :].rearrange("p (h v) -> p v h", v=DV)[:, v, :].unsqueeze(2).to_broadcast([P, H, DV])).then_inc(spread, 1)
                norm_chunk(0)
                maxima(0)
                inverse(0)
                one_minus(0, 0)

                def batch(b, more):
                    for c in range(CPB):
                        k = b * CPB + c
                        ahead = c + 1 < CPB or more
                        for v in range(2):
                            scan(k, c, v)
                        if ahead:
                            norm_chunk(k + 1)
                        for v in range(2, 4):
                            scan(k, c, v)
                        if ahead:
                            maxima(k + 1)
                        for v in range(4, 6):
                            scan(k, c, v)
                        if ahead:
                            inverse(k + 1)
                        for v in range(6, 8):
                            scan(k, c, v)
                        if ahead:
                            one_minus(k + 1, 1 - c)
                        dve.wait_ge(o_ready, k + 2)
                        xk = X[:, bass.ds(k * TPC, TPC), :]
                        nc.vector.tensor_tensor(xk, xk, psO[:, :].rearrange("p (j n) -> p j n", j=TPC), ALU.add).then_inc(x_ready, 1)
                loop(dve, NB, batch)

            @block.gpsimd
            def _(pool):
                def soften(k):
                    pool.wait_ge(inv_ready, k + 1)
                    ev = e[:, :, :, :].rearrange("p j w n -> p (j w) n")
                    nc.gpsimd.tensor_tensor(ev, ev, inv[:, :].unsqueeze(2).to_broadcast([P, 2 * TPC, P]), ALU.mult).then_inc(soft_ready, 1)

                def read(k, c, v):
                    if v == 0:
                        pool.wait_ge(o_ready, k + 1)
                    pool.wait_ge(s_ready, k * DV + v + 1)
                    nc.gpsimd.tensor_tensor(qS[:, v, :], S[:, c, v, :], qT[:, c, :], ALU.mult).then_inc(qs_ready, 1)

                norm.gpsimd(pool, 0)
                soften(0)

                def batch(b, more):
                    for c in range(CPB):
                        k = b * CPB + c
                        ahead = c + 1 < CPB or more
                        for v in range(2):
                            read(k, c, v)
                        if ahead:
                            norm.gpsimd(pool, k + 1)
                        for v in range(2, 6):
                            read(k, c, v)
                        if ahead:
                            soften(k + 1)
                        for v in range(6, 8):
                            read(k, c, v)
                loop(pool, NB, batch)

            @block.scalar
            def _(act):
                act.sem_inc(e_ready, 1)
                act.sem_inc(qf_ready, 1)

                def front(k, c):
                    act.wait_ge(turned, k + 1)
                    nc.scalar.copy(hT[:, c, :], psT[:, :]).then_inc(hT_ready, 1)
                    act.wait_ge(neg_ready, k + 1)
                    for j in range(TPC):
                        for which in range(2):
                            col = (j % 2) * 2 * P + which * P
                            last = nc.scalar.activation(e[:, j, which, :], psL[j // 2][:, col:col + P], ACT.Exp,
                                                        bias=neg[:, j, which:which + 1],
                                                        accum_out=total[:, 2 * j + which:2 * j + which + 1])
                    last.then_inc(e_ready, 1)
                    act.wait_ge(qf_turned, k + 1)
                    nc.scalar.copy(fT[:, c, :], psF[:, :])
                    nc.scalar.copy(qT[:, c, :], psQ[:, :]).then_inc(qf_ready, 1)

                act.wait_ge(loaded, 16 * LOADS)
                nc.scalar.mul(wor[:, :, :], wor[:, :, :], float(np.float32(DV ** -0.5))).then_inc(spread, 1)
                front(0, 0)

                def batch(b, more):
                    for c in range(CPB):
                        if c + 1 < CPB or more:
                            front(b * CPB + c + 1, 1 - c)
                loop(act, NB, batch)

            @block.tensor
            def _(pe):
                pe.sem_inc(o_ready, 1)

                def turn(k):
                    pe.wait_ge(h_ready, k + 1)
                    for j in range(TPC):
                        last = nc.tensor.transpose(psT[:, j * P:(j + 1) * P], h[:, j, :], ident[:, :])
                    last.then_inc(turned, 1)

                def logits(k, c):
                    pe.wait_ge(hT_ready, k + 1)
                    pe.wait_ge(e_ready, k + 1)
                    for j in range(TPC):
                        last = nc.tensor.matmul(psL[j // 2][:, (j % 2) * 2 * P:(j % 2 + 1) * 2 * P], hT[:, c, j * P:(j + 1) * P],
                                                wqf[:, :], start=True, stop=True)
                    last.then_inc(l_ready, 1)

                def turn_softmaxes(k):
                    pe.wait_ge(soft_ready, k + 1)
                    pe.wait_ge(qf_ready, k + 1)
                    for which, ps in ((0, psQ), (1, psF)):
                        for j in range(TPC):
                            last = nc.tensor.transpose(ps[:, j * P:(j + 1) * P], e[:, j, which, :], ident[:, :])
                    last.then_inc(qf_turned, 1)

                def values(k, c, v):
                    pe.wait_ge(kv_ready, k * DV + v + 1)
                    nc.tensor.matmul(psV[v % 2][:, :], wir[:, v, :], hT[:, c, :], start=True, stop=True).then_inc(v_ready, 1)

                def batch(b, more):
                    for c in range(CPB):
                        k = b * CPB + c
                        ahead = c + 1 < CPB or more
                        for v in range(4):
                            values(k, c, v)
                        if ahead:
                            turn(k + 1)
                        values(k, c, 4)
                        if ahead:
                            logits(k + 1, 1 - c)
                        for v in range(5, 8):
                            values(k, c, v)
                        if ahead:
                            turn_softmaxes(k + 1)
                        pe.wait_ge(qs_ready, (k + 1) * DV)
                        pe.wait_ge(x_ready, k + 1)
                        for j in range(TPC):
                            for v in range(DV):
                                last = nc.tensor.matmul(psO[:, j * P:(j + 1) * P], qS[:, v, j * P:(j + 1) * P], wor[:, v, :],
                                                        start=(v == 0), stop=(v == DV - 1))
                        last.then_inc(o_ready, 1)

                pe.wait_ge(spread, DV + 1)
                turn(0)
                logits(0, 0)
                turn_softmaxes(0)
                loop(pe, NB, batch)


def expert_ffn(nc, res, tag, ins):
    X, banks, ident = res.X, res.banks, res.ident
    NCH, NT = res.T // CHUNK, res.NT
    NE, D, I = ins["L0_ffn_wi"].shape
    CAP = 256
    SLOTS, IT, ST = NE * CAP, I // P, CAP // P
    tok_dram = nc.dram_tensor(f"{tag}_tokens", [SLOTS, D], F32).ap()
    out_dram = nc.dram_tensor(f"{tag}_outs", [SLOTS + 1, D], F32).ap()
    with ExitStack() as outer:
        o = Scope(nc, outer, tag)
        Hres = o.sb("Hres", [P, NT, D])
        tok = o.sb("tok", [P, NT, D])
        weight = o.sb("weight", [P, NT])
        to_slot, from_slot = o.sb("to_slot", [P, NT], U32), o.sb("from_slot", [P, NT], U32)
        zeros = o.sb("zeros", [P, SLOTS * D // P])
        zeroed = o.sem("zeroed")

        with ExitStack() as ctx:
            m = Scope(nc, ctx, tag + "r")
            norm1, norm2 = Norm(m, res, name="ln1"), Norm(m, res, name="ln2")
            gamma, beta = m.sb("gamma", [P, D]), m.sb("beta", [P, D])
            gate = m.sb("gate", [P, NE])
            n2 = m.sb("n2", [P, TPC, D])
            t2 = m.sb("t2", [P, TPC, D])
            tT = m.sb("tT", [P, CHUNK])
            lg = m.sb("lg", [P, NE, NT])
            countdown = m.sb("countdown", [P, NE])
            best, first = m.sb("best", [P, NT]), m.sb("first", [P, NT])
            a, b_, oneh, incl = (m.sb(n, [P, NE, NT]) for n in ("a", "b", "oneh", "incl"))
            keepmask = m.sb("keepmask", [P, NE, NT])
            onehb, exclb = m.sb("onehb", [P, NE, NT], BF16), m.sb("exclb", [P, NE, NT], BF16)
            rank, keep, slot, slot2 = (m.sb(n, [P, NT]) for n in ("rank", "keep", "slot", "slot2"))
            sums = m.sb("sums", [P, NT])
            before, ones = m.sb("before", [P, P], BF16), m.sb("ones", [P, P], BF16)
            psT, psL, psR = banks[0], banks[1], banks[2]
            loaded = m.sem("loaded")
            made, ones_made = m.sem("made"), m.sem("ones_made")
            n1_ready = m.sem("n1_ready")
            n2_ready = m.sem("n2_ready")
            g_ready = m.sem("g_ready")
            t2_ready = m.sem("t2_ready")
            turned = m.sem("turned")
            tT_ready = m.sem("tT_ready")
            tok_kept = m.sem("tok_kept")
            l_ready = m.sem("l_ready")
            lg_ready = m.sem("lg_ready")
            ch = m.sem("ch")
            diff_ready, exp_ready = m.sem("diff_ready"), m.sem("exp_ready")
            count_ready, r_ready = m.sem("count_ready"), m.sem("r_ready")

            with nc.Block() as block:
                @block.sync
                def _(sp):
                    sp.dma_start(gamma[:, :], ins["L0_ffn_ln_gamma"].partition_broadcast(P)).then_inc(loaded, 16)
                    sp.dma_start(beta[:, :], ins["L0_ffn_ln_beta"].partition_broadcast(P)).then_inc(loaded, 16)
                    with nc.allow_non_contiguous_dma(reason="a small matrix, turned"):
                        sp.dma_start(gate[:, :], ins["L0_ffn_gate_weight"].rearrange("e d -> d e")).then_inc(loaded, 16)
                    sp.wait_ge(made, 1)
                    sp.dma_start(tok_dram.rearrange("(p s) d -> p (s d)", p=P), zeros[:, :]).then_inc(zeroed, 16)
                    sp.dma_start(out_dram[SLOTS:SLOTS + 1, :], zeros[0:1, 0:D]).then_inc(zeroed, 16)
                    sp.wait_ge(zeroed, 32)
                    sp.wait_ge(loaded, 48)

                @block.vector
                def _(dve):
                    dve.sem_inc(lg_ready, 1)
                    nc.vector.memset(zeros[:, :], 0.0).then_inc(made, 1)
                    nc.vector.memset(keepmask[:, :, :], 1.0).then_inc(ch, 1)
                    for e in range(NE):
                        nc.vector.memset(countdown[:, e:e + 1], float(NE - e))
                    dve.wait_ge(ch, 1)
                    nc.vector.memset(keepmask[:, :, 0:1], 0.0).then_inc(ch, 1)

                    def norms(k):
                        x = lambda j: X[:, bass.ds(k * TPC + j, 1), :]
                        hr = lambda j: Hres[:, bass.ds(k * TPC + j, 1), :]
                        norm1.vector(dve, k, x, hr).then_inc(n1_ready, 1)
                        dve.wait_ge(n1_ready, k + 1)
                        nc.vector.memset(norm2.hold[:, :], 0.0)
                        norm2.vector(dve, k, hr, lambda j: n2[:, j, :]).then_inc(n2_ready, 1)

                    def chunk(k, more):
                        if more:
                            dve.wait_ge(g_ready, k + 1)
                            norms(k + 1)
                        xk, hk = X[:, bass.ds(k * TPC, TPC), :], Hres[:, bass.ds(k * TPC, TPC), :]
                        nc.vector.tensor_tensor(xk, xk, hk, ALU.add)
                        dve.wait_ge(l_ready, k + 1)
                        nc.vector.tensor_copy(lg[:, :, bass.ds(k * TPC, TPC)],
                                              psL[:, 0:TPC * NE].rearrange("p (j e) -> p e j", e=NE)).then_inc(lg_ready, 1)

                    norms(0)
                    loop(dve, NCH, chunk)

                    steps = [2]

                    def then(ins_):
                        steps[0] += 1
                        ins_.then_inc(ch, 1)
                        dve.wait_ge(ch, steps[0])

                    by_e = lambda t: t[:, :, :].rearrange("p e t -> p t e")
                    over_e = lambda t: t[:, :].unsqueeze(1).to_broadcast([P, NE, NT])
                    over_t = lambda t: t[:, :].unsqueeze(2).to_broadcast([P, NE, NT])
                    dve.wait_ge(lg_ready, NCH + 1)
                    then(nc.vector.tensor_reduce(best[:, :], by_e(lg), AX.X, ALU.max))
                    nc.vector.tensor_tensor(a[:, :, :], lg[:, :, :], over_e(best), ALU.subtract).then_inc(diff_ready, 1)
                    then(nc.vector.tensor_tensor(b_[:, :, :], lg[:, :, :], over_e(best), ALU.is_equal))
                    then(nc.vector.tensor_tensor(b_[:, :, :], b_[:, :, :], over_t(countdown), ALU.mult))
                    then(nc.vector.tensor_reduce(first[:, :], by_e(b_), AX.X, ALU.max))
                    then(nc.vector.tensor_tensor(oneh[:, :, :], over_e(first), over_t(countdown), ALU.is_equal))
                    then(nc.vector.tensor_tensor_scan(incl[:, :, :].rearrange("p e t -> p (e t)"), keepmask[:, :, :].rearrange("p e t -> p (e t)"),
                                                      oneh[:, :, :].rearrange("p e t -> p (e t)"), 0.0, ALU.mult, ALU.add))
                    nc.vector.tensor_copy(onehb[:, :, :], oneh[:, :, :])
                    nc.vector.tensor_tensor(exclb[:, :, :], incl[:, :, :], oneh[:, :, :], ALU.subtract).then_inc(count_ready, 1)
                    dve.wait_ge(exp_ready, 1)
                    then(nc.vector.tensor_reduce(sums[:, :], by_e(a), AX.X, ALU.add))
                    then(nc.vector.reciprocal(sums[:, :], sums[:, :]))
                    dve.wait_ge(r_ready, 1)
                    then(nc.vector.tensor_tensor(b_[:, :, :], psR[:, 0:NE * NT].rearrange("p (e t) -> p e t", e=NE), oneh[:, :, :], ALU.mult))
                    then(nc.vector.tensor_reduce(rank[:, :], by_e(b_), AX.X, ALU.add))
                    then(nc.vector.tensor_scalar(keep[:, :], rank[:, :], float(CAP), None, ALU.is_lt))
                    nc.vector.tensor_tensor(weight[:, :], sums[:, :], keep[:, :], ALU.mult)
                    then(nc.vector.scalar_tensor_tensor(slot[:, :], first[:, :], -float(CAP), rank[:, :], ALU.mult, ALU.add))
                    then(nc.vector.scalar_tensor_tensor(slot[:, :], keep[:, :], -2.0 * SLOTS, slot[:, :], ALU.mult, ALU.add))
                    then(nc.vector.tensor_scalar(slot[:, :], slot[:, :], float(NE * CAP + 2 * SLOTS), None, ALU.add))
                    nc.vector.tensor_copy(to_slot[:, :], slot[:, :])
                    then(nc.vector.tensor_scalar(slot2[:, :], slot[:, :], float(SLOTS), None, ALU.min))
                    nc.vector.tensor_copy(from_slot[:, :], slot2[:, :])

                @block.gpsimd
                def _(pool):
                    pool.sem_inc(turned, 1)
                    pool.memset(ones[:, :], 1.0).then_inc(ones_made, 1)
                    pool.wait_ge(ones_made, 1)
                    pool.affine_select(out=before[:, :], in_=ones[:, :], compare_op=ALU.is_gt, fill=0.0, base=0,
                                       pattern=[[1, P]], channel_multiplier=-1).then_inc(ones_made, 1)
                    pool.wait_ge(loaded, 48)

                    def chunk(k, more):
                        norm1.gpsimd(pool, k)
                        norm2.gpsimd(pool, k)
                        pool.wait_ge(n2_ready, k + 1)
                        pool.wait_ge(turned, k + 1)
                        pool.wait_ge(tok_kept, k + 1)
                        wide = lambda t: t[:, :].unsqueeze(1).to_broadcast([P, TPC, D])
                        nc.gpsimd.tensor_tensor(t2[:, :, :], n2[:, :, :], wide(gamma), ALU.mult).then_inc(g_ready, 1)
                        pool.wait_ge(g_ready, k + 1)
                        nc.gpsimd.tensor_tensor(t2[:, :, :], t2[:, :, :], wide(beta), ALU.add).then_inc(t2_ready, 1)
                    loop(pool, NCH, chunk)

                @block.scalar
                def _(act):
                    act.sem_inc(tok_kept, 1)

                    def chunk(k, more):
                        act.wait_ge(t2_ready, k + 1)
                        nc.scalar.copy(tok[:, bass.ds(k * TPC, TPC), :], t2[:, :, :]).then_inc(tok_kept, 1)
                        act.wait_ge(turned, k + 2)
                        nc.scalar.copy(tT[:, :], psT[:, :]).then_inc(tT_ready, 1)
                    loop(act, NCH, chunk)
                    act.wait_ge(diff_ready, 1)
                    nc.scalar.activation(a[:, :, :], a[:, :, :], ACT.Exp).then_inc(exp_ready, 1)

                @block.tensor
                def _(pe):
                    pe.wait_ge(loaded, 48)

                    def chunk(k, more):
                        pe.wait_ge(t2_ready, k + 1)
                        for j in range(TPC):
                            last = nc.tensor.transpose(psT[:, j * P:(j + 1) * P], t2[:, j, :], ident[:, :])
                        last.then_inc(turned, 1)
                        pe.wait_ge(tT_ready, k + 1)
                        pe.wait_ge(lg_ready, k + 1)
                        for j in range(TPC):
                            last = nc.tensor.matmul(psL[:, j * NE:(j + 1) * NE], tT[:, j * P:(j + 1) * P], gate[:, :], start=True, stop=True)
                        last.then_inc(l_ready, 1)
                    loop(pe, NCH, chunk)
                    pe.wait_ge(ones_made, 2)
                    pe.wait_ge(count_ready, 1)
                    nc.tensor.matmul(psR[:, 0:NE * NT], before[:, :], onehb[:, :, :].rearrange("p e t -> p (e t)"), start=True, stop=False)
                    nc.tensor.matmul(psR[:, 0:NE * NT], ones[:, :], exclb[:, :, :].rearrange("p e t -> p (e t)"), start=False, stop=True).then_inc(r_ready, 1)

        with ExitStack() as ctx:
            m = Scope(nc, ctx, tag + "e")
            wi, wo = m.sb("wi", [P, 2, I]), m.sb("wo", [P, 2, IT, D])
            dsp = m.sb("dsp", [P, 2, ST, D])
            dT = m.sb("dT", [P, 2, CAP])
            hid = m.sb("hid", [P, 2, IT, CAP])
            eo = m.sb("eo", [P, 2, ST, D])
            psT, psU, psD = banks[0], banks[1:5], banks[5:7]
            scattered = m.sem("scattered")
            w_in = [m.sem(f"w_in{n}") for n in range(2)]
            d_in = [m.sem(f"d_in{n}") for n in range(2)]
            turned = m.sem("turned")
            dT_ready = m.sem("dT_ready")
            u_ready = m.sem("u_ready")
            h_ready = m.sem("h_ready")
            d_ready = m.sem("d_ready")
            eo_ready = m.sem("eo_ready")
            eo_sent = m.sem("eo_sent")
            eo_free = m.sem("eo_free")

            with nc.Block() as block:
                @block.gpsimd
                def _(pool):
                    for t in range(NT):
                        pool.indirect_dma_start(out=tok_dram, out_offset=bass.IndirectOffsetOnAxis(ap=to_slot[:, t:t + 1], axis=0),
                                                in_=tok[:, t, :], in_offset=None, bounds_check=SLOTS - 1, oob_is_err=False).then_inc(scattered, 16)
                    pool.wait_ge(scattered, 16 * NT)
                    with pool.Fori(0, NE // 2) as i:
                        for par in range(2):
                            e = i * 2 + par
                            pool.wait_ge(eo_ready, e + 3)
                            pool.dma_start(out_dram[bass.ds(e * CAP, CAP), :].rearrange("(s p) d -> p s d", p=P), eo[:, par, :, :]).then_inc(eo_sent, 16)
                            pool.wait_ge(eo_sent, e * 16 + 16)
                            pool.sem_inc(eo_free, 1)

                @block.sync
                def _(sp):
                    with sp.Fori(0, NE // 2) as i:
                        for par in range(2):
                            e = i * 2 + par
                            sp.wait_ge(d_ready, e + 1)
                            sp.dma_start(wi[:, par, :], ins["L0_ffn_wi"][bass.ds(e, 1)].rearrange("o d i -> (o d) i")).then_inc(w_in[par], 16)
                            sp.dma_start(wo[:, par, :, :], ins["L0_ffn_wo"][bass.ds(e, 1)].rearrange("o (c p) d -> (o p) c d", p=P)).then_inc(w_in[par], 16)
                            sp.wait_ge(scattered, 16 * NT)
                            sp.dma_start(dsp[:, par, :, :], tok_dram[bass.ds(e * CAP, CAP), :].rearrange("(s p) d -> p s d", p=P)).then_inc(d_in[par], 16)

                @block.scalar
                def _(act):
                    act.sem_inc(dT_ready, 1)
                    act.sem_inc(h_ready, 4)
                    act.sem_inc(eo_free, 2)
                    with act.Fori(0, NE // 2) as i:
                        for par in range(2):
                            e = i * 2 + par
                            act.wait_ge(turned, e + 1)
                            nc.scalar.copy(dT[:, par, :], psT[:, 0:CAP]).then_inc(dT_ready, 1)
                            for g in range(2):
                                act.wait_ge(u_ready, e * 2 + g + 1)
                                nc.scalar.activation(hid[:, par, 2 * g:2 * g + 2, :], psU[2 * par + g][:, :].rearrange("p (c s) -> p c s", c=2),
                                                     ACT.Gelu).then_inc(h_ready, 1)

                @block.vector
                def _(dve):
                    dve.sem_inc(eo_ready, 2)
                    with dve.Fori(0, NE // 2) as i:
                        for par in range(2):
                            e = i * 2 + par
                            dve.wait_ge(d_ready, e + 3)
                            dve.wait_ge(eo_free, e + 1)
                            nc.vector.tensor_copy(eo[:, par, :, :], psD[par][:, 0:ST * D].rearrange("p (s d) -> p s d", s=ST)).then_inc(eo_ready, 1)

                @block.tensor
                def _(pe):
                    pe.sem_inc(d_ready, 2)

                    def turn(i, par):
                        e = i * 2 + par
                        pe.wait_ge(d_in[par], i * 16 + 16)
                        pe.wait_ge(dT_ready, e + 1)
                        for s in range(ST):
                            last = nc.tensor.transpose(psT[:, s * P:(s + 1) * P], dsp[:, par, s, :], ident[:, :])
                        last.then_inc(turned, 1)

                    def pair(i, more):
                        for par in range(2):
                            e = i * 2 + par
                            pe.wait_ge(w_in[par], i * 32 + 32)
                            pe.wait_ge(dT_ready, e + 2)
                            for g in range(2):
                                pe.wait_ge(h_ready, e * 2 + g + 1)
                                for c in (2 * g, 2 * g + 1):
                                    last = nc.tensor.matmul(psU[2 * par + g][:, (c % 2) * CAP:(c % 2 + 1) * CAP], wi[:, par, c * P:(c + 1) * P],
                                                            dT[:, par, :], start=True, stop=True)
                                last.then_inc(u_ready, 1)
                            if par == 0:
                                turn(i, 1)
                            elif more:
                                turn(i + 1, 0)
                            pe.wait_ge(h_ready, e * 2 + 6)
                            pe.wait_ge(eo_ready, e + 1)
                            for s in range(ST):
                                for c in range(IT):
                                    last = nc.tensor.matmul(psD[par][:, s * D:(s + 1) * D], hid[:, par, c, s * P:(s + 1) * P], wo[:, par, c, :],
                                                            start=(c == 0), stop=(c == IT - 1))
                            last.then_inc(d_ready, 1)

                    turn(0, 0)
                    loop(pe, NE // 2, pair)

        with ExitStack() as ctx:
            m = Scope(nc, ctx, tag + "c")
            back = m.sb("back", [P, NT, D])
            came = [m.sem(f"came{n}") for n in range(NCH)]
            x_ready = m.sem("x_ready")
            with nc.Block() as block:
                @block.gpsimd
                def _(pool):
                    for t in range(NT):
                        pool.indirect_dma_start(out=back[:, t, :], out_offset=None, in_=out_dram,
                                                in_offset=bass.IndirectOffsetOnAxis(ap=from_slot[:, t:t + 1], axis=0)).then_inc(came[t // TPC], 16)

                @block.vector
                def _(dve):
                    for t in range(NT):
                        if t % TPC == 0:
                            dve.wait_ge(came[t // TPC], 16 * TPC)
                        last = nc.vector.scalar_tensor_tensor(X[:, t, :], back[:, t, :], weight[:, t:t + 1], X[:, t, :], ALU.mult, ALU.add)
                    last.then_inc(x_ready, 1)


def rope_tables(L, D, hd):
    scale = np.arange(0, hd, 2, dtype=np.float32)
    freqs = (np.float32(1.0) / np.float32(10000.0) ** scale).astype(np.float32)
    angles = np.arange(L, dtype=np.float32)[:, None] * freqs[None, :]
    cos, sin = np.cos(angles).astype(np.float32), np.sin(angles).astype(np.float32)
    cos = np.tile(np.repeat(cos, 2, axis=1), (1, D // hd))
    sin = np.tile(np.stack([-sin, sin], axis=-1).reshape(L, hd), (1, D // hd))
    head = np.arange(D) // hd
    diag = (head[:, None] == head[None, :]).astype(np.float32) / np.sqrt(np.float32(hd))
    return cos, sin, diag.astype(np.float32)


def rope_attention(nc, res, tag, ins):
    X, banks, ident = res.X, res.banks, res.ident
    NB, CPB = res.B, res.L // CHUNK
    TPB = res.L // P
    assert CPB == 2
    with ExitStack() as ctx:
        m = Scope(nc, ctx, tag)
        norm = Norm(m, res)
        wqkv = m.sb("wqkv", [P, 3 * P])
        wo = m.sb("wo", [P, P])
        bqkv = m.sb("bqkv", [P, 3 * P])
        bo = m.sb("bo", [P, P])
        cos, sin = m.sb("cos", [P, TPB, P]), m.sb("sin", [P, TPB, P])
        diag = m.sb("diag", [P, P])
        h = m.sb("h", [P, TPC, P])
        hT = m.sb("hT", [P, CHUNK])
        raw = m.sb("raw", [P, CPB, TPC, 3 * P])
        byc = m.sb("byc", [P, CPB, TPC, 2 * P])
        bys = m.sb("bys", [P, CPB, TPC, 2 * P])
        qT = m.sb("qT", [P, CPB, CHUNK])
        vk = m.sb("vk", [P, P])
        G = m.sb("G_", [P, P])
        psT, psP, psKV, psQ, psG, psO = banks[0], banks[1:3], banks[3], banks[4], banks[5], banks[6:8]
        loaded = m.sem("loaded")
        h_ready = m.sem("h_ready")
        turned = m.sem("turned")
        hT_ready = m.sem("hT_ready")
        p_ready = m.sem("p_ready")
        raw_ready = m.sem("raw_ready")
        byc_ready = m.sem("byc_ready")
        bys_ready = m.sem("bys_ready")
        rot_ready = m.sem("rot_ready")
        used = m.sem("used")
        qT_ready = m.sem("qT_ready")
        vk_ready = m.sem("vk_ready")
        g_product = m.sem("g_product")
        g_ready = m.sem("g_ready")
        o_ready = m.sem("o_ready")
        x_ready = m.sem("x_ready")
        x_done = m.sem("x_done")

        def pairs(ap, first):
            return ap.rearrange("p j (n t) -> p j n t", t=2)[:, :, :, first:first + 1].squeeze(3)

        with nc.Block() as block:
            @block.sync
            def _(sp):
                for n, name in enumerate(("Wq", "Wk", "Wv")):
                    sp.dma_start(wqkv[:, n * P:(n + 1) * P], ins["L1_attn_a_" + name]).then_inc(loaded, 16)
                for n, name in enumerate(("bq", "bk", "bv")):
                    sp.dma_start(bqkv[:, n * P:(n + 1) * P], ins["L1_attn_a_" + name].partition_broadcast(P)).then_inc(loaded, 16)
                sp.dma_start(cos[:, :, :], ins["rope_cos"].rearrange("(t p) d -> p t d", p=P)).then_inc(loaded, 16)
                sp.dma_start(sin[:, :, :], ins["rope_sin"].rearrange("(t p) d -> p t d", p=P)).then_inc(loaded, 16)
                sp.dma_start(diag[:, :], ins["head_diag"]).then_inc(loaded, 16)
                sp.dma_start(wo[:, :], ins["L1_attn_a_Wo"]).then_inc(loaded, 16)
                sp.dma_start(bo[:, :], ins["L1_attn_a_bo"].partition_broadcast(P)).then_inc(loaded, 16)
                sp.wait_ge(loaded, 11 * 16)

            @block.vector
            def _(dve):
                dve.sem_inc(raw_ready, 2)
                dve.sem_inc(vk_ready, 1)
                dve.sem_inc(x_done, 1)

                def norm_chunk(k):
                    norm.vector(dve, k, lambda j: X[:, bass.ds(k * TPC + j, 1), :], lambda j: h[:, j, :]).then_inc(h_ready, 1)

                def batch(b, more):
                    for c in range(CPB):
                        k = b * CPB + c
                        dve.wait_ge(used, k + 1)
                        for j in range(TPC):
                            dve.wait_ge(p_ready, k * TPC + j + 1)
                            nc.vector.tensor_tensor(raw[:, c, j, :], psP[j % 2][:, 0:3 * P], bqkv[:, :], ALU.add).then_inc(raw_ready, 1)
                        dve.wait_ge(raw_ready, (k + 1) * TPC + 2)
                        for half in range(2):
                            s = slice(half * P, (half + 1) * P)
                            last = nc.vector.tensor_tensor(byc[:, c, :, s], raw[:, c, :, s],
                                                           cos[:, c * TPC:(c + 1) * TPC, :], ALU.mult)
                        last.then_inc(byc_ready, 1)
                        if c + 1 < CPB or more:
                            norm_chunk(k + 1)
                        dve.wait_ge(byc_ready, k + 1)
                        dve.wait_ge(bys_ready, k + 1)
                        nc.vector.tensor_tensor(byc[:, c, :, :], byc[:, c, :, :], bys[:, c, :, :], ALU.add).then_inc(rot_ready, 1)
                    dve.wait_ge(used, (b + 1) * CPB + 2)
                    nc.vector.tensor_tensor(vk[:, :], psKV[:, 0:P], diag[:, :], ALU.mult).then_inc(vk_ready, 1)
                    dve.wait_ge(o_ready, b + 1)
                    for c in range(CPB):
                        xk = X[:, bass.ds(b * TPB + c * TPC, TPC), :]
                        nc.vector.tensor_tensor(xk, xk, psO[c][:, :].rearrange("p (j n) -> p j n", j=TPC), ALU.add).then_inc(x_ready, 1)
                    dve.wait_ge(x_ready, b * 2 + 2)
                    xb = X[:, bass.ds(b * TPB, TPB), :]
                    nc.vector.tensor_tensor(xb, xb, bo[:, :].unsqueeze(1).to_broadcast([P, TPB, P]), ALU.add).then_inc(x_done, 1)

                norm_chunk(0)
                dve.wait_ge(loaded, 11 * 16)
                loop(dve, NB, batch)

            @block.gpsimd
            def _(pool):
                norm.gpsimd(pool, 0)
                pool.wait_ge(loaded, 11 * 16)

                def batch(b, more):
                    for c in range(CPB):
                        k = b * CPB + c
                        if c + 1 < CPB or more:
                            norm.gpsimd(pool, k + 1)
                        pool.wait_ge(raw_ready, (k + 1) * TPC + 2)
                        for half in range(2):
                            s = slice(half * P, (half + 1) * P)
                            for first in range(2):
                                last = nc.gpsimd.tensor_tensor(pairs(bys[:, c, :, s], first), pairs(raw[:, c, :, s], 1 - first),
                                                               pairs(sin[:, c * TPC:(c + 1) * TPC, :], first), ALU.mult)
                        last.then_inc(bys_ready, 1)
                loop(pool, NB, batch)

            @block.scalar
            def _(act):
                act.sem_inc(hT_ready, 1)
                act.sem_inc(qT_ready, 1)

                def copy_hT(k):
                    act.wait_ge(turned, k + 1)
                    nc.scalar.copy(hT[:, :], psT[:, :]).then_inc(hT_ready, 1)

                def batch(b, more):
                    for c in range(CPB):
                        k = b * CPB + c
                        if c + 1 < CPB or more:
                            copy_hT(k + 1)
                        act.wait_ge(used, k + 3)
                        nc.scalar.copy(qT[:, c, :], psQ[:, :]).then_inc(qT_ready, 1)
                    act.wait_ge(g_product, b + 1)
                    nc.scalar.copy(G[:, :], psG[:, 0:P]).then_inc(g_ready, 1)

                copy_hT(0)
                loop(act, NB, batch)

            @block.tensor
            def _(pe):
                pe.sem_inc(used, 2)

                def turn(k):
                    pe.wait_ge(h_ready, k + 1)
                    pe.wait_ge(hT_ready, k + 1)
                    for j in range(TPC):
                        last = nc.tensor.transpose(psT[:, j * P:(j + 1) * P], h[:, j, :], ident[:, :])
                    last.then_inc(turned, 1)

                def batch(b, more):
                    for c in range(CPB):
                        k = b * CPB + c
                        pe.wait_ge(hT_ready, k + 2)
                        for j in range(TPC):
                            pe.wait_ge(raw_ready, k * TPC + j + 1)
                            nc.tensor.matmul(psP[j % 2][:, 0:3 * P], hT[:, j * P:(j + 1) * P], wqkv[:, :],
                                             start=True, stop=True).then_inc(p_ready, 1)
                        if c + 1 < CPB or more:
                            turn(k + 1)
                        pe.wait_ge(rot_ready, k + 1)
                        if c == 0:
                            pe.wait_ge(vk_ready, b + 1)
                        for j in range(TPC):
                            nc.tensor.matmul(psKV[:, 0:P], raw[:, c, j, 2 * P:3 * P], byc[:, c, j, P:2 * P],
                                             start=(c == 0 and j == 0), stop=(c == CPB - 1 and j == TPC - 1))
                        pe.wait_ge(qT_ready, k + 1)
                        for j in range(TPC):
                            last = nc.tensor.transpose(psQ[:, j * P:(j + 1) * P], byc[:, c, j, 0:P], ident[:, :])
                        last.then_inc(used, 1)
                    pe.wait_ge(vk_ready, b + 2)
                    nc.tensor.matmul(psG[:, 0:P], vk[:, :], wo[:, :], start=True, stop=True).then_inc(g_product, 1)
                    pe.wait_ge(g_ready, b + 1)
                    pe.wait_ge(x_done, b + 1)
                    pe.wait_ge(qT_ready, (b + 1) * CPB + 1)
                    for c in range(CPB):
                        for j in range(TPC):
                            last = nc.tensor.matmul(psO[c][:, j * P:(j + 1) * P], qT[:, c, j * P:(j + 1) * P], G[:, :],
                                                    start=True, stop=True)
                    last.then_inc(o_ready, 1)

                turn(0)
                pe.wait_ge(loaded, 11 * 16)
                loop(pe, NB, batch)


def alibi_rows(L, H):
    import math
    start = 2.0 ** (-2.0 ** (-(math.log2(H) - 3)))
    slopes = np.array([start * start ** i for i in range(H)], dtype=np.float32)
    bf = mybir.dt.np(BF16)
    parts, rest = [], slopes
    for _ in range(3):
        parts.append(rest.astype(bf))
        rest = rest - parts[-1].astype(np.float32)
    pos = np.arange(L)
    tile, place = (pos // P * P).astype(bf), (pos % P).astype(bf)
    keys, queries = np.zeros((H, 12, L), bf), np.zeros((H, 12, L), bf)
    for n, part in enumerate(parts):
        keys[:, 4 * n], queries[:, 4 * n] = tile, part[:, None]
        keys[:, 4 * n + 1], queries[:, 4 * n + 1] = place, part[:, None]
        keys[:, 4 * n + 2], queries[:, 4 * n + 2] = part[:, None], -tile
        keys[:, 4 * n + 3], queries[:, 4 * n + 3] = part[:, None], -place
    return keys, queries


MASKED = -1e30


def softmax_attention(nc, res, tag, w):
    X, banks, ident = res.X, res.banks, res.ident
    NB, L, D, H, DK, DV = res.B, res.L, P, w.H, w.DK, w.DV
    NCH, CPB, TPB = res.T // CHUNK, L // CHUNK, L // P
    NV = H * DV
    VB = -(-NV // 512)
    VW = min(NV, 512)
    HPV = VW // DV
    qk_dram = nc.dram_tensor(f"{tag}_qk", [2, 3, D, res.T], BF16).ap()
    v_dram = nc.dram_tensor(f"{tag}_v", [NB, H, P, TPB, DV], F32).ap()
    m_dram = nc.dram_tensor(f"{tag}_m", [NB * H, 2, TPB, P], BF16).ap()

    NH = NB * H
    OCT, AHEAD = 8, 3
    NO = NH // OCT
    R0 = 9 * DK + (12 if w.alibi else 0)
    R1 = R0 + 2
    HALF = P // 2
    SHARE = HALF // DV
    SIDES = min(2, OCT // SHARE)
    OG = SHARE * SIDES
    OK = OG * DV
    NG = OCT // OG
    CB = min(2, NG)
    MAXES = [(j, 0, min(512, (j + 1) * P)) for j in range(TPB)] + [(j, 512, (j + 1) * P - 512) for j in range(4, TPB)]
    PROBS = [(i, i * P, 512 - i * P) for i in range(4)] + [(i, max(512, i * P), L - max(512, i * P)) for i in range(TPB)]
    NPR, NMX = len(PROBS), len(MAXES)
    MAX_STEPS = [[], [0, 1], [2], [3], [4], [5], [6], [7], [8, 9], [10], [11], []]
    PIECES = 8
    QKL = 6 + 2 * bool(w.alibi)
    assert L == 1024 and 64 < R0 and R1 <= P and NH % OCT == 0 and H % OCT == 0 and NPR == NMX == len(MAX_STEPS) == 12
    OPB = H // OCT

    outer = ExitStack()
    mo = Scope(nc, outer, tag + "o")
    ks = mo.sb("ks", [P, OCT, L], BF16)
    identb, upper, lower = (mo.sb(n, [P, P], BF16) for n in ("identb", "upper", "lower"))
    mask_made = mo.sem("mask_made")

    with ExitStack() as ctx:
        m = Scope(nc, ctx, tag + "p")
        norm = Norm(m, res)
        wq, wk, wv = m.sb("wq", [P, D]), m.sb("wk", [P, D]), m.sb("wv", [P, NV])
        h = m.sb("h", [P, TPC, P])
        hT = m.sb("hT", [P, CHUNK])
        qk = m.sb("qk", [P, 2, CHUNK])
        parts = m.sb("parts", [P, 2, 3, CHUNK], BF16)
        rest = m.sb("rest", [P, 2, CHUNK])
        vout = m.sb("vout", [P, 2, H, TPC, DV])
        if w.biases:
            bq, bk, bv, bo = m.sb("bq", [P, 1]), m.sb("bk", [P, 1]), m.sb("bv", [P, NV]), m.sb("bo", [P, P])
            temp, qscale, qbias = m.sb("temp", [P, 1]), m.sb("qscale", [P, 1]), m.sb("qbias", [P, 1])
        psT, psQK, psV = banks[0], banks[1:3], banks[3:7]
        loaded = m.sem("loaded")
        NLOAD = 3 + 5 * bool(w.biases)
        scaled = m.sem("scaled")
        h_ready = m.sem("h_ready")
        turned = m.sem("turned")
        hT_ready = m.sem("hT_ready")
        qk_product = m.sem("qk_product")
        qk_ready = m.sem("qk_ready")
        part1 = m.sem("part1")
        rest1 = m.sem("rest1")
        part2 = m.sem("part2")
        part3 = m.sem("part3")
        qk_sent = m.sem("qk_sent")
        v_product = m.sem("v_product")
        v_ready = [m.sem("v_even"), m.sem("v_odd")]
        v_sent = m.sem("v_sent")
        VPC = TPC * VB

        def v_bank(k, n, eng):
            j, vb = n // VB, n % VB
            eng.wait_ge(v_product, k * VPC + n + 1)
            return vout[:, bass.ds(k % 2, 1), vb * HPV:(vb + 1) * HPV, j, :].rearrange("p o h d -> p (o h) d"), psV[n % 4][:, 0:VW].rearrange("p (h d) -> p h d", d=DV)

        with nc.Block() as block:
            @block.sync
            def _(sp):
                sp.sem_inc(qk_sent, 32)
                sp.sem_inc(v_sent, 32)
                for t, src in ((wq, w.Wq), (wk, w.Wk), (wv, w.Wv)):
                    sp.dma_start(t[:, :], src).then_inc(loaded, 16)
                if w.biases:
                    for t, src in ((bq, w.bq), (bk, w.bk)):
                        sp.dma_start(t[:, :], src.rearrange("(p o) -> p o", o=1)).then_inc(loaded, 16)
                    for t, src in ((bv, w.bv), (bo, w.bo), (temp, w.temperature)):
                        sp.dma_start(t[:, :], src.partition_broadcast(P)).then_inc(loaded, 16)

                def batch(b, more):
                    for c in range(CPB):
                        k = b * CPB + c
                        sp.wait_ge(part3, k + 2)
                        for n in range(2):
                            sp.dma_start(qk_dram[n, :, :, bass.ds(k * CHUNK, CHUNK)].rearrange("r p t -> p r t"),
                                         parts[:, n, :, :]).then_inc(qk_sent, 16)
                        for v in v_ready:
                            sp.wait_ge(v, (k + 1) * VPC // 2 + 2)
                        sp.wait_ge(v_sent, k * 16 + 32)
                        sp.dma_start(v_dram[bass.ds(b, 1), :, :, c * TPC:(c + 1) * TPC, :].rearrange("o h p t e -> p (o h) (t e)"),
                                     vout[:, c % 2, :, :, :].rearrange("p h t e -> p h (t e)")).then_inc(v_sent, 16)
                loop(sp, NB, batch)
                sp.wait_ge(qk_sent, 32 * NCH + 32)
                sp.wait_ge(v_sent, 16 * (NCH + 2))

            @block.vector
            def _(dve):
                dve.sem_inc(v_ready[1], 2)

                def norm_chunk(k):
                    norm.vector(dve, k, lambda j: X[:, bass.ds(k * TPC + j, 1), :], lambda j: h[:, j, :]).then_inc(h_ready, 1)
                    if w.biases:
                        dve.wait_ge(h_ready, k + 1)
                        xk = X[:, bass.ds(k * TPC, TPC), :]
                        nc.vector.tensor_tensor(xk, xk, bo[:, :].unsqueeze(1).to_broadcast([P, TPC, P]), ALU.add)

                def chunk(k, more):
                    if more:
                        dve.wait_ge(turned, k + 1)
                        norm_chunk(k + 1)
                    dve.wait_ge(v_sent, k * 16 + 16)
                    for n in range(VPC) if w.biases else range(1, VPC, 2):
                        if n == VPC // 2 + 1:
                            dve.wait_ge(part1, k + 1)
                            nc.vector.tensor_tensor(rest[:, :, :], qk[:, :, :], parts[:, :, 0, :], ALU.subtract).then_inc(rest1, 1)
                        dst, src = v_bank(k, n, dve)
                        if w.biases:
                            nc.vector.tensor_tensor(dst, src, bv[:, :].rearrange("p (h d) -> p h d", d=DV), ALU.add).then_inc(v_ready[n % 2], 1)
                        else:
                            nc.vector.tensor_copy(dst, src).then_inc(v_ready[1], 1)

                dve.wait_ge(loaded, NLOAD * 16)
                if w.biases:
                    dve.tensor_scalar(temp[:, :], temp[:, :], float(np.float32(np.sqrt(DK))), None, ALU.mult).then_inc(scaled, 1)
                    dve.wait_ge(scaled, 1)
                    dve.reciprocal(qscale[:, :], temp[:, :]).then_inc(scaled, 1)
                    dve.wait_ge(scaled, 2)
                    dve.tensor_tensor(qbias[:, :], bq[:, :], qscale[:, :], ALU.mult).then_inc(scaled, 1)
                norm_chunk(0)
                loop(dve, NCH, chunk)

            @block.gpsimd
            def _(pool):
                pool.sem_inc(part3, 1)
                norm.gpsimd(pool, 0)
                pool.memset(ks[:, :, :], 1.0)
                for buf in (identb, upper, lower):
                    pool.memset(buf[:, :], 0.0).then_inc(mask_made, 1)
                pool.wait_ge(mask_made, 3)
                pool.affine_select(out=identb[:, :], in_=identb[:, :], compare_op=ALU.not_equal, fill=1.0, base=0,
                                   pattern=[[-1, P]], channel_multiplier=1).then_inc(mask_made, 1)
                pool.affine_select(out=upper[:, :], in_=upper[:, :], compare_op=ALU.is_ge, fill=MASKED, base=0,
                                   pattern=[[-1, P]], channel_multiplier=1).then_inc(mask_made, 1)
                pool.affine_select(out=lower[:, :], in_=lower[:, :], compare_op=ALU.is_ge, fill=MASKED, base=0,
                                   pattern=[[1, P]], channel_multiplier=-1).then_inc(mask_made, 1)

                def chunk(k, more):
                    if more:
                        norm.gpsimd(pool, k + 1)
                    pool.wait_ge(part2, k + 1)
                    nc.gpsimd.tensor_tensor(parts[:, :, 2, :], rest[:, :, :], parts[:, :, 1, :], ALU.subtract).then_inc(part3, 1)
                loop(pool, NCH, chunk)

            @block.scalar
            def _(act):
                act.sem_inc(hT_ready, 1)
                act.sem_inc(qk_ready, 1)
                act.sem_inc(v_ready[0], 2)

                def copy_hT(k):
                    act.wait_ge(turned, k + 1)
                    nc.scalar.copy(hT[:, :], psT[:, :]).then_inc(hT_ready, 1)

                def chunk(k, more):
                    act.wait_ge(part3, k + 1)
                    act.wait_ge(qk_product, k + 1)
                    if w.biases:
                        nc.scalar.activation(qk[:, 0, :], psQK[0][:, :], ACT.Identity, bias=qbias[:, 0:1], scale=qscale[:, 0:1])
                        nc.scalar.activation(qk[:, 1, :], psQK[1][:, :], ACT.Identity, bias=bk[:, 0:1]).then_inc(qk_ready, 1)
                    else:
                        nc.scalar.activation(qk[:, 0, :], psQK[0][:, :], ACT.Copy, scale=float(np.float32(DK ** -0.5)))
                        nc.scalar.copy(qk[:, 1, :], psQK[1][:, :]).then_inc(qk_ready, 1)
                    act.wait_ge(qk_ready, k + 2)
                    act.wait_ge(qk_sent, 32 * k + 32)
                    nc.scalar.copy(parts[:, :, 0, :], qk[:, :, :]).then_inc(part1, 1)
                    if not w.biases:
                        act.wait_ge(v_sent, k * 16 + 16)
                    for n in range(0, VPC, 2):
                        if n == VPC // 2:
                            act.wait_ge(rest1, k + 1)
                            nc.scalar.copy(parts[:, :, 1, :], rest[:, :, :]).then_inc(part2, 1)
                        if not w.biases:
                            dst, src = v_bank(k, n, act)
                            nc.scalar.copy(dst, src).then_inc(v_ready[0], 1)
                    if more:
                        act.wait_ge(v_product, (k + 1) * VPC)
                        copy_hT(k + 1)

                copy_hT(0)
                if w.biases:
                    act.wait_ge(scaled, 3)
                loop(act, NCH, chunk)

            @block.tensor
            def _(pe):
                def turn(k):
                    pe.wait_ge(h_ready, k + 1)
                    pe.wait_ge(hT_ready, k + 1)
                    for j in range(TPC):
                        last = nc.tensor.transpose(psT[:, j * P:(j + 1) * P], h[:, j, :], ident[:, :])
                    last.then_inc(turned, 1)

                def chunk(k, more):
                    pe.wait_ge(hT_ready, k + 2)
                    pe.wait_ge(qk_ready, k + 1)
                    for n, weight in enumerate((wq, wk)):
                        last = nc.tensor.matmul(psQK[n][:, :], weight[:, :], hT[:, :], start=True, stop=True)
                    last.then_inc(qk_product, 1)
                    for n in range(VPC):
                        j, vb = n // VB, n % VB
                        pe.wait_ge(v_ready[n % 2], k * VPC // 2 + n // 2 + 1)
                        nc.tensor.matmul(psV[n % 4][:, 0:VW], hT[:, j * P:(j + 1) * P], wv[:, vb * VW:(vb + 1) * VW],
                                         start=True, stop=True).then_inc(v_product, 1)
                        if n == VPC // 2 - 1 and more:
                            turn(k + 1)

                turn(0)
                pe.wait_ge(loaded, NLOAD * 16)
                loop(pe, NCH, chunk)

    with ExitStack() as ctx:
        m = Scope(nc, ctx, tag + "a")
        qs = m.sb("qs", [P, OCT, L], BF16)
        vs = m.sb("vs", [P, OCT, TPB, P])
        probs = m.sb("probs", [P, 2, TPB * L])
        mx, mh = m.sb("mx", [P, 2, NMX]), m.sb("mh", [P, 2, TPB])
        mparts = m.sb("mparts", [TPB, OCT, 2, P], BF16)
        ctxT = m.sb("ctxT", [P, CB, L])
        den = m.sb("den", [P, CB, L])
        yT = m.sb("yT", [P, L])
        wo, wo_now = m.sb("wo", [P, H // OG, D]), m.sb("wo_now", [P, NG, D])
        psM, psS, psO, psY = banks[0:2], banks[2:4], banks[4:6], banks[6:8]
        mT = psM[0][0:TPB, 0:P]
        wo_in = m.sem("wo_in")
        v_set = m.sem("v_set")
        NVSET = SIDES if SHARE == 1 else 1 + OCT
        qk_in = [m.sem(f"qk_in{n}") for n in range(2)]
        v_in = [m.sem(f"v_in{n}") for n in range(2)]
        m_sent = m.sem("m_sent")
        m_in = m.sem("m_in")
        m_product = m.sem("m_product")
        m_taken = m.sem("m_taken")
        mh_ready = m.sem("mh_ready")
        mT_ready = m.sem("mT_ready")
        mp_first = m.sem("mp_first")
        mp_ready = m.sem("mp_ready")
        s_product = m.sem("s_product")
        p_ready = m.sem("p_ready")
        o_product = m.sem("o_product")
        u_ready = m.sem("u_ready")
        inverted = m.sem("inverted")
        c_ready = m.sem("c_ready")
        wo_ready = m.sem("wo_ready")
        y_product = m.sem("y_product")
        yT_ready = m.sem("yT_ready")
        y_turned = m.sem("y_turned")
        x_ready = m.sem("x_ready")
        cleared = [m_product, m_taken, mh_ready, mT_ready, mp_first, mp_ready, s_product, p_ready, o_product,
                   u_ready, inverted, c_ready, wo_ready, y_product, yT_ready, y_turned, x_ready]
        numbers = [s.num for s in cleared]
        assert sorted(numbers) == list(range(min(numbers), max(numbers) + 1))

        def clear():
            nc.gpsimd.sem_clear(range(min(numbers), max(numbers) + 1))
            nc.all_engine_barrier()

        def wait(eng, sem, n):
            if not isinstance(n, int) or n > 0:
                eng.wait_ge(sem, n)

        def load_qk(sp, b, hd, slot, par):
            toks, rows = bass.ds(b * L, L), bass.ds(hd * DK, DK)
            for r in range(3):
                rr = slice(3 * DK * r, 3 * DK * (r + 1))
                sp.dma_start(qs[rr, slot, :], qk_dram[0, :, rows, toks]).then_inc(qk_in[par], 16)
                sp.dma_start(ks[rr, slot, :], qk_dram[1, r:r + 1, rows, toks].to_broadcast([3, DK, L])).then_inc(qk_in[par], 16)
            if w.alibi:
                for buf, rows12 in ((qs, w.alibi_q), (ks, w.alibi_k)):
                    sp.dma_start(buf[9 * DK:R0, slot, :], rows12[bass.ds(hd, 1)].rearrange("o r t -> (o r) t")).then_inc(qk_in[par], 16)

        def side(slot):
            return slot // SHARE % SIDES * HALF, slot % SHARE * DV

        def load_v(sp, b, hd, slot, par):
            base, col = side(slot)
            sp.dma_start(vs[:, slot, :, base + col:base + col + DV],
                         v_dram[bass.ds(b, 1), bass.ds(hd, 1)].rearrange("o u p t e -> (o u p) t e")).then_inc(v_in[par], 16)

        def send_maxima(pool, a, t, slot):
            if t is not None:
                wait(pool, m_sent, 16 * a)
                pool.wait_ge(mp_ready, t + 1)
            pool.dma_start(m_dram[bass.ds(a, 1)].rearrange("o r j q -> (o j) r q"), mparts[:, slot, :, :]).then_inc(m_sent, 16)

        def fetch_maxima(sp, a, slot):
            sp.wait_ge(m_sent, 16 * a + 16)
            wait(sp, m_in, 16 * a)
            sp.dma_start(qs[R0:R1, slot, :], m_dram[bass.ds(a, 1)].rearrange("o r j q -> (o r) (j q)")).then_inc(m_in, 16)

        def max_scores(pe, t, idx, slot):
            j, k0, nk = MAXES[idx]
            if idx == 0:
                wait(pe, mp_ready, t)
            else:
                wait(pe, m_taken, t * NMX + idx - 1)
            diagonal = k0 + nk == (j + 1) * P
            last = nc.tensor.matmul(psM[idx % 2][:, 0:nk], qs[0:R0, slot, j * P:(j + 1) * P],
                                    ks[0:R0, slot, k0:k0 + nk], start=True, stop=not diagonal)
            if diagonal:
                last = nc.tensor.matmul(psM[idx % 2][:, nk - P:nk], identb[:, :], upper[:, :], start=False, stop=True)
            last.then_inc(m_product, 1)

        def turn_maxima(pe, t, par):
            pe.wait_ge(mh_ready, t + 1)
            nc.tensor.transpose(mT, mh[:, par, :], ident[:, :]).then_inc(mT_ready, 1)

        def scores(pe, t, idx, slot):
            i, q0, nq = PROBS[idx]
            wait(pe, p_ready, t * NPR + idx - 1)
            diagonal = q0 == i * P
            last = nc.tensor.matmul(psS[idx % 2][:, 0:nq], ks[0:R1, slot, i * P:(i + 1) * P],
                                    qs[0:R1, slot, q0:q0 + nq], start=True, stop=not diagonal)
            if diagonal:
                last = nc.tensor.matmul(psS[idx % 2][:, 0:P], identb[:, :], lower[:, :], start=False, stop=True)
            last.then_inc(s_product, 1)

        def outputs(pe, t, idx):
            i, q0, nq = PROBS[idx]
            g = q0 // 512
            if i == 0:
                if t % SHARE == 0:
                    wait(pe, u_ready, t // SHARE * 2 + g - 1)
                wait(pe, p_ready, t * NPR - (0 if g else NPR - 4))
            last = nc.tensor.matmul(psO[g][:, q0 - 512 * g:q0 - 512 * g + nq], vs[:, t, i, :], probs[:, t % 2, i * L + q0:i * L + q0 + nq],
                                    start=(i == 0 and t % SHARE == 0), stop=(i == 4 * g + 3 and t % SHARE == SHARE - 1))
            if i == 4 * g + 3:
                last.then_inc(o_product, 1)

        def project(pe, n, g, half, x_need, weights):
            pe.wait_ge(c_ready, 2 * n + half + 1)
            wait(pe, x_ready, x_need)
            wait(pe, wo_ready, weights)
            nc.tensor.matmul(psY[half][:, :], wo_now[0:OK, g, :], ctxT[0:OK, g % CB, half * 512:(half + 1) * 512],
                             start=(g == 0), stop=(g == NG - 1)).then_inc(y_product, 1)

        def turn_outputs(pe, half):
            pe.wait_ge(yT_ready, half + 1)
            for j in range(4):
                last = nc.tensor.transpose(psY[half][:, j * P:(j + 1) * P], yT[:, half * 512 + j * P:half * 512 + (j + 1) * P], ident[:, :])
            last.then_inc(y_turned, 1)

        def exps(act, t, idx, par):
            i, q0, nq = PROBS[idx]
            act.wait_ge(s_product, t * NPR + idx + 1)
            nc.scalar.activation(probs[:, par, i * L + q0:i * L + q0 + nq], psS[idx % 2][:, 0:nq], ACT.Exp).then_inc(p_ready, 1)

        def copy_outputs(act, half):
            act.wait_ge(y_product, half + 1)
            nc.scalar.copy(yT[:, half * 512:(half + 1) * 512], psY[half][:, :]).then_inc(yT_ready, 1)

        def maximum(dve, t, idx, par):
            dve.wait_ge(m_product, t * NMX + idx + 1)
            nc.vector.tensor_reduce(mx[:, par, idx:idx + 1], psM[idx % 2][:, 0:MAXES[idx][2]], AX.X, ALU.max).then_inc(m_taken, 1)

        def join_maxima(dve, t, par):
            dve.wait_ge(m_taken, (t + 1) * NMX)
            nc.vector.tensor_copy(mh[:, par, 0:4], mx[:, par, 0:4])
            nc.vector.tensor_tensor(mh[:, par, 4:TPB], mx[:, par, 4:TPB], mx[:, par, TPB:NMX], ALU.max).then_inc(mh_ready, 1)

        def split_maxima(dve, t, slot):
            dve.wait_ge(mT_ready, t + 1)
            nc.vector.tensor_scalar(mparts[:, slot, 0, :], mT, -1.0, None, ALU.mult).then_inc(mp_first, 1)
            dve.wait_ge(mp_first, t + 1)
            nc.vector.scalar_tensor_tensor(mparts[:, slot, 1, :], mT, -1.0, mparts[:, slot, 0, :],
                                           ALU.mult, ALU.subtract).then_inc(mp_ready, 1)

        def take_outputs(act, t, half, before):
            base, n, g = side(t)[0], t // SHARE * 2 + half, t // OG
            mine, other, cols = slice(base, base + HALF), slice(HALF - base, 2 * HALF - base), slice(half * 512, (half + 1) * 512)
            act.wait_ge(o_product, t * 2 + half + 1)
            wait(act, y_product, before + 2 * (g - CB + 1))
            nc.scalar.copy(den[mine, g % CB, cols], psO[half][other, :])
            nc.scalar.copy(ctxT[mine, g % CB, cols], psO[half][mine, :]).then_inc(u_ready, 1)

        def invert(dve, g, piece):
            cols = slice(piece * L // PIECES, (piece + 1) * L // PIECES)
            nc.vector.reciprocal(den[0:OK, g % CB, cols], den[0:OK, g % CB, cols]).then_inc(inverted, 1)

        def normalise(dve, n, g, half):
            cols = slice(half * 512, (half + 1) * 512)
            dve.wait_ge(inverted, n * PIECES + (half + 1) * PIECES // 2)
            nc.vector.tensor_tensor(ctxT[0:OK, g % CB, cols], ctxT[0:OK, g % CB, cols], den[0:OK, g % CB, cols],
                                    ALU.mult).then_inc(c_ready, 1)

        def add_output(dve, half, tile0):
            dve.wait_ge(y_turned, half + 1)
            tiles = X[:, bass.ds(tile0 + 4 * half, 4), :]
            nc.vector.tensor_tensor(tiles, tiles, psY[half][:, :].rearrange("p (j n) -> p j n", j=4), ALU.add).then_inc(x_ready, 1)

        with nc.Block() as block:
            @block.sync
            def _(sp):
                sp.dma_start(wo[0:OK, :, :], w.Wo.rearrange("(g p) n -> p g n", p=OK)).then_inc(wo_in, 16)
                for hd in range(OCT):
                    par = hd % 2
                    wait(sp, qk_in[par], hd // 2 * QKL * 16)
                    load_qk(sp, 0, hd, hd, par)
                    wait(sp, v_in[par], hd // 2 * 16)
                    sp.wait_ge(v_set, NVSET)
                    load_v(sp, 0, hd, hd, par)
                for a in range(AHEAD - 1):
                    fetch_maxima(sp, a, a)
                sp.wait_ge(wo_in, 16)

            @block.gpsimd
            def _(pool):
                if SHARE == 1:
                    for n in range(SIDES):
                        pool.memset(vs[:, n::SIDES, :, HALF - side(n)[0]:2 * HALF - side(n)[0]], 1.0).then_inc(v_set, 1)
                else:
                    pool.memset(vs[:, :, :, :], 0.0).then_inc(v_set, 1)
                    pool.wait_ge(v_set, 1)
                    for n in range(OCT):
                        base, col = side(n)
                        pool.memset(vs[:, n, :, HALF - base + col:HALF - base + col + DV], 1.0).then_inc(v_set, 1)
                for a in range(AHEAD):
                    send_maxima(pool, a, a, a)

            @block.vector
            def _(dve):
                for a in range(AHEAD):
                    for idx in range(NMX):
                        maximum(dve, a, idx, a % 2)
                    join_maxima(dve, a, a % 2)
                    split_maxima(dve, a, a)

            @block.scalar
            def _(act):
                for idx in range(NPR):
                    exps(act, 0, idx, 0)

            @block.tensor
            def _(pe):
                for a in range(AHEAD):
                    pe.wait_ge(qk_in[a % 2], (a // 2 + 1) * QKL * 16)
                    for idx in range(NMX):
                        max_scores(pe, a, idx, a)
                    turn_maxima(pe, a, a % 2)
                    if a == AHEAD - 1:
                        pe.wait_ge(m_in, 16)
                        for idx in range(NPR):
                            scores(pe, 0, idx, 0)
        clear()

        def octet(o, first, final):
            LEAD = AHEAD if final else 0
            before = 0 if first else 2

            with nc.Block() as block:
                @block.sync
                def _(sp):
                    if not final:
                        b, hd0 = (o + 1) // OPB, (o + 1) % OPB * OCT
                    for s in range(OCT):
                        par = s % 2
                        a = o * OCT + s + AHEAD
                        if s <= OCT - LEAD:
                            fetch_maxima(sp, a - 1, (s + AHEAD - 1) % OCT)
                        if final:
                            continue
                        wait(sp, s_product, s * NPR)
                        sp.wait_ge(qk_in[par], (o * 4 + 4 + s // 2) * QKL * 16)
                        load_qk(sp, b, hd0 + s, s, par)
                        sp.wait_ge(o_product, 2 * s + 2)
                        sp.wait_ge(v_in[par], (o * 4 + 4 + s // 2) * 16)
                        load_v(sp, b, hd0 + s, s, par)

                @block.gpsimd
                def _(pool):
                    if not first:
                        send_maxima(pool, o * OCT + AHEAD - 1, None, AHEAD - 1)
                    group = o % OPB * NG
                    if NG > 1:
                        nc.gpsimd.tensor_copy(wo_now[0:OK, 0:NG - 1, :], wo[0:OK, bass.ds(group, NG - 1), :]).then_inc(wo_ready, 1)
                    for s in range(OCT - 1 - final * (LEAD - 1)):
                        send_maxima(pool, o * OCT + s + AHEAD, s, (s + AHEAD) % OCT)
                        if s == 2:
                            wait(pool, y_product, before)
                            nc.gpsimd.tensor_copy(wo_now[0:OK, NG - 1:NG, :], wo[0:OK, bass.ds(group + NG - 1, 1), :])
                    if not final:
                        pool.wait_ge(m_sent, 16 * (o * OCT + OCT - 1 + AHEAD))

                @block.vector
                def _(dve):
                    for s in range(OCT):
                        ahead = s < OCT - LEAD
                        n, half = s // OG - first, s % OG
                        due = half < 2 and n >= 0
                        if due and half == 0:
                            wait(dve, u_ready, 2 * SIDES * (s // OG))
                        for step in range(NPR):
                            if ahead:
                                for idx in MAX_STEPS[step]:
                                    maximum(dve, s, idx, s % 2)
                            if due and step in (1, 3, 5, 7):
                                invert(dve, (s // OG - 1) % NG, half * PIECES // 2 + step // 2)
                            if due and step == 8:
                                normalise(dve, n, (s // OG - 1) % NG, half)
                            if not first and s in (1, 2) and step == 4:
                                add_output(dve, s - 1, (o - 1) // OPB * TPB)
                        if ahead:
                            join_maxima(dve, s, s % 2)
                            split_maxima(dve, s, (s + AHEAD) % OCT)

                @block.scalar
                def _(act):
                    for s in range(OCT):
                        whole = s % SHARE == SHARE - 1
                        for idx in range(NPR):
                            if not (final and s == OCT - 1):
                                exps(act, s, idx, (s + 1) % 2)
                            if idx == 0 and s and (s - 1) % SHARE == SHARE - 1:
                                take_outputs(act, s - 1, 1, before)
                            if idx == 5 and whole:
                                take_outputs(act, s, 0, before)
                            if not first and s in (1, 2) and idx == 1:
                                copy_outputs(act, s - 1)
                    take_outputs(act, OCT - 1, 1, before)

                @block.tensor
                def _(pe):
                    for s in range(OCT):
                        ahead = s < OCT - LEAD
                        n, half = s // OG - first, s % OG
                        due = half < 2 and n >= 0
                        if ahead:
                            pe.wait_ge(qk_in[(s + AHEAD) % 2], (o * 4 + (s + AHEAD) // 2 + 1) * QKL * 16)
                        pe.wait_ge(v_in[s % 2], (o * 4 + s // 2 + 1) * 16)
                        if not (final and s == OCT - 1):
                            pe.wait_ge(m_in, 16 * (o * OCT + s + 2))
                        for step in range(NPR):
                            if not (final and s == OCT - 1):
                                scores(pe, s, step, (s + 1) % OCT)
                            if ahead:
                                for idx in MAX_STEPS[step]:
                                    max_scores(pe, s, idx, (s + AHEAD) % OCT)
                            outputs(pe, s, step)
                            if ahead and step == NPR - 1:
                                turn_maxima(pe, s, s % 2)
                            if due and step == 10:
                                g = s // OG - 1
                                project(pe, n, g % NG, half, half + 1 if g == 0 and not first else 0, 1 if g >= 0 else 0)
                            if not first and s in (1, 2) and step == 3:
                                turn_outputs(pe, s - 1)
            clear()

        octet(0, True, False)
        with nc.Fori(0, NO - 2) as o:
            octet(o + 1, False, False)
        octet(NO - 1, False, True)

        with nc.Block() as block:
            @block.vector
            def _(dve):
                for half in range(2):
                    for piece in range(PIECES // 2):
                        invert(dve, NG - 1, half * PIECES // 2 + piece)
                    normalise(dve, 0, NG - 1, half)
                for half in range(2):
                    add_output(dve, half, (NO - 1) // OPB * TPB)

            @block.scalar
            def _(act):
                for half in range(2):
                    copy_outputs(act, half)

            @block.tensor
            def _(pe):
                for half in range(2):
                    project(pe, 0, NG - 1, half, 0, 0)
                for half in range(2):
                    turn_outputs(pe, half)
    outer.close()


class Res:
    pass


def build_program(nc, ins, out):
    x_dram = ins["L0_attn_a_hidden_states"]
    B, L, D = x_dram.shape
    T = B * L
    NT = T // P
    res = Res()
    res.B, res.L, res.T, res.NT = B, L, T, NT
    with ExitStack() as ctx:
        g = Scope(nc, ctx, "g")
        res.X = X = g.sb("x", [P, NT, P])
        res.ident = ident = g.sb("ident", [P, P])
        res.banks = [ctx.enter_context(nc.psum_tensor(f"bank{i}", [P, 512], F32)) for i in range(8)]
        res.minus_half = g.sb("minus_half", [P, 8])
        x_in, w_in, id_ready, x_out = g.sem("x_in"), g.sem("w_in"), g.sem("id_ready"), g.sem("x_out")

        f = Res()
        DH = ins["L1_ffn_w1_w"].shape[0]
        HT = DH // P
        f.w1T, f.w2T = g.sb("w1T", [P, DH]), g.sb("w2T", [P, DH])
        f.h1T, f.h2T, f.w3T = g.sb("h1T", [P, HT, DH]), g.sb("h2T", [P, HT, DH]), g.sb("w3T", [P, HT, P])
        f.s1, f.s2, f.sh1, f.sh2 = (g.sb(n, [P, HT]) for n in ("s1", "s2", "sh1", "sh2"))
        f.s3 = g.sb("s3", [P, P])
        with ExitStack() as ctx2:
            ld = Scope(nc, ctx2, "ld")
            nat = {n: ld.sb(n, [P, HT, D]) for n in ("w1_w", "w2_w")}
            nat |= {n: ld.sb(n, [P, HT, DH]) for n in ("h1_w", "h2_w")}
            nat["w3_w"] = ld.sb("w3_w", [P, DH])
            with nc.Block() as block:
                @block.sync
                def _(sp):
                    for b in range(B):
                        sp.dma_start(X[:, b * L // P:(b + 1) * L // P, :],
                                     x_dram[b].rearrange("(t p) d -> p t d", p=P)).then_inc(x_in, 16)
                    sp.wait_ge(x_in, 16 * B)

                @block.scalar
                def _(act):
                    n = 0
                    for name in ("w1_w", "w2_w", "h1_w", "h2_w"):
                        act.dma_start(nat[name][:, :, :], ins["L1_ffn_" + name].rearrange("(o p) i -> p o i", p=P)).then_inc(w_in, 16)
                    act.dma_start(nat["w3_w"][:, :], ins["L1_ffn_w3_w"]).then_inc(w_in, 16)
                    with nc.allow_non_contiguous_dma(reason="one scale a partition"):
                        for name, t in (("w1_s", f.s1), ("w2_s", f.s2), ("h1_s", f.sh1), ("h2_s", f.sh2)):
                            act.dma_start(t[:, :], ins["L1_ffn_" + name].rearrange("(o p) -> p o", p=P)).then_inc(w_in, 16)
                    act.dma_start(f.s3[:, :], ins["L1_ffn_w3_s"].partition_broadcast(P)).then_inc(w_in, 16)
                    act.wait_ge(w_in, 160)

                @block.gpsimd
                def _(pool):
                    pool.memset(res.minus_half[:, :], -0.5)
                    pool.memset(ident[:, :], 0.0).then_inc(id_ready, 1)
                    pool.wait_ge(id_ready, 1)
                    pool.affine_select(out=ident[:, :], in_=ident[:, :], compare_op=ALU.not_equal, fill=1.0, base=0,
                                       pattern=[[-1, P]], channel_multiplier=1).then_inc(id_ready, 1)

            jobs = []
            for o in range(HT):
                so = slice(o * P, (o + 1) * P)
                jobs += [(f.w1T[:, so], nat["w1_w"][:, o, :]), (f.w2T[:, so], nat["w2_w"][:, o, :])]
                for i in range(HT):
                    si = slice(i * P, (i + 1) * P)
                    jobs += [(f.h1T[:, i, so], nat["h1_w"][:, o, si]), (f.h2T[:, i, so], nat["h2_w"][:, o, si])]
                jobs.append((f.w3T[:, o, :], nat["w3_w"][:, so]))
            transpose_blocks(nc, res, "ffnw", jobs, [(w_in, 160), (id_ready, 2)])

        wb = Res()
        wb.Wq, wb.Wk, wb.Wv, wb.Wo = (ins["L0_attn_b_" + n] for n in ("Wq", "Wk", "Wv", "Wo"))
        wb.H, wb.DK, wb.DV, wb.biases, wb.alibi = 16, 8, 64, False, False
        wc = Res()
        wat, bat = ins["L1_attn_b_W_attn"], ins["L1_attn_b_b_attn"]
        wc.Wq, wc.Wk, wc.Wv = (wat[:, n * D:(n + 1) * D] for n in range(3))
        wc.bq, wc.bk, wc.bv = (bat[n * D:(n + 1) * D] for n in range(3))
        wc.Wo, wc.bo, wc.temperature = ins["L1_attn_b_W_proj"], ins["L1_attn_b_b_proj"], ins["L1_attn_b_temperature"]
        wc.alibi_q, wc.alibi_k = ins["alibi_q"], ins["alibi_k"]
        wc.H, wc.DK, wc.DV, wc.biases, wc.alibi = 16, 8, 8, True, True
        steps = [lambda: gated_attention(nc, res, 'gla', ins), lambda: expert_ffn(nc, res, 'moe1', ins), lambda: softmax_attention(nc, res, "sma", wb), lambda: expert_ffn(nc, res, 'moe2', ins), lambda: rope_attention(nc, res, 'rope', ins),
                 lambda: ternary_ffn(nc, res, "ffn5", f), lambda: softmax_attention(nc, res, "smb", wc),
                 lambda: ternary_ffn(nc, res, "ffn7", f)]
        for step in steps:
            with nc.cleanup_on_exit():
                step()

        with nc.Block() as block:
            @block.sync
            def _(sp):
                for b in range(B):
                    sp.dma_start(out[b].rearrange("(t p) d -> p t d", p=P), X[:, b * L // P:(b + 1) * L // P, :]).then_inc(x_out, 16)
                sp.wait_ge(x_out, 16 * B)


def kernel(**inputs):
    import numpy as _np
    import concourse.bacc as _bacc
    from concourse import mybir as _mybir
    from concourse.bass_utils import run_bass_kernel_spmd as _run

    nc = _bacc.Bacc("TRN2", target_bir_lowering=False, num_devices=1)
    arrays, args = {}, {}
    x = inputs["L0_attn_a_hidden_states"]
    items = dict(inputs)
    items["rope_cos"], items["rope_sin"], items["head_diag"] = rope_tables(x.shape[1], x.shape[2], x.shape[2] // HEADS)
    items["alibi_k"], items["alibi_q"] = alibi_rows(x.shape[1], HEADS)
    for name, a in items.items():
        a = _np.ascontiguousarray(a)
        arrays[f"in_{name}_dram"] = a
        args[name] = nc.dram_tensor(f"in_{name}_dram", a.shape, _mybir.dt.from_np(a.dtype), kind="ExternalInput").ap()
    out = nc.dram_tensor("out_0_dram", x.shape, F32, kind="ExternalOutput").ap()
    build_program(nc, args, out)
    r = _run(nc, [arrays], core_ids=[0])
    return r.results[0]["out_0_dram"]
```

```python
from contextlib import ExitStack

import numpy as np

import concourse.bass as bass
from concourse import mybir

F32 = mybir.dt.float32
BF16 = mybir.dt.bfloat16
U32 = mybir.dt.uint32
ALU = mybir.AluOpType
ACT = mybir.ActivationFunctionType
AX = mybir.AxisListType

P = 128
CHUNK = 512
TPC = CHUNK // P
EPS = 1e-5
HEADS = 16


class Scope:

    def __init__(self, nc, ctx, tag):
        self.nc, self.ctx, self.tag = nc, ctx, tag

    def sb(self, name, shape, dt=F32):
        return self.ctx.enter_context(self.nc.sbuf_tensor(f"{self.tag}_{name}", shape, dt))

    def sem(self, name):
        return self.nc.alloc_semaphore(name=f"{self.tag}_{name}")


def loop(eng, n, body):
    if n > 1:
        with eng.Fori(0, n - 1) as k:
            body(k, True)
    body(n - 1, False)


class Norm:

    def __init__(self, m, res, tiles=TPC, name="ln"):
        self.tiles = tiles
        self.minus_half = res.minus_half
        self.stats = m.sb(f"{name}_stats", [P, tiles, 6])
        self.mv = m.sb(f"{name}_mv", [P, tiles, 2])
        self.var = m.sb(f"{name}_var", [P, tiles])
        self.rstd = m.sb(f"{name}_rstd", [P, tiles])
        self.hold = m.sb(f"{name}_hold", [P, 1])
        self.step = m.sem(f"{name}_step")
        self.root = m.sem(f"{name}_root")

    def vector(self, dve, k, src, dst):
        norm_statistics(self, dve, k, src)
        return norm_result(self, dve, k, src, dst)

    def gpsimd(self, pool, k):
        pool.wait_ge(self.step, k * 3 + 3)
        pool.tensor_tensor(self.rstd[:, :], self.var[:, :], self.minus_half[:, 0:self.tiles], ALU.pow).then_inc(self.root, 1)


def norm_statistics(norm, dve, k, src):
    for j in range(norm.tiles):
        last = dve.bn_stats(norm.stats[:, j, :], src(j))
    last.then_inc(norm.step, 1)
    dve.wait_ge(norm.step, k * 3 + 1)
    dve.memset(norm.hold[:, :], 0.0)
    for j in range(norm.tiles):
        last = dve.bn_aggr(norm.mv[:, j, :], norm.stats[:, j, :])
    last.then_inc(norm.step, 1)
    dve.wait_ge(norm.step, k * 3 + 2)
    dve.tensor_scalar(norm.var[:, :], norm.mv[:, :, 1], EPS, None, ALU.add).then_inc(norm.step, 1)


def norm_result(norm, dve, k, src, dst):
    dve.wait_ge(norm.root, k + 1)
    for j in range(norm.tiles):
        last = dve.tensor_scalar(dst(j), src(j), norm.mv[:, j, 0:1], norm.rstd[:, j:j + 1],
                                 ALU.subtract, ALU.mult)
    return last


def transpose_blocks(nc, res, tag, jobs, arrived):
    turned, copied = nc.alloc_semaphore(name=f"{tag}_turned"), nc.alloc_semaphore(name=f"{tag}_copied")
    NB = len(res.banks)
    with nc.Block() as block:
        @block.tensor
        def _(pe):
            for sem, n in arrived:
                pe.wait_ge(sem, n)
            for i, (_, src) in enumerate(jobs):
                if i >= NB:
                    pe.wait_ge(copied, i - NB + 1)
                nc.tensor.transpose(res.banks[i % NB][:, 0:P], src, res.ident[:, :]).then_inc(turned, 1)

        @block.scalar
        def _(act):
            for i, (dst, _) in enumerate(jobs):
                act.wait_ge(turned, i + 1)
                nc.scalar.copy(dst, res.banks[i % NB][:, 0:P]).then_inc(copied, 1)


def ternary_ffn(nc, res, tag, w):
    X, banks, ident = res.X, res.banks, res.ident
    NCH = res.T // CHUNK
    HT = w.w1T.shape[1] // P
    with ExitStack() as ctx:
        m = Scope(nc, ctx, tag)
        norm = Norm(m, res)
        h = m.sb("h", [P, TPC, P])
        hT = m.sb("hT", [P, CHUNK])
        gate = m.sb("gate", [P, HT, CHUNK])
        acts = [m.sb(f"act{n}", [P, HT, CHUNK]) for n in range(3)]
        scaled = m.sb("scaled", [P, TPC, P])
        psA, psB, psT, psO = banks[0:3], banks[3:5], banks[5], banks[6]
        h_ready = m.sem("h_ready")
        turned = m.sem("turned")
        hT_ready = m.sem("hT_ready")
        a_ready = m.sem("a_ready")
        a_out = m.sem("a_out")
        b_ready = m.sem("b_ready")
        b_out = m.sem("b_out")
        o_ready = m.sem("o_ready")
        o_out = m.sem("o_out")
        x_ready = m.sem("x_ready")
        EARLY = HT // 2

        def place(layer, mt, more):
            return {0: HT + mt + (HT if mt >= EARLY else 0), 1: mt, 2: HT + mt + (EARLY if more else 0)}[layer]

        with nc.Block() as block:
            @block.vector
            def _(dve):
                dve.sem_inc(b_out, 2)
                dve.sem_inc(o_out, 1)
                dve.sem_inc(x_ready, 1)

                def norm_chunk(k):
                    norm.vector(dve, k, lambda j: X[:, bass.ds(k * TPC + j, 1), :], lambda j: h[:, j, :]).then_inc(h_ready, 1)

                def gated(k, mt, n):
                    dve.wait_ge(b_ready, k * HT + mt + 1)
                    dve.wait_ge(a_out, n + 4)
                    nc.vector.scalar_tensor_tensor(acts[0][:, mt, :], psB[mt % 2][:, :], w.s2[:, mt:mt + 1],
                                                   gate[:, mt, :], ALU.mult, ALU.mult).then_inc(b_out, 1)

                def chunk(k, more):
                    if more:
                        dve.wait_ge(turned, k + 1)
                        norm_chunk(k + 1)
                        for mt in range(HT):
                            gated(k + 1, mt, HT + k * 3 * HT + place(0, mt, more))
                    dve.wait_ge(x_ready, k + 1)
                    dve.wait_ge(o_ready, k + 1)
                    nc.vector.tensor_tensor(scaled[:, :, :], psO[:, :].rearrange("p (j n) -> p j n", j=TPC),
                                            w.s3[:, :].unsqueeze(1).to_broadcast([P, TPC, P]), ALU.mult).then_inc(o_out, 1)
                    dve.wait_ge(o_out, k + 2)
                    xk = X[:, bass.ds(k * TPC, TPC), :]
                    nc.vector.tensor_tensor(xk, xk, scaled[:, :, :], ALU.add).then_inc(x_ready, 1)

                norm_chunk(0)
                for mt in range(HT):
                    gated(0, mt, mt)
                loop(dve, NCH, chunk)

            @block.gpsimd
            def _(pool):
                with pool.Fori(0, NCH) as k:
                    norm.gpsimd(pool, k)

            @block.scalar
            def _(act):
                act.sem_inc(hT_ready, 1)
                act.sem_inc(a_out, 3)

                def copy_hT(k):
                    act.wait_ge(turned, k + 1)
                    nc.scalar.copy(hT[:, :], psT[:, :]).then_inc(hT_ready, 1)

                def silu(mt, n, bank):
                    act.wait_ge(a_ready, n + 1)
                    nc.scalar.activation(gate[:, mt, :], psA[bank][:, :], ACT.Silu, scale=w.s1[:, mt:mt + 1]).then_inc(a_out, 1)

                def chunk(k, more):
                    first = HT + k * 3 * HT

                    def gelu(layer, scale, mt):
                        n = place(layer, mt, more)
                        act.wait_ge(a_ready, first + n + 1)
                        nc.scalar.activation(acts[layer][:, mt, :], psA[(HT + n) % 3][:, :], ACT.Gelu,
                                             scale=scale[:, mt:mt + 1]).then_inc(a_out, 1)

                    def next_silu(mts):
                        for mt in mts:
                            n = place(0, mt, more)
                            silu(mt, first + n, (HT + n) % 3)

                    for mt in range(HT):
                        gelu(1, w.sh1, mt)
                        if more and mt == HT - 2:
                            copy_hT(k + 1)
                    if more:
                        next_silu(range(EARLY))
                    for mt in range(HT):
                        gelu(2, w.sh2, mt)
                    if more:
                        next_silu(range(EARLY, HT))

                copy_hT(0)
                for mt in range(HT):
                    silu(mt, mt, mt % 3)
                loop(act, NCH, chunk)

            @block.tensor
            def _(pe):
                def turn(k):
                    pe.wait_ge(h_ready, k + 1)
                    pe.wait_ge(hT_ready, k + 1)
                    for j in range(TPC):
                        last = nc.tensor.transpose(psT[:, j * P:(j + 1) * P], h[:, j, :], ident[:, :])
                    last.then_inc(turned, 1)

                def first_layer(k, mt, n, bank):
                    pe.wait_ge(hT_ready, k + 2)
                    pe.wait_ge(a_out, n + 1)
                    nc.tensor.matmul(psA[bank][:, :], w.w1T[:, mt * P:(mt + 1) * P], hT[:, :],
                                     start=True, stop=True).then_inc(a_ready, 1)
                    pe.wait_ge(b_out, k * HT + mt + 1)
                    nc.tensor.matmul(psB[mt % 2][:, :], w.w2T[:, mt * P:(mt + 1) * P], hT[:, :],
                                     start=True, stop=True).then_inc(b_ready, 1)

                def chunk(k, more):
                    first = HT + k * 3 * HT

                    def hidden(layer, wT, mt):
                        n = place(layer, mt, more)
                        pe.wait_ge(a_out, first + n + 1)
                        for kt in range(HT):
                            if mt == 0:
                                if layer == 1:
                                    pe.wait_ge(b_out, k * HT + kt + 3)
                                else:
                                    pe.wait_ge(a_out, first + place(1, kt, more) + 4)
                            last = nc.tensor.matmul(psA[(HT + n) % 3][:, :], wT[:, kt, mt * P:(mt + 1) * P],
                                                    acts[layer - 1][:, kt, :], start=(kt == 0), stop=(kt == HT - 1))
                        last.then_inc(a_ready, 1)

                    def next_layer(mts):
                        for mt in mts:
                            n = place(0, mt, more)
                            first_layer(k + 1, mt, first + n, (HT + n) % 3)

                    for mt in range(HT):
                        if more and mt == HT - 1:
                            turn(k + 1)
                        hidden(1, w.h1T, mt)
                    if more:
                        next_layer(range(EARLY))
                    for mt in range(HT):
                        hidden(2, w.h2T, mt)
                    if more:
                        next_layer(range(EARLY, HT))
                    pe.wait_ge(o_out, k + 1)
                    pe.wait_ge(a_out, first + place(2, HT - 1, more) + 4)
                    for j in range(TPC):
                        for kt in range(HT):
                            last = nc.tensor.matmul(psO[:, j * P:(j + 1) * P], acts[2][:, kt, j * P:(j + 1) * P],
                                                    w.w3T[:, kt, :], start=(kt == 0), stop=(kt == HT - 1))
                    last.then_inc(o_ready, 1)

                turn(0)
                for mt in range(HT):
                    first_layer(0, mt, mt, mt % 3)
                loop(pe, NCH, chunk)


def gated_attention(nc, res, tag, ins):
    X, banks, ident = res.X, res.banks, res.ident
    NB, CPB, TPB = res.B, res.L // CHUNK, res.L // P
    D, H = P, 16
    DV = D // H
    assert CPB == 2
    with ExitStack() as ctx:
        m = Scope(nc, ctx, tag)
        norm = Norm(m, res)
        wqf, wi = m.sb("wqf", [P, 2 * D]), m.sb("wi", [P, D])
        wir, wor = m.sb("wir", [P, DV, D]), m.sb("wor", [P, DV, D])
        h = m.sb("h", [P, TPC, P])
        hT = m.sb("hT", [P, CPB, CHUNK])
        neg, total, inv = m.sb("neg", [P, TPC, 2]), m.sb("total", [P, TPC * 2]), m.sb("inv", [P, TPC * 2])
        e = m.sb("e", [P, TPC, 2, P])
        qT, fT, kT = (m.sb(n, [P, CPB, CHUNK]) for n in ("qT", "fT", "kT"))
        kv = m.sb("kv", [P, 2, CHUNK])
        S = m.sb("S", [P, CPB, DV, CHUNK])
        qS = m.sb("qS", [P, CPB, DV, CHUNK])
        psT, psL, psV, psQ, psF, psO = banks[0], banks[1:3], banks[3:5], banks[5], banks[6], banks[7]
        loaded = m.sem("loaded")
        spread = m.sem("spread")
        h_ready = m.sem("h_ready")
        turned = m.sem("turned")
        hT_ready = m.sem("hT_ready")
        l_ready = m.sem("l_ready")
        neg_ready = m.sem("neg_ready")
        e_ready = m.sem("e_ready")
        inv_ready = m.sem("inv_ready")
        soft_ready = m.sem("soft_ready")
        qf_turned = m.sem("qf_turned")
        qf_ready = m.sem("qf_ready")
        k_ready = m.sem("k_ready")
        v_ready = m.sem("v_ready")
        kv_ready = m.sem("kv_ready")
        s_ready = m.sem("s_ready")
        qs_ready = m.sem("qs_ready")
        o_ready = m.sem("o_ready")
        x_ready = m.sem("x_ready")
        LOADS = 4

        def batches(eng, batch):
            batch(0, True, True)
            with eng.Fori(1, NB - 1) as b:
                batch(b, False, True)
            batch(NB - 1, False, False)

        with nc.Block() as block:
            @block.sync
            def _(sp):
                for t, name in ((wqf[:, 0:D], "Wq"), (wqf[:, D:2 * D], "Wf"), (wi[:, :], "Wi")):
                    sp.dma_start(t, ins["L0_attn_a_" + name]).then_inc(loaded, 16)
                sp.dma_start(wor[:, :, :].rearrange("p v n -> p (v n)"),
                             ins["L0_attn_a_Wo"].rearrange("(h v) n -> h (v n)", v=DV).unsqueeze(1).to_broadcast([H, DV, DV * D])).then_inc(loaded, 16)
                sp.wait_ge(loaded, 16 * LOADS)

            @block.vector
            def _(dve):
                dve.sem_inc(k_ready, 1)
                dve.sem_inc(kv_ready, 2)
                dve.sem_inc(x_ready, 1)

                x = lambda k: lambda j: X[:, bass.ds(k * TPC + j, 1), :]

                def normalised(k):
                    norm_result(norm, dve, k, x(k), lambda j: h[:, j, :]).then_inc(h_ready, 1)

                def maxima(k):
                    dve.wait_ge(l_ready, k + 1)
                    for half in range(2):
                        last = nc.vector.tensor_reduce(neg[:, 2 * half:2 * half + 2, :], psL[half][:, :].rearrange("p (j w n) -> p j w n", j=2, w=2),
                                                       AX.X, ALU.max, negate=True)
                    last.then_inc(neg_ready, 1)

                def inverse(k):
                    dve.wait_ge(e_ready, k + 2)
                    nc.vector.reciprocal(inv[:, :], total[:, :]).then_inc(inv_ready, 1)

                def one_minus(k, c):
                    dve.wait_ge(qf_ready, k + 2)
                    nc.vector.tensor_scalar(kT[:, c, :], fT[:, c, :], -1.0, 1.0, ALU.mult, ALU.add).then_inc(k_ready, 1)

                def scan(k, c, v):
                    n = k * DV + v
                    dve.wait_ge(v_ready, n + 1)
                    if v == 0:
                        dve.wait_ge(k_ready, k + 2)
                    nc.vector.tensor_tensor(kv[:, v % 2, :], psV[v % 2][:, :], kT[:, c, :], ALU.mult).then_inc(kv_ready, 1)
                    dve.wait_ge(kv_ready, n + 3)
                    nc.vector.tensor_tensor_scan(S[:, c, v, :], fT[:, c, :], kv[:, v % 2, :],
                                                 0.0 if c == 0 else S[:, 0, v, CHUNK - 1:CHUNK], ALU.mult, ALU.add).then_inc(s_ready, 1)

                norm_statistics(norm, dve, 0, x(0))
                normalised(0)
                maxima(0)
                dve.wait_ge(loaded, 16 * LOADS)
                for v in range(DV):
                    nc.vector.tensor_copy(wir[:, v, :].rearrange("p (h k) -> p h k", k=DV),
                                          wi[:, :].rearrange("p (h v) -> p v h", v=DV)[:, v, :].unsqueeze(2).to_broadcast([P, H, DV])).then_inc(spread, 1)
                norm_statistics(norm, dve, 1, x(1))
                normalised(1)
                inverse(0)
                one_minus(0, 0)

                def add_output(k):
                    dve.wait_ge(o_ready, k + 3)
                    xk = X[:, bass.ds(k * TPC, TPC), :]
                    nc.vector.tensor_tensor(xk, xk, psO[:, :].rearrange("p (j n) -> p j n", j=TPC), ALU.add).then_inc(x_ready, 1)

                def batch(b, first, more):
                    for c in range(CPB):
                        k = b * CPB + c
                        ahead = c + 1 < CPB or more
                        for v in range(DV):
                            if v == 3 and ahead:
                                maxima(k + 1)
                            if v == 5 and ahead:
                                inverse(k + 1)
                            if v == 0 and more:
                                norm_statistics(norm, dve, k + 2, x(k + 2))
                            if v == 5 and more:
                                normalised(k + 2)
                            scan(k, c, v)
                        if c or not first:
                            add_output(k - 1)
                        if ahead:
                            one_minus(k + 1, 1 - c)
                batches(dve, batch)
                add_output(NB * CPB - 1)

            @block.gpsimd
            def _(pool):
                def soften(k):
                    pool.wait_ge(inv_ready, k + 1)
                    ev = e[:, :, :, :].rearrange("p j w n -> p (j w) n")
                    nc.gpsimd.tensor_tensor(ev, ev, inv[:, :].unsqueeze(2).to_broadcast([P, 2 * TPC, P]), ALU.mult).then_inc(soft_ready, 1)

                def read(k, c, v):
                    if v == 0:
                        pool.wait_ge(o_ready, k + 1)
                    pool.wait_ge(s_ready, k * DV + v + 1)
                    nc.gpsimd.tensor_tensor(qS[:, c, v, :], S[:, c, v, :], qT[:, c, :], ALU.mult).then_inc(qs_ready, 1)

                norm.gpsimd(pool, 0)
                norm.gpsimd(pool, 1)
                soften(0)

                def batch(b, first, more):
                    for c in range(CPB):
                        k = b * CPB + c
                        ahead = c + 1 < CPB or more
                        if more:
                            norm.gpsimd(pool, k + 2)
                        for v in range(5):
                            read(k, c, v)
                        if ahead:
                            soften(k + 1)
                        for v in range(5, DV):
                            read(k, c, v)
                batches(pool, batch)

            @block.scalar
            def _(act):
                act.sem_inc(e_ready, 1)
                act.sem_inc(qf_ready, 1)

                def front(k, c):
                    act.wait_ge(turned, k + 1)
                    nc.scalar.copy(hT[:, c, :], psT[:, :]).then_inc(hT_ready, 1)
                    act.wait_ge(neg_ready, k + 1)
                    for j in range(TPC):
                        for which in range(2):
                            col = (j % 2) * 2 * P + which * P
                            last = nc.scalar.activation(e[:, j, which, :], psL[j // 2][:, col:col + P], ACT.Exp,
                                                        bias=neg[:, j, which:which + 1],
                                                        accum_out=total[:, 2 * j + which:2 * j + which + 1])
                    last.then_inc(e_ready, 1)
                    act.wait_ge(qf_turned, k + 1)
                    nc.scalar.copy(fT[:, c, :], psF[:, :])
                    nc.scalar.copy(qT[:, c, :], psQ[:, :]).then_inc(qf_ready, 1)

                front(0, 0)
                act.wait_ge(loaded, 16 * LOADS)
                nc.scalar.mul(wor[:, :, :], wor[:, :, :], float(np.float32(DV ** -0.5))).then_inc(spread, 1)

                def batch(b, first, more):
                    for c in range(CPB):
                        if c + 1 < CPB or more:
                            front(b * CPB + c + 1, 1 - c)
                batches(act, batch)

            @block.tensor
            def _(pe):
                pe.sem_inc(o_ready, 2)

                def turn(k):
                    pe.wait_ge(h_ready, k + 1)
                    for j in range(TPC):
                        last = nc.tensor.transpose(psT[:, j * P:(j + 1) * P], h[:, j, :], ident[:, :])
                    last.then_inc(turned, 1)

                def logits(k, c):
                    pe.wait_ge(hT_ready, k + 1)
                    pe.wait_ge(e_ready, k + 1)
                    for j in range(TPC):
                        last = nc.tensor.matmul(psL[j // 2][:, (j % 2) * 2 * P:(j % 2 + 1) * 2 * P], hT[:, c, j * P:(j + 1) * P],
                                                wqf[:, :], start=True, stop=True)
                    last.then_inc(l_ready, 1)

                def turn_softmaxes(k):
                    pe.wait_ge(soft_ready, k + 1)
                    pe.wait_ge(qf_ready, k + 1)
                    for which, ps in ((0, psQ), (1, psF)):
                        for j in range(TPC):
                            last = nc.tensor.transpose(ps[:, j * P:(j + 1) * P], e[:, j, which, :], ident[:, :])
                    last.then_inc(qf_turned, 1)

                def values(k, c, v):
                    pe.wait_ge(kv_ready, k * DV + v + 1)
                    nc.tensor.matmul(psV[v % 2][:, :], wir[:, v, :], hT[:, c, :], start=True, stop=True).then_inc(v_ready, 1)

                def output(k, c, j):
                    if j == 0:
                        pe.wait_ge(qs_ready, (k + 1) * DV)
                        pe.wait_ge(x_ready, k + 1)
                    for v in range(DV):
                        last = nc.tensor.matmul(psO[:, j * P:(j + 1) * P], qS[:, c, v, j * P:(j + 1) * P], wor[:, v, :],
                                                start=(v == 0), stop=(v == DV - 1))
                    if j == TPC - 1:
                        last.then_inc(o_ready, 1)

                def batch(b, first, more):
                    for c in range(CPB):
                        k = b * CPB + c
                        ahead = c + 1 < CPB or more
                        for v in range(DV):
                            if v == 0 and ahead:
                                turn(k + 1)
                            if v == 2 and ahead:
                                logits(k + 1, 1 - c)
                            values(k, c, v)
                            if 2 <= v < 2 + TPC and (c or not first):
                                output(k - 1, 1 - c, v - 2)
                        if ahead:
                            turn_softmaxes(k + 1)

                turn(0)
                pe.wait_ge(loaded, 16 * LOADS)
                logits(0, 0)
                turn_softmaxes(0)
                pe.wait_ge(spread, DV + 1)
                batches(pe, batch)
                for j in range(TPC):
                    output(NB * CPB - 1, 1, j)


def expert_ffn(nc, res, tag, ins):
    X, banks, ident = res.X, res.banks, res.ident
    NCH, NT = res.T // CHUNK, res.NT
    NE, D, I = ins["L0_ffn_wi"].shape
    CAP = 256
    SLOTS, IT, ST = NE * CAP, I // P, CAP // P
    W = D + 1
    tok_dram = nc.dram_tensor(f"{tag}_tokens", [SLOTS, W], F32).ap()
    out_dram = nc.dram_tensor(f"{tag}_outs", [res.T, D], F32).ap()
    with ExitStack() as outer:
        o = Scope(nc, outer, tag)
        Hres = o.sb("Hres", [P, NT, D])
        tok = o.sb("tok", [P, NT, W])
        weight = o.sb("weight", [P, NT])
        to_slot = o.sb("to_slot", [P, NT], U32)
        zeros = o.sb("zeros", [P, SLOTS * W // P])
        HALF_OUT = res.T * D // P // 2
        zeroed = o.sem("zeroed")

        with ExitStack() as ctx:
            m = Scope(nc, ctx, tag + "r")
            norm1, norm2 = Norm(m, res, name="ln1"), Norm(m, res, name="ln2")
            gamma, beta = m.sb("gamma", [P, D]), m.sb("beta", [P, D])
            gate = m.sb("gate", [P, NE])
            marks = m.sb("marks", [P, NT])
            n2 = m.sb("n2", [P, TPC, D])
            t2 = m.sb("t2", [P, TPC, D])
            tT = m.sb("tT", [P, CHUNK])
            lg = m.sb("lg", [P, NE, NT])
            countdown = m.sb("countdown", [P, NE])
            best, first = m.sb("best", [P, NT]), m.sb("first", [P, NT])
            a, b_, oneh, incl = (m.sb(n, [P, NE, NT]) for n in ("a", "b", "oneh", "incl"))
            keepmask = m.sb("keepmask", [P, NE, NT])
            onehb, exclb = m.sb("onehb", [P, NE, NT], BF16), m.sb("exclb", [P, NE, NT], BF16)
            rank, keep, slot = (m.sb(n, [P, NT]) for n in ("rank", "keep", "slot"))
            sums = m.sb("sums", [P, NT])
            before, ones = m.sb("before", [P, P], BF16), m.sb("ones", [P, P], BF16)
            psT, psL, psR = banks[0], banks[1], banks[2]
            loaded = m.sem("loaded")
            made, ones_made = m.sem("made"), m.sem("ones_made")
            n1_ready = m.sem("n1_ready")
            n2_ready = m.sem("n2_ready")
            g_ready = m.sem("g_ready")
            t2_ready = m.sem("t2_ready")
            turned = m.sem("turned")
            tT_ready = m.sem("tT_ready")
            tok_kept = m.sem("tok_kept")
            l_ready = m.sem("l_ready")
            lg_ready = m.sem("lg_ready")
            ch = m.sem("ch")
            diff_ready, exp_ready = m.sem("diff_ready"), m.sem("exp_ready")
            count_ready, r_ready = m.sem("count_ready"), m.sem("r_ready")

            with nc.Block() as block:
                @block.sync
                def _(sp):
                    sp.dma_start(gamma[:, :], ins["L0_ffn_ln_gamma"].partition_broadcast(P)).then_inc(loaded, 16)
                    sp.dma_start(beta[:, :], ins["L0_ffn_ln_beta"].partition_broadcast(P)).then_inc(loaded, 16)
                    sp.dma_start(marks[:, :], ins["token_marks"]).then_inc(loaded, 16)
                    with nc.allow_non_contiguous_dma(reason="a small matrix, turned"):
                        sp.dma_start(gate[:, :], ins["L0_ffn_gate_weight"].rearrange("e d -> d e")).then_inc(loaded, 16)
                    sp.wait_ge(made, 1)
                    sp.dma_start(tok_dram.rearrange("(p s) d -> p (s d)", p=P), zeros[:, :]).then_inc(zeroed, 16)
                    for half in out_dram.rearrange("(o p s) d -> o p (s d)", o=2, p=P):
                        sp.dma_start(half, zeros[:, 0:HALF_OUT]).then_inc(zeroed, 16)
                    sp.wait_ge(zeroed, 48)
                    sp.wait_ge(loaded, 64)

                @block.vector
                def _(dve):
                    nc.vector.memset(zeros[:, :], 0.0).then_inc(made, 1)
                    nc.vector.memset(keepmask[:, :, :], 1.0).then_inc(ch, 1)
                    for e in range(NE):
                        nc.vector.memset(countdown[:, e:e + 1], float(NE - e))
                    dve.wait_ge(ch, 1)
                    nc.vector.memset(keepmask[:, :, 0:1], 0.0).then_inc(ch, 1)

                    x = lambda k: lambda j: X[:, bass.ds(k * TPC + j, 1), :]
                    hr = lambda k: lambda j: Hres[:, bass.ds(k * TPC + j, 1), :]

                    def first_norm(k):
                        norm_result(norm1, dve, k, x(k), hr(k)).then_inc(n1_ready, 1)
                        dve.wait_ge(n1_ready, k + 1)
                        nc.vector.memset(norm2.hold[:, :], 0.0)
                        norm_statistics(norm2, dve, k, hr(k))

                    def chunk(k, more):
                        if more:
                            norm_statistics(norm1, dve, k + 1, x(k + 1))
                        dve.wait_ge(g_ready, k + 1)
                        norm_result(norm2, dve, k, hr(k), lambda j: n2[:, j, :]).then_inc(n2_ready, 1)
                        xk, hk = X[:, bass.ds(k * TPC, TPC), :], Hres[:, bass.ds(k * TPC, TPC), :]
                        nc.vector.tensor_tensor(xk, xk, hk, ALU.add)
                        if more:
                            first_norm(k + 1)

                    norm_statistics(norm1, dve, 0, x(0))
                    first_norm(0)
                    loop(dve, NCH, chunk)

                    steps = [2]

                    def then(ins_):
                        steps[0] += 1
                        ins_.then_inc(ch, 1)
                        dve.wait_ge(ch, steps[0])

                    by_e = lambda t: t[:, :, :].rearrange("p e t -> p t e")
                    over_e = lambda t: t[:, :].unsqueeze(1).to_broadcast([P, NE, NT])
                    over_t = lambda t: t[:, :].unsqueeze(2).to_broadcast([P, NE, NT])
                    dve.wait_ge(lg_ready, NCH + 1)
                    then(nc.vector.tensor_reduce(best[:, :], by_e(lg), AX.X, ALU.max))
                    nc.vector.tensor_tensor(a[:, :, :], lg[:, :, :], over_e(best), ALU.subtract).then_inc(diff_ready, 1)
                    then(nc.vector.tensor_tensor(b_[:, :, :], lg[:, :, :], over_e(best), ALU.is_equal))
                    then(nc.vector.tensor_tensor(b_[:, :, :], b_[:, :, :], over_t(countdown), ALU.mult))
                    then(nc.vector.tensor_reduce(first[:, :], by_e(b_), AX.X, ALU.max))
                    then(nc.vector.tensor_tensor(oneh[:, :, :], over_e(first), over_t(countdown), ALU.is_equal))
                    then(nc.vector.tensor_tensor_scan(incl[:, :, :].rearrange("p e t -> p (e t)"), keepmask[:, :, :].rearrange("p e t -> p (e t)"),
                                                      oneh[:, :, :].rearrange("p e t -> p (e t)"), 0.0, ALU.mult, ALU.add))
                    nc.vector.tensor_copy(onehb[:, :, :], oneh[:, :, :])
                    nc.vector.tensor_tensor(exclb[:, :, :], incl[:, :, :], oneh[:, :, :], ALU.subtract).then_inc(count_ready, 1)
                    dve.wait_ge(exp_ready, 1)
                    then(nc.vector.tensor_reduce(sums[:, :], by_e(a), AX.X, ALU.add))
                    then(nc.vector.reciprocal(sums[:, :], sums[:, :]))
                    dve.wait_ge(r_ready, 1)
                    then(nc.vector.tensor_tensor(b_[:, :, :], psR[:, 0:NE * NT].rearrange("p (e t) -> p e t", e=NE), oneh[:, :, :], ALU.mult))
                    then(nc.vector.tensor_reduce(rank[:, :], by_e(b_), AX.X, ALU.add))
                    then(nc.vector.tensor_scalar(keep[:, :], rank[:, :], float(CAP), None, ALU.is_lt))
                    nc.vector.tensor_tensor(weight[:, :], sums[:, :], keep[:, :], ALU.mult)
                    then(nc.vector.scalar_tensor_tensor(slot[:, :], first[:, :], -float(CAP), rank[:, :], ALU.mult, ALU.add))
                    then(nc.vector.scalar_tensor_tensor(slot[:, :], keep[:, :], -2.0 * SLOTS, slot[:, :], ALU.mult, ALU.add))
                    then(nc.vector.tensor_scalar(slot[:, :], slot[:, :], float(NE * CAP + 2 * SLOTS), None, ALU.add))
                    nc.vector.tensor_copy(to_slot[:, :], slot[:, :])

                @block.gpsimd
                def _(pool):
                    pool.sem_inc(turned, 1)
                    pool.sem_inc(g_ready, 1)
                    pool.memset(ones[:, :], 1.0).then_inc(ones_made, 1)
                    pool.wait_ge(ones_made, 1)
                    pool.affine_select(out=before[:, :], in_=ones[:, :], compare_op=ALU.is_gt, fill=0.0, base=0,
                                       pattern=[[1, P]], channel_multiplier=-1).then_inc(ones_made, 1)
                    pool.wait_ge(loaded, 64)

                    def chunk(k, more):
                        norm2.gpsimd(pool, k)
                        if more:
                            norm1.gpsimd(pool, k + 1)
                        pool.wait_ge(n2_ready, k + 1)
                        pool.wait_ge(turned, k + 1)
                        pool.wait_ge(tok_kept, k + 1)
                        wide = lambda t: t[:, :].unsqueeze(1).to_broadcast([P, TPC, D])
                        nc.gpsimd.tensor_tensor(t2[:, :, :], n2[:, :, :], wide(gamma), ALU.mult).then_inc(g_ready, 1)
                        pool.wait_ge(g_ready, k + 2)
                        nc.gpsimd.tensor_tensor(t2[:, :, :], t2[:, :, :], wide(beta), ALU.add).then_inc(t2_ready, 1)
                    norm1.gpsimd(pool, 0)
                    loop(pool, NCH, chunk)

                @block.scalar
                def _(act):
                    act.sem_inc(tok_kept, 1)
                    act.sem_inc(lg_ready, 1)
                    act.wait_ge(loaded, 64)
                    nc.scalar.copy(tok[:, :, D:W], marks[:, :].unsqueeze(2))

                    def chunk(k, more):
                        act.wait_ge(t2_ready, k + 1)
                        nc.scalar.copy(tok[:, bass.ds(k * TPC, TPC), 0:D], t2[:, :, :]).then_inc(tok_kept, 1)
                        act.wait_ge(turned, k + 2)
                        nc.scalar.copy(tT[:, :], psT[:, :]).then_inc(tT_ready, 1)
                        act.wait_ge(l_ready, k + 1)
                        nc.scalar.copy(lg[:, :, bass.ds(k * TPC, TPC)],
                                       psL[:, 0:TPC * NE].rearrange("p (j e) -> p e j", e=NE)).then_inc(lg_ready, 1)
                    loop(act, NCH, chunk)
                    act.wait_ge(diff_ready, 1)
                    nc.scalar.activation(a[:, :, :], a[:, :, :], ACT.Exp).then_inc(exp_ready, 1)

                @block.tensor
                def _(pe):
                    pe.wait_ge(loaded, 64)

                    def chunk(k, more):
                        pe.wait_ge(t2_ready, k + 1)
                        for j in range(TPC):
                            last = nc.tensor.transpose(psT[:, j * P:(j + 1) * P], t2[:, j, :], ident[:, :])
                        last.then_inc(turned, 1)
                        pe.wait_ge(tT_ready, k + 1)
                        pe.wait_ge(lg_ready, k + 1)
                        for j in range(TPC):
                            last = nc.tensor.matmul(psL[:, j * NE:(j + 1) * NE], tT[:, j * P:(j + 1) * P], gate[:, :], start=True, stop=True)
                        last.then_inc(l_ready, 1)
                    loop(pe, NCH, chunk)
                    pe.wait_ge(ones_made, 2)
                    pe.wait_ge(count_ready, 1)
                    nc.tensor.matmul(psR[:, 0:NE * NT], before[:, :], onehb[:, :, :].rearrange("p e t -> p (e t)"), start=True, stop=False)
                    nc.tensor.matmul(psR[:, 0:NE * NT], ones[:, :], exclb[:, :, :].rearrange("p e t -> p (e t)"), start=False, stop=True).then_inc(r_ready, 1)

        with ExitStack() as ctx:
            m = Scope(nc, ctx, tag + "e")
            Q = 4
            wi, wo = m.sb("wi", [P, Q, I]), m.sb("wo", [P, Q, IT, D])
            dsp = m.sb("dsp", [P, Q, ST, W])
            home = m.sb("home", [P, 2, ST], U32)
            dT = m.sb("dT", [P, 2, CAP])
            hid = m.sb("hid", [P, 2, IT, CAP])
            eo = m.sb("eo", [P, 2, ST, D])
            psT, psU, psD = banks[0], banks[1:5], banks[5:7]
            scattered = m.sem("scattered")
            w_in = [m.sem(f"w_in{n}") for n in range(Q)]
            d_in = [m.sem(f"d_in{n}") for n in range(Q)]
            turned = m.sem("turned")
            dT_ready = m.sem("dT_ready")
            u_ready = m.sem("u_ready")
            h_ready = m.sem("h_ready")
            d_ready = m.sem("d_ready")
            eo_ready = m.sem("eo_ready")
            eo_sent = m.sem("eo_sent")
            eo_free = m.sem("eo_free")

            with nc.Block() as block:
                @block.gpsimd
                def _(pool):
                    for t in range(NT):
                        pool.indirect_dma_start(out=tok_dram, out_offset=bass.IndirectOffsetOnAxis(ap=to_slot[:, t:t + 1], axis=0),
                                                in_=tok[:, t, :], in_offset=None, bounds_check=SLOTS - 1, oob_is_err=False).then_inc(scattered, 16)
                    pool.wait_ge(scattered, 16 * NT)
                    for e in range(NE):
                        pool.wait_ge(eo_ready, e + 3)
                        for n in range(ST):
                            pool.indirect_dma_start(out=out_dram, out_offset=bass.IndirectOffsetOnAxis(ap=home[:, e % 2, n:n + 1], axis=0),
                                                    in_=eo[:, e % 2, n, :], in_offset=None, bounds_check=res.T - 1, oob_is_err=False).then_inc(eo_sent, 16)
                        pool.wait_ge(eo_sent, (e + 1) * ST * 16)
                        pool.sem_inc(eo_free, 1)

                @block.sync
                def _(sp):
                    def weights(e):
                        if e >= Q:
                            sp.wait_ge(d_ready, e - Q + 1)
                        sp.dma_start(wi[:, e % Q, :], ins["L0_ffn_wi"][e]).then_inc(w_in[e % Q], 16)
                        sp.dma_start(wo[:, e % Q, :, :], ins["L0_ffn_wo"][e].rearrange("(c p) d -> p c d", p=P)).then_inc(w_in[e % Q], 16)

                    def rows(e):
                        if e >= Q:
                            sp.wait_ge(eo_ready, e - Q + 3)
                        sp.dma_start(dsp[:, e % Q, :, :], tok_dram[e * CAP:(e + 1) * CAP, :].rearrange("(s p) d -> p s d", p=P)).then_inc(d_in[e % Q], 16)

                    for e in range(Q):
                        weights(e)
                    sp.wait_ge(scattered, 16 * NT)
                    for e in range(Q):
                        rows(e)
                    for e in range(Q, NE):
                        weights(e)
                        rows(e)

                @block.scalar
                def _(act):
                    act.sem_inc(dT_ready, 1)
                    act.sem_inc(h_ready, 4)
                    act.sem_inc(eo_free, 2)
                    with act.Fori(0, NE // 2) as i:
                        for par in range(2):
                            e = i * 2 + par
                            act.wait_ge(turned, e + 1)
                            nc.scalar.copy(dT[:, par, :], psT[:, 0:CAP]).then_inc(dT_ready, 1)
                            for g in range(2):
                                act.wait_ge(u_ready, e * 2 + g + 1)
                                nc.scalar.activation(hid[:, par, 2 * g:2 * g + 2, :], psU[2 * par + g][:, :].rearrange("p (c s) -> p c s", c=2),
                                                     ACT.Gelu).then_inc(h_ready, 1)

                @block.vector
                def _(dve):
                    dve.sem_inc(eo_ready, 2)
                    with dve.Fori(0, NE // Q) as i:
                        for q in range(Q):
                            e, par = i * Q + q, q % 2
                            dve.wait_ge(d_ready, e + 1)
                            dve.wait_ge(eo_free, e + 1)
                            nc.vector.tensor_scalar(home[:, par, :], dsp[:, q, :, D:W].rearrange("p s o -> p (s o)"), -1.0, float(res.T),
                                                    ALU.mult, ALU.add)
                            nc.vector.tensor_copy(eo[:, par, :, :], psD[par][:, 0:ST * D].rearrange("p (s d) -> p s d", s=ST)).then_inc(eo_ready, 1)

                @block.tensor
                def _(pe):
                    def turn(i, q):
                        e = i * Q + q
                        pe.wait_ge(d_in[q], i * 16 + 16)
                        pe.wait_ge(dT_ready, e + 1)
                        for s in range(ST):
                            last = nc.tensor.transpose(psT[:, s * P:(s + 1) * P], dsp[:, q, s, 0:D], ident[:, :])
                        last.then_inc(turned, 1)

                    def first_product(i, q):
                        e, par = i * Q + q, q % 2
                        pe.wait_ge(w_in[q], i * 32 + 32)
                        pe.wait_ge(dT_ready, e + 2)
                        for g in range(2):
                            pe.wait_ge(h_ready, e * 2 + g + 1)
                            for c in (2 * g, 2 * g + 1):
                                last = nc.tensor.matmul(psU[2 * par + g][:, (c % 2) * CAP:(c % 2 + 1) * CAP], wi[:, q, c * P:(c + 1) * P],
                                                        dT[:, par, :], start=True, stop=True)
                            last.then_inc(u_ready, 1)

                    def some(i, more):
                        for q in range(Q):
                            e, par = i * Q + q, q % 2
                            if q + 1 < Q:
                                first_product(i, q + 1)
                            elif more:
                                first_product(i + 1, 0)
                            if q + 2 < Q:
                                turn(i, q + 2)
                            elif more:
                                turn(i + 1, q + 2 - Q)
                            pe.wait_ge(h_ready, e * 2 + 6)
                            pe.wait_ge(eo_ready, e + 1)
                            for s in range(ST):
                                for c in range(IT):
                                    last = nc.tensor.matmul(psD[par][:, s * D:(s + 1) * D], hid[:, par, c, s * P:(s + 1) * P], wo[:, q, c, :],
                                                            start=(c == 0), stop=(c == IT - 1))
                            last.then_inc(d_ready, 1)

                    turn(0, 0)
                    first_product(0, 0)
                    turn(0, 1)
                    loop(pe, NE // Q, some)

        with ExitStack() as ctx:
            m = Scope(nc, ctx, tag + "c")
            back = m.sb("back", [P, NT, D])
            came = [m.sem(f"came{n}") for n in range(NCH)]
            x_ready = m.sem("x_ready")
            with nc.Block() as block:
                @block.sync
                def _(sp):
                    for k in range(NCH):
                        sp.dma_start(back[:, k * TPC:(k + 1) * TPC, :],
                                     out_dram[k * CHUNK:(k + 1) * CHUNK, :].rearrange("(t p) d -> p t d", p=P)).then_inc(came[k], 16)

                @block.vector
                def _(dve):
                    for t in range(NT):
                        if t % TPC == 0:
                            dve.wait_ge(came[t // TPC], 16)
                        last = nc.vector.scalar_tensor_tensor(X[:, t, :], back[:, t, :], weight[:, t:t + 1], X[:, t, :], ALU.mult, ALU.add)
                    last.then_inc(x_ready, 1)


def token_marks(T):
    return (T - np.arange(T, dtype=np.float32)).reshape(T // P, P).T.copy()


def rope_tables(L, D, hd):
    scale = np.arange(0, hd, 2, dtype=np.float32)
    freqs = (np.float32(1.0) / np.float32(10000.0) ** scale).astype(np.float32)
    angles = np.arange(L, dtype=np.float32)[:, None] * freqs[None, :]
    cos, sin = np.cos(angles).astype(np.float32), np.sin(angles).astype(np.float32)
    cos = np.tile(np.repeat(cos, 2, axis=1), (1, D // hd))
    sin = np.tile(np.stack([-sin, sin], axis=-1).reshape(L, hd), (1, D // hd))
    head = np.arange(D) // hd
    diag = (head[:, None] == head[None, :]).astype(np.float32) / np.sqrt(np.float32(hd))
    return cos, sin, diag.astype(np.float32)


def rope_attention(nc, res, tag, ins):
    X, banks, ident = res.X, res.banks, res.ident
    NB, CPB = res.B, res.L // CHUNK
    TPB = res.L // P
    assert CPB == 2
    with ExitStack() as ctx:
        m = Scope(nc, ctx, tag)
        norm = Norm(m, res)
        wqkv = m.sb("wqkv", [P, 3 * P])
        wo = m.sb("wo", [P, P])
        bqkv = m.sb("bqkv", [P, 3 * P])
        bo = m.sb("bo", [P, P])
        cos, sin = m.sb("cos", [P, TPB, P]), m.sb("sin", [P, TPB, P])
        diag = m.sb("diag", [P, P])
        h = m.sb("h", [P, TPC, P])
        hT = m.sb("hT", [P, CHUNK])
        raw = m.sb("raw", [P, CPB, TPC, 3 * P])
        byc = m.sb("byc", [P, CPB, TPC, 2 * P])
        bys = m.sb("bys", [P, CPB, TPC, 2 * P])
        qT = m.sb("qT", [P, CPB, CHUNK])
        vk = m.sb("vk", [P, P])
        G = m.sb("G_", [P, P])
        psT, psP, psKV, psQ, psG, psO = banks[0], banks[1:3], banks[3], banks[4], banks[5], banks[6:8]
        loaded = m.sem("loaded")
        h_ready = m.sem("h_ready")
        turned = m.sem("turned")
        hT_ready = m.sem("hT_ready")
        p_ready = m.sem("p_ready")
        raw_ready = m.sem("raw_ready")
        byc_ready = m.sem("byc_ready")
        bys_ready = m.sem("bys_ready")
        rot_ready = m.sem("rot_ready")
        used = m.sem("used")
        qT_ready = m.sem("qT_ready")
        vk_ready = m.sem("vk_ready")
        g_product = m.sem("g_product")
        g_ready = m.sem("g_ready")
        o_ready = m.sem("o_ready")
        x_ready = m.sem("x_ready")
        x_done = m.sem("x_done")

        def pairs(ap, first):
            return ap.rearrange("p j (n t) -> p j n t", t=2)[:, :, :, first:first + 1].squeeze(3)

        with nc.Block() as block:
            @block.sync
            def _(sp):
                for n, name in enumerate(("Wq", "Wk", "Wv")):
                    sp.dma_start(wqkv[:, n * P:(n + 1) * P], ins["L1_attn_a_" + name]).then_inc(loaded, 16)
                for n, name in enumerate(("bq", "bk", "bv")):
                    sp.dma_start(bqkv[:, n * P:(n + 1) * P], ins["L1_attn_a_" + name].partition_broadcast(P)).then_inc(loaded, 16)
                sp.dma_start(cos[:, :, :], ins["rope_cos"].rearrange("(t p) d -> p t d", p=P)).then_inc(loaded, 16)
                sp.dma_start(sin[:, :, :], ins["rope_sin"].rearrange("(t p) d -> p t d", p=P)).then_inc(loaded, 16)
                sp.dma_start(diag[:, :], ins["head_diag"]).then_inc(loaded, 16)
                sp.dma_start(wo[:, :], ins["L1_attn_a_Wo"]).then_inc(loaded, 16)
                sp.dma_start(bo[:, :], ins["L1_attn_a_bo"].partition_broadcast(P)).then_inc(loaded, 16)
                sp.wait_ge(loaded, 11 * 16)

            @block.vector
            def _(dve):
                dve.sem_inc(raw_ready, 2)
                dve.sem_inc(vk_ready, 1)
                dve.sem_inc(x_done, 1)

                x = lambda k: lambda j: X[:, bass.ds(k * TPC + j, 1), :]

                def rotate(k, c, later, finished=None):
                    if later:
                        norm_statistics(norm, dve, k + 1, x(k + 1))
                    dve.wait_ge(used, k + 1)
                    for j in range(TPC):
                        dve.wait_ge(p_ready, k * TPC + j + 1)
                        nc.vector.tensor_tensor(raw[:, c, j, :], psP[j % 2][:, 0:3 * P], bqkv[:, :], ALU.add).then_inc(raw_ready, 1)
                    dve.wait_ge(raw_ready, (k + 1) * TPC + 2)
                    for half in range(2):
                        s = slice(half * P, (half + 1) * P)
                        last = nc.vector.tensor_tensor(byc[:, c, :, s], raw[:, c, :, s],
                                                       cos[:, c * TPC:(c + 1) * TPC, :], ALU.mult)
                    last.then_inc(byc_ready, 1)
                    if finished is not None:
                        take_vk(finished)
                    if later:
                        norm_result(norm, dve, k + 1, x(k + 1), lambda j: h[:, j, :]).then_inc(h_ready, 1)
                    dve.wait_ge(byc_ready, k + 1)
                    dve.wait_ge(bys_ready, k + 1)
                    nc.vector.tensor_tensor(byc[:, c, :, :], byc[:, c, :, :], bys[:, c, :, :], ALU.add).then_inc(rot_ready, 1)

                def take_vk(b):
                    dve.wait_ge(used, (b + 1) * CPB + 2)
                    nc.vector.tensor_tensor(vk[:, :], psKV[:, 0:P], diag[:, :], ALU.mult).then_inc(vk_ready, 1)

                def batch(b, more):
                    rotate(b * CPB + 1, 1, more)
                    if more:
                        rotate((b + 1) * CPB, 0, True, b)
                    else:
                        take_vk(b)
                    dve.wait_ge(o_ready, b + 1)
                    for c in range(CPB):
                        xk = X[:, bass.ds(b * TPB + c * TPC, TPC), :]
                        nc.vector.tensor_tensor(xk, xk, psO[c][:, :].rearrange("p (j n) -> p j n", j=TPC), ALU.add).then_inc(x_ready, 1)
                    dve.wait_ge(x_ready, b * 2 + 2)
                    xb = X[:, bass.ds(b * TPB, TPB), :]
                    nc.vector.tensor_tensor(xb, xb, bo[:, :].unsqueeze(1).to_broadcast([P, TPB, P]), ALU.add).then_inc(x_done, 1)

                norm.vector(dve, 0, x(0), lambda j: h[:, j, :]).then_inc(h_ready, 1)
                dve.wait_ge(loaded, 11 * 16)
                rotate(0, 0, True)
                loop(dve, NB, batch)

            @block.gpsimd
            def _(pool):
                norm.gpsimd(pool, 0)
                pool.wait_ge(loaded, 11 * 16)

                def partners(k, c, later):
                    if later:
                        norm.gpsimd(pool, k + 1)
                    pool.wait_ge(raw_ready, (k + 1) * TPC + 2)
                    for half in range(2):
                        s = slice(half * P, (half + 1) * P)
                        for first in range(2):
                            last = nc.gpsimd.tensor_tensor(pairs(bys[:, c, :, s], first), pairs(raw[:, c, :, s], 1 - first),
                                                           pairs(sin[:, c * TPC:(c + 1) * TPC, :], first), ALU.mult)
                    last.then_inc(bys_ready, 1)

                def batch(b, more):
                    partners(b * CPB + 1, 1, more)
                    if more:
                        partners((b + 1) * CPB, 0, True)

                partners(0, 0, True)
                loop(pool, NB, batch)

            @block.scalar
            def _(act):
                act.sem_inc(hT_ready, 1)
                act.sem_inc(qT_ready, 1)

                def copy_hT(k):
                    act.wait_ge(turned, k + 1)
                    nc.scalar.copy(hT[:, :], psT[:, :]).then_inc(hT_ready, 1)

                def batch(b, more):
                    for c in range(CPB):
                        k = b * CPB + c
                        act.wait_ge(used, k + 3)
                        nc.scalar.copy(qT[:, c, :], psQ[:, :]).then_inc(qT_ready, 1)
                        if c == CPB - 1:
                            act.wait_ge(g_product, b + 1)
                            nc.scalar.copy(G[:, :], psG[:, 0:P]).then_inc(g_ready, 1)
                        if more:
                            copy_hT(k + 2)

                copy_hT(0)
                copy_hT(1)
                loop(act, NB, batch)

            @block.tensor
            def _(pe):
                pe.sem_inc(used, 2)

                def turn(k):
                    pe.wait_ge(h_ready, k + 1)
                    pe.wait_ge(hT_ready, k + 1)
                    for j in range(TPC):
                        last = nc.tensor.transpose(psT[:, j * P:(j + 1) * P], h[:, j, :], ident[:, :])
                    last.then_inc(turned, 1)

                def projections(k):
                    pe.wait_ge(hT_ready, k + 2)
                    for j in range(TPC):
                        pe.wait_ge(raw_ready, k * TPC + j + 1)
                        nc.tensor.matmul(psP[j % 2][:, 0:3 * P], hT[:, j * P:(j + 1) * P], wqkv[:, :],
                                         start=True, stop=True).then_inc(p_ready, 1)

                def batch(b, more):
                    for c in range(CPB):
                        k = b * CPB + c
                        if c + 1 < CPB or more:
                            projections(k + 1)
                        pe.wait_ge(rot_ready, k + 1)
                        if c == 0:
                            pe.wait_ge(vk_ready, b + 1)
                        for j in range(TPC):
                            nc.tensor.matmul(psKV[:, 0:P], raw[:, c, j, 2 * P:3 * P], byc[:, c, j, P:2 * P],
                                             start=(c == 0 and j == 0), stop=(c == CPB - 1 and j == TPC - 1))
                        pe.wait_ge(qT_ready, k + 1)
                        for j in range(TPC):
                            last = nc.tensor.transpose(psQ[:, j * P:(j + 1) * P], byc[:, c, j, 0:P], ident[:, :])
                        last.then_inc(used, 1)
                        if c == CPB - 1:
                            pe.wait_ge(vk_ready, b + 2)
                            nc.tensor.matmul(psG[:, 0:P], vk[:, :], wo[:, :], start=True, stop=True).then_inc(g_product, 1)
                        if more:
                            turn(k + 2)
                    pe.wait_ge(g_ready, b + 1)
                    pe.wait_ge(x_done, b + 1)
                    pe.wait_ge(qT_ready, (b + 1) * CPB + 1)
                    for c in range(CPB):
                        for j in range(TPC):
                            last = nc.tensor.matmul(psO[c][:, j * P:(j + 1) * P], qT[:, c, j * P:(j + 1) * P], G[:, :],
                                                    start=True, stop=True)
                    last.then_inc(o_ready, 1)

                turn(0)
                pe.wait_ge(loaded, 11 * 16)
                projections(0)
                turn(1)
                loop(pe, NB, batch)


def alibi_rows(L, H):
    import math
    start = 2.0 ** (-2.0 ** (-(math.log2(H) - 3)))
    slopes = np.array([start * start ** i for i in range(H)], dtype=np.float32)
    bf = mybir.dt.np(BF16)
    parts, rest = [], slopes
    for _ in range(3):
        parts.append(rest.astype(bf))
        rest = rest - parts[-1].astype(np.float32)
    pos = np.arange(L)
    tile, place = (pos // P * P).astype(bf), (pos % P).astype(bf)
    keys, queries = np.zeros((H, 12, L), bf), np.zeros((H, 12, L), bf)
    for n, part in enumerate(parts):
        keys[:, 4 * n], queries[:, 4 * n] = tile, part[:, None]
        keys[:, 4 * n + 1], queries[:, 4 * n + 1] = place, part[:, None]
        keys[:, 4 * n + 2], queries[:, 4 * n + 2] = part[:, None], -tile
        keys[:, 4 * n + 3], queries[:, 4 * n + 3] = part[:, None], -place
    return keys, queries


MASKED = -1e30


def softmax_attention(nc, res, tag, w):
    X, banks, ident = res.X, res.banks, res.ident
    NB, L, D, H, DK, DV = res.B, res.L, P, w.H, w.DK, w.DV
    NCH, CPB, TPB = res.T // CHUNK, L // CHUNK, L // P
    NV = H * DV
    VB = -(-NV // 512)
    VW = min(NV, 512)
    HPV = VW // DV
    q_dram = nc.dram_tensor(f"{tag}_q", [D, 3, res.T], BF16).ap()
    k_dram = nc.dram_tensor(f"{tag}_k", [H, 3, DK, res.T], BF16).ap()
    v_dram = nc.dram_tensor(f"{tag}_v", [NB, H, P, TPB, DV], F32).ap()
    m_dram = nc.dram_tensor(f"{tag}_m", [NB * H, 2, TPB, P], BF16).ap()

    NH = NB * H
    SLOTS, AHEAD = 8, 3
    R0 = 9 * DK + (12 if w.alibi else 0)
    R1 = R0 + 2
    HALF = P // 2
    SHARE = HALF // DV
    SIDES = min(2, SLOTS // SHARE)
    OG = SHARE * SIDES
    OK = OG * DV
    NG = H // OG
    CB = min(2, NG)
    MAXES = [(j, 0, min(512, (j + 1) * P)) for j in range(TPB)] + [(j, 512, (j + 1) * P - 512) for j in range(4, TPB)]
    PROBS = [(i, i * P, 512 - i * P) for i in range(4)] + [(i, max(512, i * P), L - max(512, i * P)) for i in range(TPB)]
    NPR, NMX = len(PROBS), len(MAXES)
    MAX_STEPS = [[], [0, 1], [2], [3], [4], [5], [6], [7], [8, 9], [10], [11], []]
    PIECES = 8
    QKL = 2 + 2 * bool(w.alibi)
    QKS = 4
    assert L == 1024 and 64 < R0 and R1 <= P and H % SLOTS == 0 and SLOTS % OG == 0 and NPR == NMX == len(MAX_STEPS) == 12

    outer = ExitStack()
    mo = Scope(nc, outer, tag + "o")
    qs, ks = mo.sb("qs", [P, SLOTS, L], BF16), mo.sb("ks", [P, SLOTS, L], BF16)
    identb, upper, lower = (mo.sb(n, [P, P], BF16) for n in ("identb", "upper", "lower"))
    mask_made = mo.sem("mask_made")
    qk_sent = mo.sem("qk_sent")
    v_sent = mo.sem("v_sent")
    ks_set = mo.sem("ks_set")
    qk_in = [mo.sem(f"qk_in{n}") for n in range(2)]

    def load_qk(sp, b, hd, slot, par):
        toks, rows = bass.ds(b * L, L), bass.ds(hd * DK, DK)
        sp.dma_start(qs[0:9 * DK, slot, :], q_dram[rows, :, toks].rearrange("f r t -> (f r) t").unsqueeze(0).to_broadcast([3, 3 * DK, L])).then_inc(qk_in[par], 16)
        sp.dma_start(ks[0:9 * DK, slot, :], k_dram[bass.ds(hd, 1), :, :, toks].rearrange("o r f t -> (o r f) t").unsqueeze(1).to_broadcast([3 * DK, 3, L])).then_inc(qk_in[par], 16)
        if w.alibi:
            for buf, rows12 in ((qs, w.alibi_q), (ks, w.alibi_k)):
                sp.dma_start(buf[9 * DK:R0, slot, :], rows12[bass.ds(hd, 1)].rearrange("o r t -> (o r) t")).then_inc(qk_in[par], 16)

    with ExitStack() as ctx:
        m = Scope(nc, ctx, tag + "p")
        norm = Norm(m, res)
        wq, wk, wv = m.sb("wq", [P, D]), m.sb("wk", [P, D]), m.sb("wv", [P, NV])
        h = m.sb("h", [P, TPC, P])
        hT = m.sb("hT", [P, CHUNK])
        qk = m.sb("qk", [P, 2, CHUNK])
        parts = m.sb("parts", [P, 2, 3, CHUNK], BF16)
        rest = m.sb("rest", [P, 2, CHUNK])
        vout = m.sb("vout", [P, 2, H, TPC, DV])
        if w.biases:
            bq, bk, bv, bo = m.sb("bq", [P, 1]), m.sb("bk", [P, 1]), m.sb("bv", [P, NV]), m.sb("bo", [P, P])
            temp, qscale, qbias = m.sb("temp", [P, 1]), m.sb("qscale", [P, 1]), m.sb("qbias", [P, 1])
        psT, psQK, psV = banks[0], banks[1:3], banks[3:7]
        loaded = m.sem("loaded")
        NLOAD = 3 + 5 * bool(w.biases)
        scaled = m.sem("scaled")
        h_ready = m.sem("h_ready")
        turned = m.sem("turned")
        hT_ready = m.sem("hT_ready")
        qk_product = m.sem("qk_product")
        qk_ready = m.sem("qk_ready")
        part1 = m.sem("part1")
        rest1 = m.sem("rest1")
        part2 = m.sem("part2")
        part3 = m.sem("part3")
        v_product = m.sem("v_product")
        v_ready = [m.sem("v_even"), m.sem("v_odd")]
        VPC = TPC * VB

        def v_bank(k, n, eng):
            j, vb = n // VB, n % VB
            eng.wait_ge(v_product, k * VPC + n + 1)
            return vout[:, bass.ds(k % 2, 1), vb * HPV:(vb + 1) * HPV, j, :].rearrange("p o h d -> p (o h) d"), psV[n % 4][:, 0:VW].rearrange("p (h d) -> p h d", d=DV)

        with nc.Block() as block:
            @block.sync
            def _(sp):
                sp.sem_inc(qk_sent, 16 * QKS)
                sp.sem_inc(v_sent, 32)
                for t, src in ((wq, w.Wq), (wk, w.Wk), (wv, w.Wv)):
                    sp.dma_start(t[:, :], src).then_inc(loaded, 16)
                if w.biases:
                    for t, src in ((bq, w.bq), (bk, w.bk)):
                        sp.dma_start(t[:, :], src.rearrange("(p o) -> p o", o=1)).then_inc(loaded, 16)
                    for t, src in ((bv, w.bv), (bo, w.bo), (temp, w.temperature)):
                        sp.dma_start(t[:, :], src.partition_broadcast(P)).then_inc(loaded, 16)

                def load_first(hd):
                    if hd >= 2:
                        sp.wait_ge(qk_in[hd % 2], hd // 2 * QKL * 16)
                    load_qk(sp, 0, hd, hd, hd % 2)

                def batch(b, more):
                    for c in range(CPB):
                        k = b * CPB + c
                        if not more and c == 0:
                            sp.wait_ge(ks_set, 1)
                            sp.wait_ge(qk_sent, 16 * QKS * (CPB + 1))
                            load_first(0)
                        t = bass.ds(k * CHUNK, CHUNK)
                        for r, (part, n) in enumerate(((part1, k + 1), (part2, k + 1), (part3, k + 2))):
                            sp.wait_ge(part, n)
                            sp.dma_start(k_dram[:, r, :, t], parts[:, 1, r, :]).then_inc(qk_sent, 16)
                        sp.dma_start(q_dram[:, :, t], parts[:, 0, :, :]).then_inc(qk_sent, 16)
                        for v in v_ready:
                            sp.wait_ge(v, (k + 1) * VPC // 2 + 2)
                        sp.wait_ge(v_sent, k * 16 + 32)
                        sp.dma_start(v_dram[bass.ds(b, 1), :, :, c * TPC:(c + 1) * TPC, :].rearrange("o h p t e -> p (o h) (t e)"),
                                     vout[:, c % 2, :, :, :].rearrange("p h t e -> p h (t e)")).then_inc(v_sent, 16)
                        if not more:
                            load_first(c + 1)
                loop(sp, NB, batch)

            @block.vector
            def _(dve):
                dve.sem_inc(v_ready[1], 2)

                def norm_chunk(k):
                    norm.vector(dve, k, lambda j: X[:, bass.ds(k * TPC + j, 1), :], lambda j: h[:, j, :]).then_inc(h_ready, 1)

                def add_bias(k):
                    if w.biases:
                        dve.wait_ge(h_ready, k + 1)
                        xk = X[:, bass.ds(k * TPC, TPC), :]
                        nc.vector.tensor_tensor(xk, xk, bo[:, :].unsqueeze(1).to_broadcast([P, TPC, P]), ALU.add)

                def chunk(k, more):
                    if more:
                        dve.wait_ge(turned, k + 1)
                        norm_chunk(k + 1)
                        add_bias(k + 1)
                    dve.wait_ge(v_sent, k * 16 + 16)
                    for n in range(VPC) if w.biases else range(1, VPC, 2):
                        if n == VPC // 2 + 1:
                            dve.wait_ge(part1, k + 1)
                            nc.vector.tensor_tensor(rest[:, :, :], qk[:, :, :], parts[:, :, 0, :], ALU.subtract).then_inc(rest1, 1)
                        dst, src = v_bank(k, n, dve)
                        if w.biases:
                            nc.vector.tensor_tensor(dst, src, bv[:, :].rearrange("p (h d) -> p h d", d=DV), ALU.add).then_inc(v_ready[n % 2], 1)
                        else:
                            nc.vector.tensor_copy(dst, src).then_inc(v_ready[1], 1)

                norm_chunk(0)
                dve.wait_ge(loaded, NLOAD * 16)
                if w.biases:
                    dve.tensor_scalar(temp[:, :], temp[:, :], float(np.float32(np.sqrt(DK))), None, ALU.mult).then_inc(scaled, 1)
                    dve.wait_ge(scaled, 1)
                    dve.reciprocal(qscale[:, :], temp[:, :]).then_inc(scaled, 1)
                    dve.wait_ge(scaled, 2)
                    dve.tensor_tensor(qbias[:, :], bq[:, :], qscale[:, :], ALU.mult).then_inc(scaled, 1)
                add_bias(0)
                loop(dve, NCH, chunk)

            @block.gpsimd
            def _(pool):
                pool.sem_inc(part3, 1)
                norm.gpsimd(pool, 0)
                pool.memset(ks[:, :, :], 1.0).then_inc(ks_set, 1)
                for buf in (identb, upper, lower):
                    pool.memset(buf[:, :], 0.0).then_inc(mask_made, 1)
                pool.wait_ge(mask_made, 3)
                pool.affine_select(out=identb[:, :], in_=identb[:, :], compare_op=ALU.not_equal, fill=1.0, base=0,
                                   pattern=[[-1, P]], channel_multiplier=1).then_inc(mask_made, 1)
                pool.affine_select(out=upper[:, :], in_=upper[:, :], compare_op=ALU.is_ge, fill=MASKED, base=0,
                                   pattern=[[-1, P]], channel_multiplier=1).then_inc(mask_made, 1)
                pool.affine_select(out=lower[:, :], in_=lower[:, :], compare_op=ALU.is_ge, fill=MASKED, base=0,
                                   pattern=[[1, P]], channel_multiplier=-1).then_inc(mask_made, 1)

                def chunk(k, more):
                    if more:
                        norm.gpsimd(pool, k + 1)
                    pool.wait_ge(part2, k + 1)
                    nc.gpsimd.tensor_tensor(parts[:, :, 2, :], rest[:, :, :], parts[:, :, 1, :], ALU.subtract).then_inc(part3, 1)
                loop(pool, NCH, chunk)

            @block.scalar
            def _(act):
                act.sem_inc(hT_ready, 1)
                act.sem_inc(qk_ready, 1)
                act.sem_inc(v_ready[0], 2)

                def copy_hT(k):
                    act.wait_ge(turned, k + 1)
                    nc.scalar.copy(hT[:, :], psT[:, :]).then_inc(hT_ready, 1)

                def chunk(k, more):
                    act.wait_ge(part3, k + 1)
                    act.wait_ge(qk_product, k + 1)
                    if w.biases:
                        nc.scalar.activation(qk[:, 0, :], psQK[0][:, :], ACT.Identity, bias=qbias[:, 0:1], scale=qscale[:, 0:1])
                        nc.scalar.activation(qk[:, 1, :], psQK[1][:, :], ACT.Identity, bias=bk[:, 0:1]).then_inc(qk_ready, 1)
                    else:
                        nc.scalar.activation(qk[:, 0, :], psQK[0][:, :], ACT.Copy, scale=float(np.float32(DK ** -0.5)))
                        nc.scalar.copy(qk[:, 1, :], psQK[1][:, :]).then_inc(qk_ready, 1)
                    act.wait_ge(qk_ready, k + 2)
                    act.wait_ge(qk_sent, 16 * QKS * k + 16 * QKS)
                    nc.scalar.copy(parts[:, :, 0, :], qk[:, :, :]).then_inc(part1, 1)
                    if not w.biases:
                        act.wait_ge(v_sent, k * 16 + 16)
                    for n in range(0, VPC, 2):
                        if n == VPC // 2:
                            act.wait_ge(rest1, k + 1)
                            nc.scalar.copy(parts[:, :, 1, :], rest[:, :, :]).then_inc(part2, 1)
                        if not w.biases:
                            dst, src = v_bank(k, n, act)
                            nc.scalar.copy(dst, src).then_inc(v_ready[0], 1)
                    if more:
                        act.wait_ge(v_product, (k + 1) * VPC)
                        copy_hT(k + 1)

                copy_hT(0)
                if w.biases:
                    act.wait_ge(scaled, 3)
                loop(act, NCH, chunk)

            @block.tensor
            def _(pe):
                def turn(k):
                    pe.wait_ge(h_ready, k + 1)
                    pe.wait_ge(hT_ready, k + 1)
                    for j in range(TPC):
                        last = nc.tensor.transpose(psT[:, j * P:(j + 1) * P], h[:, j, :], ident[:, :])
                    last.then_inc(turned, 1)

                def chunk(k, more):
                    pe.wait_ge(hT_ready, k + 2)
                    pe.wait_ge(qk_ready, k + 1)
                    for n, weight in enumerate((wq, wk)):
                        last = nc.tensor.matmul(psQK[n][:, :], weight[:, :], hT[:, :], start=True, stop=True)
                    last.then_inc(qk_product, 1)
                    for n in range(VPC):
                        j, vb = n // VB, n % VB
                        pe.wait_ge(v_ready[n % 2], k * VPC // 2 + n // 2 + 1)
                        nc.tensor.matmul(psV[n % 4][:, 0:VW], hT[:, j * P:(j + 1) * P], wv[:, vb * VW:(vb + 1) * VW],
                                         start=True, stop=True).then_inc(v_product, 1)
                        if n == VPC // 2 - 1 and more:
                            turn(k + 1)

                turn(0)
                pe.wait_ge(loaded, NLOAD * 16)
                loop(pe, NCH, chunk)

    with ExitStack() as ctx:
        m = Scope(nc, ctx, tag + "a")
        probs = m.sb("probs", [P, 2, TPB * L])
        vs = m.sb("vs", [P, SLOTS, TPB, P])
        mx, mh = m.sb("mx", [P, 2, NMX]), m.sb("mh", [P, 2, TPB])
        mparts = m.sb("mparts", [TPB, SLOTS, 2, P], BF16)
        ctxT = m.sb("ctxT", [P, CB, L])
        den = m.sb("den", [P, CB, L])
        yT = m.sb("yT", [P, L])
        wo = m.sb("wo", [P, NG, D])
        psM, psS, psO, psY = banks[0:2], banks[2:4], banks[4:6], banks[6:8]
        mT = psM[0][0:TPB, 0:P]
        wo_in = m.sem("wo_in")
        v_set = m.sem("v_set")
        NVSET = SIDES if SHARE == 1 else 1 + SLOTS
        v_in = [m.sem(f"v_in{n}") for n in range(2)]
        m_sent = m.sem("m_sent")
        m_in = m.sem("m_in")
        m_product = m.sem("m_product")
        m_taken = m.sem("m_taken")
        mh_ready = m.sem("mh_ready")
        mT_ready = m.sem("mT_ready")
        mp_first = m.sem("mp_first")
        mp_ready = m.sem("mp_ready")
        s_product = m.sem("s_product")
        p_ready = m.sem("p_ready")
        o_product = m.sem("o_product")
        u_ready = m.sem("u_ready")
        inverted = m.sem("inverted")
        c_ready = m.sem("c_ready")
        y_product = m.sem("y_product")
        yT_ready = m.sem("yT_ready")
        y_turned = m.sem("y_turned")
        x_ready = m.sem("x_ready")
        cleared = [m_product, m_taken, mh_ready, mT_ready, mp_first, mp_ready, s_product, p_ready, o_product,
                   u_ready, inverted, c_ready, y_product, yT_ready, y_turned, x_ready]
        numbers = [s.num for s in cleared]
        assert sorted(numbers) == list(range(min(numbers), max(numbers) + 1))

        def clear():
            nc.gpsimd.sem_clear(range(min(numbers), max(numbers) + 1))
            nc.all_engine_barrier()

        def wait(eng, sem, n):
            if not isinstance(n, int) or n > 0:
                eng.wait_ge(sem, n)

        def side(slot):
            return slot // SHARE % SIDES * HALF, slot % SHARE * DV

        def load_v(sp, b, hd, slot, par):
            base, col = side(slot)
            sp.dma_start(vs[:, slot, :, base + col:base + col + DV],
                         v_dram[bass.ds(b, 1), bass.ds(hd, 1)].rearrange("o u p t e -> (o u p) t e")).then_inc(v_in[par], 16)

        def send_maxima(pool, a, t, slot):
            if t is not None:
                wait(pool, m_sent, 16 * a)
                pool.wait_ge(mp_ready, t + 1)
            pool.dma_start(m_dram[bass.ds(a, 1)].rearrange("o r j q -> (o j) r q"), mparts[:, slot, :, :]).then_inc(m_sent, 16)

        def fetch_maxima(sp, a, slot):
            sp.wait_ge(m_sent, 16 * a + 16)
            wait(sp, m_in, 16 * a)
            sp.dma_start(qs[R0:R1, slot, :], m_dram[bass.ds(a, 1)].rearrange("o r j q -> (o r) (j q)")).then_inc(m_in, 16)

        def max_scores(pe, t, idx, slot):
            j, k0, nk = MAXES[idx]
            if idx == 0:
                wait(pe, mp_ready, t)
            else:
                wait(pe, m_taken, t * NMX + idx - 1)
            diagonal = k0 + nk == (j + 1) * P
            last = nc.tensor.matmul(psM[idx % 2][:, 0:nk], qs[0:R0, slot, j * P:(j + 1) * P],
                                    ks[0:R0, slot, k0:k0 + nk], start=True, stop=not diagonal)
            if diagonal:
                last = nc.tensor.matmul(psM[idx % 2][:, nk - P:nk], identb[:, :], upper[:, :], start=False, stop=True)
            last.then_inc(m_product, 1)

        def turn_maxima(pe, t, par):
            pe.wait_ge(mh_ready, t + 1)
            nc.tensor.transpose(mT, mh[:, par, :], ident[:, :]).then_inc(mT_ready, 1)

        def scores(pe, t, idx, slot):
            i, q0, nq = PROBS[idx]
            wait(pe, p_ready, t * NPR + idx - 1)
            diagonal = q0 == i * P
            last = nc.tensor.matmul(psS[idx % 2][:, 0:nq], ks[0:R1, slot, i * P:(i + 1) * P],
                                    qs[0:R1, slot, q0:q0 + nq], start=True, stop=not diagonal)
            if diagonal:
                last = nc.tensor.matmul(psS[idx % 2][:, 0:P], identb[:, :], lower[:, :], start=False, stop=True)
            last.then_inc(s_product, 1)

        def outputs(pe, t, idx):
            i, q0, nq = PROBS[idx]
            g = q0 // 512
            if i == 0:
                if t % SHARE == 0:
                    wait(pe, u_ready, t // SHARE * 2 + g - 1)
                wait(pe, p_ready, t * NPR - (0 if g else NPR - 4))
            last = nc.tensor.matmul(psO[g][:, q0 - 512 * g:q0 - 512 * g + nq], vs[:, t % SLOTS, i, :], probs[:, t % 2, i * L + q0:i * L + q0 + nq],
                                    start=(i == 0 and t % SHARE == 0), stop=(i == 4 * g + 3 and t % SHARE == SHARE - 1))
            if i == 4 * g + 3:
                last.then_inc(o_product, 1)

        def project(pe, n, g, half, x_need):
            pe.wait_ge(c_ready, 2 * n + half + 1)
            wait(pe, x_ready, x_need)
            nc.tensor.matmul(psY[half][:, :], wo[0:OK, g, :], ctxT[0:OK, g % CB, half * 512:(half + 1) * 512],
                             start=(g == 0), stop=(g == NG - 1)).then_inc(y_product, 1)

        def turn_outputs(pe, half):
            pe.wait_ge(yT_ready, half + 1)
            for j in range(4):
                last = nc.tensor.transpose(psY[half][:, j * P:(j + 1) * P], yT[:, half * 512 + j * P:half * 512 + (j + 1) * P], ident[:, :])
            last.then_inc(y_turned, 1)

        def exps(act, t, idx, par):
            i, q0, nq = PROBS[idx]
            act.wait_ge(s_product, t * NPR + idx + 1)
            nc.scalar.activation(probs[:, par, i * L + q0:i * L + q0 + nq], psS[idx % 2][:, 0:nq], ACT.Exp).then_inc(p_ready, 1)

        def copy_outputs(act, half):
            act.wait_ge(y_product, half + 1)
            nc.scalar.copy(yT[:, half * 512:(half + 1) * 512], psY[half][:, :]).then_inc(yT_ready, 1)

        def maximum(dve, t, idx, par):
            dve.wait_ge(m_product, t * NMX + idx + 1)
            nc.vector.tensor_reduce(mx[:, par, idx:idx + 1], psM[idx % 2][:, 0:MAXES[idx][2]], AX.X, ALU.max).then_inc(m_taken, 1)

        def join_maxima(dve, t, par):
            dve.wait_ge(m_taken, (t + 1) * NMX)
            nc.vector.tensor_copy(mh[:, par, 0:4], mx[:, par, 0:4])
            nc.vector.tensor_tensor(mh[:, par, 4:TPB], mx[:, par, 4:TPB], mx[:, par, TPB:NMX], ALU.max).then_inc(mh_ready, 1)

        def split_maxima(dve, t, slot):
            dve.wait_ge(mT_ready, t + 1)
            nc.vector.tensor_scalar(mparts[:, slot, 0, :], mT, -1.0, None, ALU.mult).then_inc(mp_first, 1)
            dve.wait_ge(mp_first, t + 1)
            nc.vector.scalar_tensor_tensor(mparts[:, slot, 1, :], mT, -1.0, mparts[:, slot, 0, :],
                                           ALU.mult, ALU.subtract).then_inc(mp_ready, 1)

        def take_outputs(act, t, half, before):
            base, n, g = side(t)[0], t // SHARE * 2 + half, t // OG
            mine, other, cols = slice(base, base + HALF), slice(HALF - base, 2 * HALF - base), slice(half * 512, (half + 1) * 512)
            act.wait_ge(o_product, t * 2 + half + 1)
            wait(act, y_product, before + 2 * (g - CB + 1))
            nc.scalar.copy(den[mine, g % CB, cols], psO[half][other, :])
            nc.scalar.copy(ctxT[mine, g % CB, cols], psO[half][mine, :]).then_inc(u_ready, 1)

        def invert(dve, g, piece):
            cols = slice(piece * L // PIECES, (piece + 1) * L // PIECES)
            nc.vector.reciprocal(den[0:OK, g % CB, cols], den[0:OK, g % CB, cols]).then_inc(inverted, 1)

        def normalise(dve, n, g, half):
            cols = slice(half * 512, (half + 1) * 512)
            dve.wait_ge(inverted, n * PIECES + (half + 1) * PIECES // 2)
            nc.vector.tensor_tensor(ctxT[0:OK, g % CB, cols], ctxT[0:OK, g % CB, cols], den[0:OK, g % CB, cols],
                                    ALU.mult).then_inc(c_ready, 1)

        def add_output(dve, half, tile0):
            dve.wait_ge(y_turned, half + 1)
            tiles = X[:, bass.ds(tile0 + 4 * half, 4), :]
            nc.vector.tensor_tensor(tiles, tiles, psY[half][:, :].rearrange("p (j n) -> p j n", j=4), ALU.add).then_inc(x_ready, 1)

        with nc.Block() as block:
            @block.sync
            def _(sp):
                sp.dma_start(wo[0:OK, :, :], w.Wo.rearrange("(g p) n -> p g n", p=OK)).then_inc(wo_in, 16)
                for hd in range(AHEAD, SLOTS):
                    sp.wait_ge(qk_in[hd % 2], hd // 2 * QKL * 16)
                    load_qk(sp, 0, hd, hd, hd % 2)
                sp.wait_ge(v_sent, 16 * (NCH + 2))
                sp.wait_ge(v_set, NVSET)
                for hd in range(SLOTS):
                    wait(sp, v_in[hd % 2], hd // 2 * 16)
                    load_v(sp, 0, hd, hd, hd % 2)
                sp.wait_ge(wo_in, 16)

            @block.gpsimd
            def _(pool):
                if SHARE == 1:
                    for n in range(SIDES):
                        pool.memset(vs[:, n::SIDES, :, HALF - side(n)[0]:2 * HALF - side(n)[0]], 1.0).then_inc(v_set, 1)
                else:
                    pool.memset(vs[:, :, :, :], 0.0).then_inc(v_set, 1)
                    pool.wait_ge(v_set, 1)
                    for n in range(SLOTS):
                        base, col = side(n)
                        pool.memset(vs[:, n, :, HALF - base + col:HALF - base + col + DV], 1.0).then_inc(v_set, 1)
                for a in range(AHEAD):
                    send_maxima(pool, a, a, a)

            @block.vector
            def _(dve):
                for a in range(AHEAD):
                    for idx in range(NMX):
                        maximum(dve, a, idx, a % 2)
                    join_maxima(dve, a, a % 2)
                    split_maxima(dve, a, a)

            @block.scalar
            def _(act):
                for a in range(AHEAD - 1):
                    fetch_maxima(act, a, a)
                act.wait_ge(qk_sent, 16 * QKS * (NCH + 1))
                act.wait_ge(v_sent, 16 * (NCH + 2))
                for idx in range(NPR):
                    exps(act, 0, idx, 0)

            @block.tensor
            def _(pe):
                for a in range(AHEAD):
                    pe.wait_ge(qk_in[a % 2], (a // 2 + 1) * QKL * 16)
                    for idx in range(NMX):
                        max_scores(pe, a, idx, a)
                    turn_maxima(pe, a, a % 2)
                    if a == AHEAD - 1:
                        pe.wait_ge(m_in, 16)
                        for idx in range(NPR):
                            scores(pe, 0, idx, 0)
        clear()

        def batch(o, first, final):
            LEAD = AHEAD if final else 0
            before = 0 if first else 2

            with nc.Block() as block:
                @block.sync
                def _(sp):
                    for s in range(H):
                        par = s % 2
                        a = o * H + s + AHEAD
                        if s <= H - LEAD:
                            fetch_maxima(sp, a - 1, (s + AHEAD - 1) % SLOTS)
                        if final and s + SLOTS >= H:
                            continue
                        b, hd, slot = o + (s + SLOTS) // H, (s + SLOTS) % H, s % SLOTS
                        wait(sp, s_product, s * NPR)
                        sp.wait_ge(qk_in[par], (o * (H // 2) + (SLOTS + s) // 2) * QKL * 16)
                        load_qk(sp, b, hd, slot, par)
                        sp.wait_ge(o_product, 2 * s + 2)
                        sp.wait_ge(v_in[par], (o * (H // 2) + (SLOTS + s) // 2) * 16)
                        load_v(sp, b, hd, slot, par)

                @block.gpsimd
                def _(pool):
                    if not first:
                        send_maxima(pool, o * H + AHEAD - 1, None, AHEAD - 1)
                    for s in range(H - 1 - final * (LEAD - 1)):
                        send_maxima(pool, o * H + s + AHEAD, s, (s + AHEAD) % SLOTS)
                    if not final:
                        pool.wait_ge(m_sent, 16 * (o * H + H - 1 + AHEAD))

                @block.vector
                def _(dve):
                    for s in range(H):
                        ahead = s < H - LEAD
                        n, half = s // OG - first, s % OG
                        due = half < 2 and n >= 0
                        if due and half == 0:
                            wait(dve, u_ready, 2 * SIDES * (s // OG))
                        for step in range(NPR):
                            if ahead:
                                for idx in MAX_STEPS[step]:
                                    maximum(dve, s, idx, s % 2)
                            if due and step in (1, 3, 5, 7):
                                invert(dve, (s // OG - 1) % NG, half * PIECES // 2 + step // 2)
                            if due and step == 8:
                                normalise(dve, n, (s // OG - 1) % NG, half)
                            if not first and s in (1, 2) and step == 4:
                                add_output(dve, s - 1, (o - 1) * TPB)
                        if ahead:
                            join_maxima(dve, s, s % 2)
                            split_maxima(dve, s, (s + AHEAD) % SLOTS)

                @block.scalar
                def _(act):
                    for s in range(H):
                        whole = s % SHARE == SHARE - 1
                        for idx in range(NPR):
                            if not (final and s == H - 1):
                                exps(act, s, idx, (s + 1) % 2)
                            if idx == 0 and s and (s - 1) % SHARE == SHARE - 1:
                                take_outputs(act, s - 1, 1, before)
                            if idx == 5 and whole:
                                take_outputs(act, s, 0, before)
                            if not first and s in (1, 2) and idx == 1:
                                copy_outputs(act, s - 1)
                    take_outputs(act, H - 1, 1, before)

                @block.tensor
                def _(pe):
                    for s in range(H):
                        ahead = s < H - LEAD
                        n, half = s // OG - first, s % OG
                        due = half < 2 and n >= 0
                        if ahead:
                            pe.wait_ge(qk_in[(s + AHEAD) % 2], (o * (H // 2) + (s + AHEAD) // 2 + 1) * QKL * 16)
                        pe.wait_ge(v_in[s % 2], (o * (H // 2) + s // 2 + 1) * 16)
                        if not (final and s == H - 1):
                            pe.wait_ge(m_in, 16 * (o * H + s + 2))
                        for step in range(NPR):
                            if not (final and s == H - 1):
                                scores(pe, s, step, (s + 1) % SLOTS)
                            if ahead:
                                for idx in MAX_STEPS[step]:
                                    max_scores(pe, s, idx, (s + AHEAD) % SLOTS)
                            outputs(pe, s, step)
                            if ahead and step == NPR - 1:
                                turn_maxima(pe, s, s % 2)
                            if due and step == 10:
                                g = s // OG - 1
                                project(pe, n, g % NG, half, half + 1 if g == 0 and not first else 0)
                            if not first and s in (1, 2) and step == 3:
                                turn_outputs(pe, s - 1)
            clear()

        batch(0, True, False)
        with nc.Fori(0, NB - 2) as o:
            batch(o + 1, False, False)
        batch(NB - 1, False, True)

        with nc.Block() as block:
            @block.vector
            def _(dve):
                for half in range(2):
                    for piece in range(PIECES // 2):
                        invert(dve, NG - 1, half * PIECES // 2 + piece)
                    normalise(dve, 0, NG - 1, half)
                for half in range(2):
                    add_output(dve, half, (NB - 1) * TPB)

            @block.scalar
            def _(act):
                for half in range(2):
                    copy_outputs(act, half)

            @block.tensor
            def _(pe):
                for half in range(2):
                    project(pe, 0, NG - 1, half, 0)
                for half in range(2):
                    turn_outputs(pe, half)
    outer.close()


class Res:
    pass


def build_program(nc, ins, out):
    x_dram = ins["L0_attn_a_hidden_states"]
    B, L, D = x_dram.shape
    T = B * L
    NT = T // P
    res = Res()
    res.B, res.L, res.T, res.NT = B, L, T, NT
    with ExitStack() as ctx:
        g = Scope(nc, ctx, "g")
        res.X = X = g.sb("x", [P, NT, P])
        res.ident = ident = g.sb("ident", [P, P])
        res.banks = [ctx.enter_context(nc.psum_tensor(f"bank{i}", [P, 512], F32)) for i in range(8)]
        res.minus_half = g.sb("minus_half", [P, 8])
        x_in, w_in, id_ready, x_out = g.sem("x_in"), g.sem("w_in"), g.sem("id_ready"), g.sem("x_out")

        f = Res()
        DH = ins["L1_ffn_w1_w"].shape[0]
        HT = DH // P
        f.w1T, f.w2T = g.sb("w1T", [P, DH]), g.sb("w2T", [P, DH])
        f.h1T, f.h2T, f.w3T = g.sb("h1T", [P, HT, DH]), g.sb("h2T", [P, HT, DH]), g.sb("w3T", [P, HT, P])
        f.s1, f.s2, f.sh1, f.sh2 = (g.sb(n, [P, HT]) for n in ("s1", "s2", "sh1", "sh2"))
        f.s3 = g.sb("s3", [P, P])
        with ExitStack() as ctx2:
            ld = Scope(nc, ctx2, "ld")
            nat = {n: ld.sb(n, [P, HT, D]) for n in ("w1_w", "w2_w")}
            nat |= {n: ld.sb(n, [P, HT, DH]) for n in ("h1_w", "h2_w")}
            nat["w3_w"] = ld.sb("w3_w", [P, DH])
            with nc.Block() as block:
                @block.sync
                def _(sp):
                    for b in range(B):
                        sp.dma_start(X[:, b * L // P:(b + 1) * L // P, :],
                                     x_dram[b].rearrange("(t p) d -> p t d", p=P)).then_inc(x_in, 16)
                    sp.wait_ge(x_in, 16 * B)

                @block.scalar
                def _(act):
                    n = 0
                    for name in ("w1_w", "w2_w", "h1_w", "h2_w"):
                        act.dma_start(nat[name][:, :, :], ins["L1_ffn_" + name].rearrange("(o p) i -> p o i", p=P)).then_inc(w_in, 16)
                    act.dma_start(nat["w3_w"][:, :], ins["L1_ffn_w3_w"]).then_inc(w_in, 16)
                    with nc.allow_non_contiguous_dma(reason="one scale a partition"):
                        for name, t in (("w1_s", f.s1), ("w2_s", f.s2), ("h1_s", f.sh1), ("h2_s", f.sh2)):
                            act.dma_start(t[:, :], ins["L1_ffn_" + name].rearrange("(o p) -> p o", p=P)).then_inc(w_in, 16)
                    act.dma_start(f.s3[:, :], ins["L1_ffn_w3_s"].partition_broadcast(P)).then_inc(w_in, 16)
                    act.wait_ge(w_in, 160)

                @block.gpsimd
                def _(pool):
                    pool.memset(res.minus_half[:, :], -0.5)
                    pool.memset(ident[:, :], 0.0).then_inc(id_ready, 1)
                    pool.wait_ge(id_ready, 1)
                    pool.affine_select(out=ident[:, :], in_=ident[:, :], compare_op=ALU.not_equal, fill=1.0, base=0,
                                       pattern=[[-1, P]], channel_multiplier=1).then_inc(id_ready, 1)

            jobs = []
            for o in range(HT):
                so = slice(o * P, (o + 1) * P)
                jobs += [(f.w1T[:, so], nat["w1_w"][:, o, :]), (f.w2T[:, so], nat["w2_w"][:, o, :])]
                for i in range(HT):
                    si = slice(i * P, (i + 1) * P)
                    jobs += [(f.h1T[:, i, so], nat["h1_w"][:, o, si]), (f.h2T[:, i, so], nat["h2_w"][:, o, si])]
                jobs.append((f.w3T[:, o, :], nat["w3_w"][:, so]))
            transpose_blocks(nc, res, "ffnw", jobs, [(w_in, 160), (id_ready, 2)])

        wb = Res()
        wb.Wq, wb.Wk, wb.Wv, wb.Wo = (ins["L0_attn_b_" + n] for n in ("Wq", "Wk", "Wv", "Wo"))
        wb.H, wb.DK, wb.DV, wb.biases, wb.alibi = 16, 8, 64, False, False
        wc = Res()
        wat, bat = ins["L1_attn_b_W_attn"], ins["L1_attn_b_b_attn"]
        wc.Wq, wc.Wk, wc.Wv = (wat[:, n * D:(n + 1) * D] for n in range(3))
        wc.bq, wc.bk, wc.bv = (bat[n * D:(n + 1) * D] for n in range(3))
        wc.Wo, wc.bo, wc.temperature = ins["L1_attn_b_W_proj"], ins["L1_attn_b_b_proj"], ins["L1_attn_b_temperature"]
        wc.alibi_q, wc.alibi_k = ins["alibi_q"], ins["alibi_k"]
        wc.H, wc.DK, wc.DV, wc.biases, wc.alibi = 16, 8, 8, True, True
        steps = [lambda: gated_attention(nc, res, 'gla', ins), lambda: expert_ffn(nc, res, 'moe1', ins), lambda: softmax_attention(nc, res, "sma", wb), lambda: expert_ffn(nc, res, 'moe2', ins), lambda: rope_attention(nc, res, 'rope', ins),
                 lambda: ternary_ffn(nc, res, "ffn5", f), lambda: softmax_attention(nc, res, "smb", wc),
                 lambda: ternary_ffn(nc, res, "ffn7", f)]
        for step in steps:
            with nc.cleanup_on_exit():
                step()

        with nc.Block() as block:
            @block.sync
            def _(sp):
                for b in range(B):
                    sp.dma_start(out[b].rearrange("(t p) d -> p t d", p=P), X[:, b * L // P:(b + 1) * L // P, :]).then_inc(x_out, 16)
                sp.wait_ge(x_out, 16 * B)


def kernel(**inputs):
    import numpy as _np
    import concourse.bacc as _bacc
    from concourse import mybir as _mybir
    from concourse.bass_utils import run_bass_kernel_spmd as _run

    nc = _bacc.Bacc("TRN2", target_bir_lowering=False, num_devices=1)
    arrays, args = {}, {}
    x = inputs["L0_attn_a_hidden_states"]
    items = dict(inputs)
    items["rope_cos"], items["rope_sin"], items["head_diag"] = rope_tables(x.shape[1], x.shape[2], x.shape[2] // HEADS)
    items["token_marks"] = token_marks(x.shape[0] * x.shape[1])
    items["alibi_k"], items["alibi_q"] = alibi_rows(x.shape[1], HEADS)
    for name, a in items.items():
        a = _np.ascontiguousarray(a)
        arrays[f"in_{name}_dram"] = a
        args[name] = nc.dram_tensor(f"in_{name}_dram", a.shape, _mybir.dt.from_np(a.dtype), kind="ExternalInput").ap()
    out = nc.dram_tensor("out_0_dram", x.shape, F32, kind="ExternalOutput").ap()
    build_program(nc, args, out)
    r = _run(nc, [arrays], core_ids=[0])
    return r.results[0]["out_0_dram"]
```
